# Optimizing a Trainium2 kernel written in Bass

```python
import numpy as np
import jax
import jax.numpy as jnp

def _softmax(x, axis=-1):
    return jax.nn.softmax(x, axis=axis)

def _gelu(x):
    return jax.nn.gelu(x, approximate=True)

def _silu(x):
    return jax.nn.silu(x)

def _sigmoid(x):
    return jax.nn.sigmoid(x)

def _layernorm(x, axis=-1, eps=1e-05):
    m = jnp.mean(x, axis=axis, keepdims=True)
    v = jnp.var(x, axis=axis, keepdims=True)
    return (x - m) / jnp.sqrt(v + eps)

def _scatter_add(tgt, idx, src, axis=0):
    return tgt.at[idx].add(src)

def _segment_sum(src, seg, n):
    return jax.ops.segment_sum(src, seg, n)
kernel_name = 'mk_conv_attn_hybrid_d4_conv_nchw128_r4_69c72a'

def setup_inputs(seed: int=0):
    np.random.seed(seed)
    _w = jnp.asarray

    def _rec_inputs():
        import jax
        import jax.numpy as jnp
        _gk = jax.random.key(seed)
        x = -0.0005207 + 1.001 * jax.random.normal(jax.random.fold_in(_gk, 1), (4, 32, 16, 16), jnp.float32)
        return x
    x = _rec_inputs()

    def _L0_conv_setup():
        import jax, jax.numpy as jnp
        import numpy as np
        key = jax.random.key(seed)
        ks = jax.random.split(key, 8)
        B, C, H, W = (4, 32, 16, 16)
        d = C // 8
        return {'x': jax.random.normal(ks[0], (B, C, H, W), dtype=jnp.float32), 'wq': jax.random.normal(ks[1], (d, C), dtype=jnp.float32) * 0.05, 'bq': jax.random.normal(ks[2], (d,), dtype=jnp.float32) * 0.05, 'wk': jax.random.normal(ks[3], (d, C), dtype=jnp.float32) * 0.05, 'bk': jax.random.normal(ks[4], (d,), dtype=jnp.float32) * 0.05, 'wv': jax.random.normal(ks[5], (C, C), dtype=jnp.float32) * 0.05, 'bv': jax.random.normal(ks[6], (C,), dtype=jnp.float32) * 0.05, 'gamma': jax.random.normal(ks[7], (1,), dtype=jnp.float32)}
    _L0_conv_all = _L0_conv_setup()
    _L0_conv_in = {k: v for k, v in _L0_conv_all.items() if k in ('wq', 'bq', 'wk', 'bk', 'wv', 'bv', 'gamma')}
    del _L0_conv_all

    def _L1_conv_setup():
        import jax, jax.numpy as jnp
        import numpy as np
        from jax import lax
        EPS_NORM = 1e-12
        KS = 3
        K2 = KS * KS
        MIN_CONN, MAX_CONN = (1, 8)
        NUM_GROUPS = 16
        GN_EPS = 1e-05

        def _unfold3x3_reflect(x):
            B, C, H, W = x.shape
            p = jnp.pad(x, ((0, 0), (0, 0), (1, 1), (1, 1)), mode='reflect')
            pats = [p[:, :, dy:dy + H, dx:dx + W] for dy in range(KS) for dx in range(KS)]
            return jnp.stack(pats, axis=2)

        def _df_counts(x):
            B = x.shape[0]
            avg = jnp.mean(x, axis=1, keepdims=True)
            kern = jnp.array([[0.0, -1.0, 0.0], [-1.0, 4.0, -1.0], [0.0, -1.0, 0.0]], dtype=x.dtype).reshape(1, 1, 3, 3)
            df = jnp.abs(lax.conv_general_dilated(avg, kern, window_strides=(1, 1), padding=((1, 1), (1, 1)), dimension_numbers=('NCHW', 'OIHW', 'NCHW')))
            dmin = df.reshape(B, -1).min(axis=1).reshape(B, 1, 1, 1)
            dmax = df.reshape(B, -1).max(axis=1).reshape(B, 1, 1, 1)
            dn = (df - dmin) / (dmax - dmin + 1e-08)
            return MIN_CONN + jnp.round(dn * (MAX_CONN - MIN_CONN))

        def _group_norm(x, w, b):
            B, C, H, W = x.shape
            g = x.reshape(B, NUM_GROUPS, -1)
            mu = g.mean(-1, keepdims=True)
            var = g.var(-1, keepdims=True)
            g = (g - mu) * lax.rsqrt(var + GN_EPS)
            return g.reshape(B, C, H, W) * w[None, :, None, None] + b[None, :, None, None]
        key = jax.random.key(seed)
        ks = jax.random.split(key, 7)
        B, C, H, W = (8, 32, 24, 24)
        return {'x': jax.random.normal(ks[0], (B, C, H, W), jnp.float32), 'gn_weight': jax.random.uniform(ks[1], (C,), jnp.float32, 0.5, 1.5), 'gn_bias': jax.random.normal(ks[2], (C,), jnp.float32) * 0.1, 'w1': jax.random.normal(ks[3], (2 * C, C), jnp.float32) * 0.02, 'b1': jax.random.normal(ks[4], (2 * C,), jnp.float32) * 0.02, 'w2': jax.random.normal(ks[5], (C, 2 * C), jnp.float32) * 0.02, 'b2': jax.random.normal(ks[6], (C,), jnp.float32) * 0.02}
    _L1_conv_all = _L1_conv_setup()
    _L1_conv_in = {k: v for k, v in _L1_conv_all.items() if k in ('gn_weight', 'gn_bias', 'w1', 'b1', 'w2', 'b2')}
    del _L1_conv_all

    def _L2_attn_setup():
        import jax, jax.numpy as jnp
        import numpy as np
        B, S, D = (4, 1024, 32)
        key = jax.random.key(seed)
        kx, kq, kk, kv = jax.random.split(key, 4)
        x = jax.random.normal(kx, (B, S, D), dtype=jnp.float32)
        Wq = jax.random.normal(kq, (D, D), dtype=jnp.float32) * (1.0 / np.sqrt(D))
        Wk = jax.random.normal(kk, (D, D), dtype=jnp.float32) * (1.0 / np.sqrt(D))
        Wv = jax.random.normal(kv, (D, D), dtype=jnp.float32) * (1.0 / np.sqrt(D))
        return {'x': x, 'Wq': Wq, 'Wk': Wk, 'Wv': Wv}
    _L2_attn_all = _L2_attn_setup()
    _L2_attn_in = {k: v for k, v in _L2_attn_all.items() if k in ('Wq', 'Wk', 'Wv')}
    del _L2_attn_all

    def _L2_ffn_setup():
        import jax, jax.numpy as jnp
        import numpy as np
        PADDED_SL = 2048
        TEMPERATURE = 1.0
        SIGMA_POW = 0.25

        def _stu_conv(phi, u, n):
            b, sl, d = u.shape
            sgn = jnp.where(jnp.arange(sl) % 2 == 0, 1.0, -1.0).astype(u.dtype)
            sgn3 = sgn[None, :, None]
            Vf = jnp.fft.rfft(phi, n=n, axis=0)
            Uf_p = jnp.fft.rfft(u, n=n, axis=1)
            Uf_m = jnp.fft.rfft(u * sgn3, n=n, axis=1)
            U_plus = jnp.fft.irfft(Vf[None, :, :, None] * Uf_p[:, :, None, :], n=n, axis=1)[:, :sl]
            U_minus = jnp.fft.irfft(Vf[None, :, :, None] * Uf_m[:, :, None, :], n=n, axis=1)[:, :sl]
            U_minus = U_minus * sgn[None, :, None, None]
            return (U_plus, U_minus)

        def _compute_spectral(u, sigma, phi, Mpp, Mpm):
            U_plus, U_minus = _stu_conv(phi, u, PADDED_SL)
            s = sigma ** SIGMA_POW
            out = jnp.einsum('btkd,k,kde->bte', U_plus, s, Mpp)
            out = out + jnp.einsum('btkd,k,kde->bte', U_minus, s, Mpm)
            return out

        def _compute_ar_u(Mu, u):
            sl = u.shape[1]
            out = jnp.zeros(u.shape[:2] + (Mu.shape[-1],), dtype=u.dtype)
            for i in range(Mu.shape[0]):
                ui = jnp.pad(u, ((0, 0), (i, 0), (0, 0)))[:, :sl]
                out = out + jnp.einsum('btd,de->bte', ui, Mu[i])
            return out

        def _stu(u, sigma, phi, Mu, Mpp, Mpm):
            return _compute_spectral(u, sigma, phi, Mpp, Mpm) + _compute_ar_u(Mu, u)
        key = jax.random.key(seed)
        ks = jax.random.split(key, 8)
        b, sl, d, K, k_u = (2, 1024, 32, 16, 3)
        x = jax.random.normal(ks[0], (b, sl, d), dtype=jnp.float32)
        sigma = jax.random.uniform(ks[1], (K,), dtype=jnp.float32, minval=0.001, maxval=1.0)
        phi = jax.random.normal(ks[2], (sl, K), dtype=jnp.float32) / np.sqrt(sl)
        M_u = jax.random.normal(ks[3], (4, k_u, d, d), dtype=jnp.float32) * 0.02
        M_phi_plus = jax.random.normal(ks[4], (4, K, d, d), dtype=jnp.float32) * 0.02
        M_phi_minus = jax.random.normal(ks[5], (4, K, d, d), dtype=jnp.float32) * 0.02
        log_weights = jnp.ones((4,), dtype=jnp.float32)
        u01 = jax.random.uniform(ks[6], (4,), dtype=jnp.float32, minval=1e-06, maxval=1.0 - 1e-06)
        gumbel = -jnp.log(-jnp.log(u01))
        return {'x': x, 'sigma': sigma, 'phi': phi, 'M_u': M_u, 'M_phi_plus': M_phi_plus, 'M_phi_minus': M_phi_minus, 'log_weights': log_weights, 'gumbel': gumbel}
    _L2_ffn_all = _L2_ffn_setup()
    _L2_ffn_in = {k: v for k, v in _L2_ffn_all.items() if k in ('sigma', 'phi', 'M_u', 'M_phi_plus', 'M_phi_minus', 'log_weights', 'gumbel')}
    del _L2_ffn_all

    def _L3_attn_setup():
        import jax, jax.numpy as jnp
        import numpy as np
        B, S, D, H = (4, 1024, 32, 16)
        DH = D * H
        key = jax.random.key(seed)
        ks = jax.random.split(key, 10)
        sc = lambda fan: 1.0 / np.sqrt(fan)
        return {'x': jax.random.normal(ks[0], (B, S, D), jnp.float32), 'mask': jnp.ones((B, S), jnp.bool_), 'wq_w': jax.random.normal(ks[1], (DH, D), jnp.float32) * sc(D), 'wq_b': jax.random.normal(ks[2], (DH,), jnp.float32) * 0.01, 'wk_w': jax.random.normal(ks[3], (DH, D), jnp.float32) * sc(D), 'wk_b': jax.random.normal(ks[4], (DH,), jnp.float32) * 0.01, 'wv_w': jax.random.normal(ks[5], (DH, D), jnp.float32) * sc(D), 'wv_b': jax.random.normal(ks[6], (DH,), jnp.float32) * 0.01, 'dense_w': jax.random.normal(ks[7], (D, DH), jnp.float32) * sc(DH), 'dense_b': jax.random.normal(ks[8], (D,), jnp.float32) * 0.01}
    _L3_attn_all = _L3_attn_setup()
    _L3_attn_in = {k: v for k, v in _L3_attn_all.items() if k in ('mask', 'wq_w', 'wq_b', 'wk_w', 'wk_b', 'wv_w', 'wv_b', 'dense_w', 'dense_b')}
    del _L3_attn_all

    def _L3_ffn_setup():
        import jax, jax.numpy as jnp
        import numpy as np
        B, N, D, C, E, K = (8, 2048, 32, 32, 8, 2)
        key = jax.random.key(seed)
        k0, k1, k2 = jax.random.split(key, 3)
        x = jax.random.normal(k0, (B, N, D), dtype=jnp.float32)
        router_w = jax.random.normal(k1, (D, E), dtype=jnp.float32) * 0.05
        router_b = jnp.zeros((E,), dtype=jnp.float32)
        expert_w = jax.random.normal(k2, (E, D, C), dtype=jnp.float32) * (1.0 / np.sqrt(D))
        expert_b = jnp.zeros((E, C), dtype=jnp.float32)
        return {'x': x, 'router_w': router_w, 'router_b': router_b, 'expert_w': expert_w, 'expert_b': expert_b}
    _L3_ffn_all = _L3_ffn_setup()
    _L3_ffn_in = {k: v for k, v in _L3_ffn_all.items() if k in ('router_w', 'router_b', 'expert_w', 'expert_b')}
    del _L3_ffn_all
    return {'x': x, 'L0_conv_wq': _L0_conv_in['wq'], 'L0_conv_bq': _L0_conv_in['bq'], 'L0_conv_wk': _L0_conv_in['wk'], 'L0_conv_bk': _L0_conv_in['bk'], 'L0_conv_wv': _L0_conv_in['wv'], 'L0_conv_bv': _L0_conv_in['bv'], 'L0_conv_gamma': _L0_conv_in['gamma'], 'L1_conv_gn_weight': _L1_conv_in['gn_weight'], 'L1_conv_gn_bias': _L1_conv_in['gn_bias'], 'L1_conv_w1': _L1_conv_in['w1'], 'L1_conv_b1': _L1_conv_in['b1'], 'L1_conv_w2': _L1_conv_in['w2'], 'L1_conv_b2': _L1_conv_in['b2'], 'L2_attn_Wq': _L2_attn_in['Wq'], 'L2_attn_Wk': _L2_attn_in['Wk'], 'L2_attn_Wv': _L2_attn_in['Wv'], 'L2_ffn_sigma': _L2_ffn_in['sigma'], 'L2_ffn_phi': _L2_ffn_in['phi'], 'L2_ffn_M_u': _L2_ffn_in['M_u'], 'L2_ffn_M_phi_plus': _L2_ffn_in['M_phi_plus'], 'L2_ffn_M_phi_minus': _L2_ffn_in['M_phi_minus'], 'L2_ffn_log_weights': _L2_ffn_in['log_weights'], 'L2_ffn_gumbel': _L2_ffn_in['gumbel'], 'L3_attn_mask': _L3_attn_in['mask'], 'L3_attn_wq_w': _L3_attn_in['wq_w'], 'L3_attn_wq_b': _L3_attn_in['wq_b'], 'L3_attn_wk_w': _L3_attn_in['wk_w'], 'L3_attn_wk_b': _L3_attn_in['wk_b'], 'L3_attn_wv_w': _L3_attn_in['wv_w'], 'L3_attn_wv_b': _L3_attn_in['wv_b'], 'L3_attn_dense_w': _L3_attn_in['dense_w'], 'L3_attn_dense_b': _L3_attn_in['dense_b'], 'L3_ffn_router_w': _L3_ffn_in['router_w'], 'L3_ffn_router_b': _L3_ffn_in['router_b'], 'L3_ffn_expert_w': _L3_ffn_in['expert_w'], 'L3_ffn_expert_b': _L3_ffn_in['expert_b']}

def reference(x, L0_conv_wq, L0_conv_bq, L0_conv_wk, L0_conv_bk, L0_conv_wv, L0_conv_bv, L0_conv_gamma, L1_conv_gn_weight, L1_conv_gn_bias, L1_conv_w1, L1_conv_b1, L1_conv_w2, L1_conv_b2, L2_attn_Wq, L2_attn_Wk, L2_attn_Wv, L2_ffn_sigma, L2_ffn_phi, L2_ffn_M_u, L2_ffn_M_phi_plus, L2_ffn_M_phi_minus, L2_ffn_log_weights, L2_ffn_gumbel, L3_attn_mask, L3_attn_wq_w, L3_attn_wq_b, L3_attn_wk_w, L3_attn_wk_b, L3_attn_wv_w, L3_attn_wv_b, L3_attn_dense_w, L3_attn_dense_b, L3_ffn_router_w, L3_ffn_router_b, L3_ffn_expert_w, L3_ffn_expert_b):
    import jax
    import jax.numpy as jnp

    def _L0_conv_ref(x, wq, bq, wk, bk, wv, bv, gamma):
        import jax, jax.numpy as jnp
        import numpy as np
        B, C, H, W = x.shape
        N = H * W
        xf = x.reshape(B, C, N)
        q = jnp.einsum('bcn,dc->bdn', xf, wq) + bq[None, :, None]
        k = jnp.einsum('bcn,dc->bdn', xf, wk) + bk[None, :, None]
        v = jnp.einsum('bcn,oc->bon', xf, wv) + bv[None, :, None]
        scale = jnp.asarray(C, x.dtype) ** 0.5
        scores = jnp.einsum('bdn,bdm->bnm', q, k) / scale
        attn = jax.nn.softmax(scores, axis=2)
        out = jnp.einsum('bcm,bnm->bcn', v, attn).reshape(B, C, H, W)
        return gamma[0] * out + x

    def _L1_conv_ref(x, gn_weight, gn_bias, w1, b1, w2, b2):
        import jax, jax.numpy as jnp
        import numpy as np
        from jax import lax
        EPS_NORM = 1e-12
        KS = 3
        K2 = KS * KS
        MIN_CONN, MAX_CONN = (1, 8)
        NUM_GROUPS = 16
        GN_EPS = 1e-05

        def _unfold3x3_reflect(x):
            B, C, H, W = x.shape
            p = jnp.pad(x, ((0, 0), (0, 0), (1, 1), (1, 1)), mode='reflect')
            pats = [p[:, :, dy:dy + H, dx:dx + W] for dy in range(KS) for dx in range(KS)]
            return jnp.stack(pats, axis=2)

        def _df_counts(x):
            B = x.shape[0]
            avg = jnp.mean(x, axis=1, keepdims=True)
            kern = jnp.array([[0.0, -1.0, 0.0], [-1.0, 4.0, -1.0], [0.0, -1.0, 0.0]], dtype=x.dtype).reshape(1, 1, 3, 3)
            df = jnp.abs(lax.conv_general_dilated(avg, kern, window_strides=(1, 1), padding=((1, 1), (1, 1)), dimension_numbers=('NCHW', 'OIHW', 'NCHW')))
            dmin = df.reshape(B, -1).min(axis=1).reshape(B, 1, 1, 1)
            dmax = df.reshape(B, -1).max(axis=1).reshape(B, 1, 1, 1)
            dn = (df - dmin) / (dmax - dmin + 1e-08)
            return MIN_CONN + jnp.round(dn * (MAX_CONN - MIN_CONN))

        def _group_norm(x, w, b):
            B, C, H, W = x.shape
            g = x.reshape(B, NUM_GROUPS, -1)
            mu = g.mean(-1, keepdims=True)
            var = g.var(-1, keepdims=True)
            g = (g - mu) * lax.rsqrt(var + GN_EPS)
            return g.reshape(B, C, H, W) * w[None, :, None, None] + b[None, :, None, None]
        B, C, H, W = x.shape
        P = H * W
        counts = lax.stop_gradient(_df_counts(x))
        kvals = jnp.minimum(counts, K2).astype(jnp.int32).reshape(B, 1, P)
        patches = _unfold3x3_reflect(x).reshape(B, C, K2, P)
        xc = x.reshape(B, C, P)
        cn = xc / jnp.maximum(jnp.linalg.norm(xc, axis=1, keepdims=True), EPS_NORM)
        pn = patches / jnp.maximum(jnp.linalg.norm(patches, axis=1, keepdims=True), EPS_NORM)
        sim = jnp.einsum('bcp,bckp->bkp', cn, pn)
        order = jnp.argsort(-sim, axis=1)
        top_sim = jnp.take_along_axis(sim, order, axis=1)
        mask = jnp.arange(K2)[None, :, None] < kvals
        wts = jnp.exp(top_sim) * mask
        wts = wts / jnp.sum(wts, axis=1, keepdims=True)
        pat_sorted = jnp.take_along_axis(patches, order[:, None, :, :], axis=2)
        out = jnp.einsum('bckp,bkp->bcp', pat_sorted, wts).reshape(B, C, H, W)
        enhanced = out + _group_norm(x, gn_weight, gn_bias)
        h = jax.nn.relu(jnp.einsum('oi,bihw->bohw', w1, enhanced) + b1[None, :, None, None])
        ffn = jnp.einsum('oi,bihw->bohw', w2, h) + b2[None, :, None, None]
        return enhanced + ffn

    def _L2_attn_ref(x, Wq, Wk, Wv):
        import jax, jax.numpy as jnp
        import numpy as np
        B, S, D = (4, 1024, 32)
        b, s, d = x.shape
        q = jnp.einsum('bsd,ed->bse', x, Wq)
        k = jnp.einsum('bsd,ed->bse', x, Wk)
        v = jnp.einsum('bsd,ed->bse', x, Wv)
        scores = jnp.einsum('bqd,bkd->bqk', q, k) / jnp.sqrt(jnp.float32(d))
        causal = jnp.tril(jnp.ones((s, s), dtype=bool))
        scores = jnp.where(causal, scores, jnp.float32(-jnp.inf))
        weights = jax.nn.softmax(scores.astype(jnp.float32), axis=-1)
        out = jnp.einsum('bqk,bkd->bqd', weights, v)
        return out

    def _L2_ffn_ref(x, sigma, phi, M_u, M_phi_plus, M_phi_minus, log_weights, gumbel):
        import jax, jax.numpy as jnp
        import numpy as np
        PADDED_SL = 2048
        TEMPERATURE = 1.0
        SIGMA_POW = 0.25

        def _stu_conv(phi, u, n):
            b, sl, d = u.shape
            sgn = jnp.where(jnp.arange(sl) % 2 == 0, 1.0, -1.0).astype(u.dtype)
            sgn3 = sgn[None, :, None]
            Vf = jnp.fft.rfft(phi, n=n, axis=0)
            Uf_p = jnp.fft.rfft(u, n=n, axis=1)
            Uf_m = jnp.fft.rfft(u * sgn3, n=n, axis=1)
            U_plus = jnp.fft.irfft(Vf[None, :, :, None] * Uf_p[:, :, None, :], n=n, axis=1)[:, :sl]
            U_minus = jnp.fft.irfft(Vf[None, :, :, None] * Uf_m[:, :, None, :], n=n, axis=1)[:, :sl]
            U_minus = U_minus * sgn[None, :, None, None]
            return (U_plus, U_minus)

        def _compute_spectral(u, sigma, phi, Mpp, Mpm):
            U_plus, U_minus = _stu_conv(phi, u, PADDED_SL)
            s = sigma ** SIGMA_POW
            out = jnp.einsum('btkd,k,kde->bte', U_plus, s, Mpp)
            out = out + jnp.einsum('btkd,k,kde->bte', U_minus, s, Mpm)
            return out

        def _compute_ar_u(Mu, u):
            sl = u.shape[1]
            out = jnp.zeros(u.shape[:2] + (Mu.shape[-1],), dtype=u.dtype)
            for i in range(Mu.shape[0]):
                ui = jnp.pad(u, ((0, 0), (i, 0), (0, 0)))[:, :sl]
                out = out + jnp.einsum('btd,de->bte', ui, Mu[i])
            return out

        def _stu(u, sigma, phi, Mu, Mpp, Mpm):
            return _compute_spectral(u, sigma, phi, Mpp, Mpm) + _compute_ar_u(Mu, u)
        T = x.shape[1]
        outs = []
        for i, frac in enumerate((1, 2, 4, 8)):
            xi = x[:, :T // frac]
            si = _stu(xi, sigma, phi, M_u[i], M_phi_plus[i], M_phi_minus[i])
            si = jnp.pad(si, ((0, 0), (0, T - si.shape[1]), (0, 0)))
            outs.append(si)
        y_soft = jax.nn.softmax((log_weights + gumbel) / TEMPERATURE)
        y_hard = jax.nn.one_hot(jnp.argmax(y_soft), 4, dtype=y_soft.dtype)
        weights = y_hard - jax.lax.stop_gradient(y_soft) + y_soft
        stacked = jnp.stack(outs, axis=-1)
        return jnp.sum(stacked * weights, axis=-1)

    def _L3_attn_ref(x, mask, wq_w, wq_b, wk_w, wk_b, wv_w, wv_b, dense_w, dense_b):
        import jax, jax.numpy as jnp
        import numpy as np
        B, S, D, H = (4, 1024, 32, 16)
        DH = D * H
        b, s, d = x.shape
        h = wq_w.shape[0] // d
        q = (x @ wq_w.T + wq_b).reshape(b, s, h, d)
        k = (x @ wk_w.T + wk_b).reshape(b, s, h, d)
        v = (x @ wv_w.T + wv_b).reshape(b, s, h, d)
        q = jax.nn.elu(q) + 1.0
        k = jax.nn.elu(k) + 1.0
        pos = 1.57 * jnp.arange(s, dtype=x.dtype) / s
        cos = jnp.cos(pos)[None, :, None, None]
        sin = jnp.sin(pos)[None, :, None, None]
        q_cos, q_sin = (q * cos, q * sin)
        k_cos, k_sin = (k * cos, k * sin)
        kv_cos = jnp.einsum('bshx,bshz->bhxz', k_cos, v)
        kv_sin = jnp.einsum('bshx,bshz->bhxz', k_sin, v)
        qkv = jnp.einsum('bshx,bhxz->bshz', q_cos, kv_cos) + jnp.einsum('bshx,bhxz->bshz', q_sin, kv_sin)
        denom = 1.0 / (jnp.einsum('bshd,bhd->bsh', q_cos, k_cos.sum(axis=1)) + jnp.einsum('bshd,bhd->bsh', q_sin, k_sin.sum(axis=1)) + 1e-05)
        o = qkv * denom[..., None]
        concat = o.reshape(b, s, h * d)
        return concat @ dense_w.T + dense_b

    def _L3_ffn_ref(x, router_w, router_b, expert_w, expert_b):
        import jax, jax.numpy as jnp
        import numpy as np
        B, N, D, C, E, K = (8, 2048, 32, 32, 8, 2)
        router_probs = jax.nn.softmax(x @ router_w + router_b, axis=-1)
        top_p, top_i = jax.lax.top_k(router_probs, K)
        top_p = top_p / jnp.sum(top_p, axis=-1, keepdims=True)
        expert_out = jnp.einsum('bnd,edc->bnec', x, expert_w) + expert_b
        gathered = jnp.take_along_axis(expert_out, top_i[..., None], axis=2)
        return jnp.einsum('bnk,bnkc->bnc', top_p, gathered)

    def _gn(v, G=32, eps=1e-05):
        B_, C_, H_, W_ = v.shape
        g = v.reshape(B_, G, C_ // G, H_, W_)
        m = jnp.mean(g, axis=(2, 3, 4), keepdims=True)
        s = jnp.var(g, axis=(2, 3, 4), keepdims=True)
        return ((g - m) / jnp.sqrt(s + eps)).reshape(v.shape)

    def _ln_c(v, eps=1e-06):
        m = jnp.mean(v, axis=1, keepdims=True)
        s = jnp.var(v, axis=1, keepdims=True)
        return (v - m) / jnp.sqrt(s + eps)

    def _ln_t(v, eps=1e-05):
        m = jnp.mean(v, axis=-1, keepdims=True)
        s = jnp.var(v, axis=-1, keepdims=True)
        return (v - m) / jnp.sqrt(s + eps)

    def _to_tokens(v):
        B_, C_, H_, W_ = v.shape
        return v.reshape(B_, C_, H_ * W_).transpose(0, 2, 1)

    def _from_tokens(t, like):
        B_, C_, H_, W_ = like.shape
        return t.transpose(0, 2, 1).reshape(B_, C_, H_, W_)
    x = _L0_conv_ref(x, L0_conv_wq, L0_conv_bq, L0_conv_wk, L0_conv_bk, L0_conv_wv, L0_conv_bv, L0_conv_gamma)
    x = x + _L1_conv_ref(_gn(x), L1_conv_gn_weight, L1_conv_gn_bias, L1_conv_w1, L1_conv_b1, L1_conv_w2, L1_conv_b2)
    t = _to_tokens(x)
    t = t + _L2_attn_ref(_ln_t(t), L2_attn_Wq, L2_attn_Wk, L2_attn_Wv)
    t = t + _L2_ffn_ref(_ln_t(t), L2_ffn_sigma, L2_ffn_phi, L2_ffn_M_u, L2_ffn_M_phi_plus, L2_ffn_M_phi_minus, L2_ffn_log_weights, L2_ffn_gumbel)
    t = t + _L3_attn_ref(_ln_t(t), L3_attn_mask, L3_attn_wq_w, L3_attn_wq_b, L3_attn_wk_w, L3_attn_wk_b, L3_attn_wv_w, L3_attn_wv_b, L3_attn_dense_w, L3_attn_dense_b)
    t = t + _L3_ffn_ref(_ln_t(t), L3_ffn_router_w, L3_ffn_router_b, L3_ffn_expert_w, L3_ffn_expert_b)
    x = _from_tokens(t, x)
    return x

_drawn_inputs = setup_inputs


def setup_inputs(seed=0):
    import zlib

    import numpy as np

    out = dict(_drawn_inputs(seed))
    spreads = {'L2_ffn_log_weights': (1.0, 0.2),
     'L3_ffn_router_b': (0.0, 0.1),
     'L3_ffn_expert_b': (0.0, 0.328)}
    factors = {'L0_conv_wq': 8.0,
     'L0_conv_bq': 8.0,
     'L0_conv_wk': 8.0,
     'L0_conv_bk': 64.0,
     'L0_conv_wv': 8.0,
     'L0_conv_bv': 14.362,
     'L1_conv_w1': 3.056,
     'L1_conv_b1': 8.0,
     'L1_conv_w2': 3.093,
     'L3_attn_wq_w': 7.581,
     'L3_attn_wq_b': 64.0,
     'L3_attn_wk_b': 64.0,
     'L3_attn_wv_b': 3.434,
     'L3_attn_dense_b': 3.978}
    for name, (base, spread) in spreads.items():
        noise = np.random.default_rng([zlib.crc32(name.encode()), seed]).standard_normal(out[name].shape)
        drawn = base * np.exp(spread * noise) if base else spread * noise
        out[name] = jnp.asarray(drawn.astype(out[name].dtype))
    for name, factor in factors.items():
        out[name] = (out[name] * factor).astype(out[name].dtype)
    return out
```

```python
from contextlib import ExitStack

import numpy as np

import concourse.bass as bass
from concourse import mybir

B, C, HW = 4, 32, 16
N = HW * HW
P = 128
NH = N // P
PAD = HW + 2
KN = 9
HEADS = 16
HG = HEADS // 4
KF = 16
NRES = 4
NE = 8
XA = 2 * (C + 1)
TAPS = 3
PH = 4
NA = N // PH

F32 = mybir.dt.float32
BF16 = mybir.dt.bfloat16
ALU = mybir.AluOpType
ACT = mybir.ActivationFunctionType
AX = mybir.AxisListType.X
MAGIC = 12582912.0
MASKED = -1e30
LN2 = 0.6931471805599453

(COL_BQ, COL_BK, COL_GAMMA, COL_BV, COL_GNW, COL_GNB, COL_B1, COL_B2, COL_SIGMA,
 COL_COS, COL_SIN, COL_LOGW, COL_GUMBEL, COL_RES, COL_MCOS, COL_MSIN, COL_KVM, NCOL) = (
    0, 1, 2, 3, 4, 5, 6, 7, 8, 9, 11, 13, 17, 21, 25, 26, 27, 31)

C1 = dict(ident=128, center=128, mean=128, bo=4)
C2 = dict(lap=NH * N, lower=KN * KN, rankoff=NE + 2, pair=128, causal=2 * 128)
C3 = dict(seg=NRES * NA, selr=HG * 128, ksel=32)


def places(parts):
    at, out = 0, {}
    for name, width in parts.items():
        out[name] = (at, at + width)
        at += width
    return out, at


P1, W1 = places(C1)
P2, W2 = places(C2)
P3, W3 = places(C3)


def build(nc, x, w0, cols, c1, c2, c3, wl2, wmlp1, wmlp2, mstu, phi, sign, mu, bias3, biasone,
          wq3, wk3, wva, dwbd, kone, denseb, wrout, routb, wexp, out):
    with ExitStack() as ctx:
        def sb(name, shape, dt=F32):
            return ctx.enter_context(nc.sbuf_tensor(name, shape, dt))

        sems = {}

        def s(name):
            if name not in sems:
                sems[name] = ctx.enter_context(nc.semaphore(name))
            return sems[name]

        x_cl = sb("x_cl", [P, N])
        w0_sb = sb("w0_sb", [P, 3, P])
        col = sb("col", [P, NCOL])
        c1_sb = sb("c1_sb", [P, W1])
        c2_sb = sb("c2_sb", [P, W2])
        c3_sb = sb("c3_sb", [P, W3])
        wl2_sb = sb("wl2_sb", [P, 3, P])
        wmlp1_sb = sb("wmlp1_sb", [P, 2, P])
        wmlp2_sb = sb("wmlp2_sb", [P, 2, P])
        mstu_sb = sb("mstu_sb", [P, C * C])
        phi_sb = sb("phi_sb", [2 * KF, N])
        sign_sb = sb("sign_sb", [2 * KF, N])
        mu_sb = sb("mu_sb", [P, NRES, 8 * TAPS])
        bias3_sb = sb("bias3_sb", [P, 10])
        biasone_sb = sb("biasone_sb", [P, 10])
        wq3_sb = sb("wq3_sb", [P, 512])
        wk3_sb = sb("wk3_sb", [P, 512])
        wva_sb = sb("wva_sb", [P, HG, XA])
        dwbd_sb = sb("dwbd_sb", [P, HG, P])
        kone_sb = sb("kone_sb", [XA, 2])
        denseb_sb = sb("denseb_sb", [P, P])
        wrout_sb = sb("wrout_sb", [P, B * NE])
        routb_sb = sb("routb_sb", [P, NH * B * NE])
        wexp_sb = sb("wexp_sb", [P, NE * C])

        def part(tile, table, name):
            return tile[:, table[name][0]:table[name][1]]

        ident = part(c1_sb, P1, "ident")
        center = part(c1_sb, P1, "center")
        meanw = part(c1_sb, P1, "mean")
        bo = part(c1_sb, P1, "bo")
        lap = part(c2_sb, P2, "lap").rearrange("p (h n) -> p h n", h=NH)
        lower = part(c2_sb, P2, "lower").rearrange("p (j k) -> p j k", j=KN)
        rankoff = part(c2_sb, P2, "rankoff")
        pairw = part(c2_sb, P2, "pair")
        seg = part(c3_sb, P3, "seg").rearrange("p (i a) -> p i a", i=NRES)
        ksel = part(c3_sb, P3, "ksel")

        ident_bf = sb("ident_bf", [P, P], BF16)
        causal_bf = sb("causal_bf", [P, 2, P], BF16)
        selr_bf = sb("selr_bf", [P, HG, P], BF16)
        ones_bf = sb("ones_bf", [P, N], BF16)

        q0 = sb("q0", [P, N])
        k0 = sb("k0", [P, N])
        xg = sb("xg", [P, N])
        vaug = sb("vaug", [P, NH, B, C + 1])
        nmax = sb("nmax", [P, NH, B])
        nmhl = sb("nmhl", [P, NH, B, 32])
        nmb = sb("nmb", [P, NH, B], BF16)
        nmt = sb("nmt", [P, N], BF16)
        pT = sb("pT", [P, B, NH, N])
        orec = sb("orec", [P, NH * B])
        onorm = sb("onorm", [P, NH, P])
        x0 = sb("x0", [P, N])
        st6 = sb("st6", [P, 6])
        st2 = sb("st2", [P, 2])
        rs = sb("rs", [P, 2])
        y3 = sb("y3", [P, 3, PAD, HW])
        sq3 = sb("sq3", [P, 3, PAD, HW])
        prod = sb("prod", [P, 3, 3, N])
        gst6 = sb("gst6", [P, 6])
        gst = sb("gst", [P, 2])
        gme = sb("gme", [P, 2])
        gmu = sb("gmu", [P, 8])
        gy = sb("gy", [P, N])
        av = sb("av", [P, NH, B])
        absd = sb("absd", [B, N])
        dstat = sb("dstat", [B, 8])
        cnt = sb("cnt", [B, N])
        rk = sb("rk", [P, KN, NH * B])
        n2 = sb("n2", [P, KN, NH * B])
        rn = sb("rn", [P, KN, NH * B])
        nt = sb("nt", [P, KN, NH * B])
        sim = sb("sim", [P, KN, NH * B])
        ge = sb("ge", [P, KN, KN, NH * B])
        gd = sb("gd", [P, KN, KN, NH * B])
        rank = sb("rank", [P, KN, NH * B])
        wts = sb("wts", [P, KN, NH * B])
        wsum = sb("wsum", [P, NH * B])
        wprod = sb("wprod", [P, KN, NH, P])
        enh = sb("enh", [P, N])
        hid = sb("hid", [P, 2, N])
        xe = sb("xe", [P, N])
        x1 = sb("x1", [P, N])
        sq = sb("sq", [P, N])
        rstd = sb("rstd", [P, N])
        xln = sb("xln", [P, N])
        abd = sb("abd", [P, P])
        gq = sb("gq", [P, N])
        t2 = sb("t2", [P, N])
        wl = sb("wl", [P, 32])
        mixw = sb("mixw", [P, 2 * KF])
        ms = wprod[0:2 * KF, 0:4, :, :].rearrange("p k h n -> p (k h n)")
        mumix = sb("mumix", [P, 8 * TAPS])
        gtap = sb("gtap", [P, 8, N])
        fraw = sb("fraw", [P, 2, 8, N])
        big = sb("big", [P, 2 * HG * B * N])
        ftap = big[:, :].rearrange("p (t e) -> p t e", e=C)
        segm = sb("segm", [P, NA])
        xtr = sb("xtr", [P, 2, PH, C])
        u4 = sb("u4", [P, B, NA])
        ys = sb("ys", [P, 2, B, NA // 2])
        ych = sb("ych", [P, N])
        t3 = sb("t3", [P, N])
        b3f = sb("b3f", [P, 10])
        b3r = sb("b3r", [P, 10])
        b3 = sb("b3", [P, 3, 10], BF16)
        brow = sb("brow", [P, P * 10], BF16)
        xa = sb("xa", [P, NH, B, XA])
        t3b = sb("t3b", [P, NH, P])
        ee = pT[:, :, :, :].rearrange("p b h n -> p b (h n)")
        qf = big[:, 0:HG * B * N].rearrange("p (g b n) -> p g b n", g=HG, b=B)
        kf = big[:, HG * B * N:].rearrange("p (b h n) -> p b h n", b=B, h=NH)
        w2h = sb("w2h", [XA, HEADS, 66])
        kxt = sb("kxt", [XA, B, 512])
        kvd = sb("kvd", [P, B, HG, 66])
        ksb = sb("ksb", [P, B * HG, 4, 2])
        den = sb("den", [P, NH, B * HEADS])
        r3 = sb("r3", [P, NH, B, 64], BF16)
        rT = sb("rT", [P, 2, N], BF16)
        t4a = sb("t4a", [P, NH, P])
        t4 = sb("t4", [P, NH, P])
        mn4 = sb("mn4", [P, NH * B])
        xc4 = sb("xc4", [P, NH * B, C])
        sq4 = sb("sq4", [P, NH * B, C])
        rs4 = sb("rs4", [P, NH * B])
        xl4t = sb("xl4t", [P, NH, P])
        xl4 = sb("xl4", [P, N])
        lg = sb("lg", [P, NH * B, NE])
        lm = sb("lm", [P, NH * B])
        lx = sb("lx", [P, NH * B, NE])
        ge4 = sb("ge4", [P, NH * B, NE, NE])
        gd4 = sb("gd4", [P, NH * B, NE, NE])
        rank4 = sb("rank4", [P, NH * B, NE])
        eprod = wprod[:, 0:NE]
        x_out = sb("x_out", [P, N])

        ps = ctx.enter_context(nc.psum_tensor("ps", [P, 8, 512], F32))

        def bank(i, lo=0, hi=512):
            return ps[:, i, lo:hi]

        sc_bank = ps[:, 0:4, :].rearrange("p b (h n) -> p b h n", h=NH)
        o_ps = bank(6, 0, NH * B * (C + 1)).rearrange("p (h b c) -> p h b c", h=NH, b=B)
        sim_ps = bank(4, 0, 72).rearrange("p (k h b) -> p k h b", k=KN, h=NH)
        n2_ps = bank(4, 128, 200).rearrange("p (k h b) -> p k h b", k=KN, h=NH)
        av_ps = bank(5, 256, 264).rearrange("p (h b) -> p h b", h=NH)
        pt_a = ps[:, 0:4, :].rearrange("p b (k n) -> p (b k) n", k=4).rearrange("p (k h) n -> p k h n", h=NH)
        pt_b = bank(6, 0, 256).rearrange("p (h n) -> p h n", h=NH)
        nbr = [(dy, dx) for dy in (-1, 0, 1) for dx in (-1, 0, 1)]

        def shifted(tile, dy, dx, h=None):
            rows = slice(1 + dy, 1 + dy + HW) if h is None else slice(1 + dy + 8 * h, 9 + dy + 8 * h)
            return tile[:, 1 + dx, rows, :].rearrange("p r c -> p (r c)")

        loads = [
            ("in_a", [(x_cl, x), (w0_sb, w0), (col, cols)]),
            ("in_b", [(c1_sb, c1)]),
            ("in_c", [(c2_sb, c2), (mstu_sb, mstu), (c3_sb, c3)]),
            ("in_d", [(wl2_sb, wl2), (phi_sb, phi), (sign_sb, sign), (mu_sb, mu)]),
            ("in_e", [(wmlp1_sb, wmlp1), (wmlp2_sb, wmlp2)]),
            ("in_f", [(bias3_sb, bias3), (biasone_sb, biasone), (wva_sb, wva), (dwbd_sb, dwbd), (kone_sb, kone)]),
            ("in_g", [(wq3_sb, wq3), (wk3_sb, wk3), (denseb_sb, denseb), (wrout_sb, wrout),
                      (routb_sb, routb), (wexp_sb, wexp)]),
        ]
        landed = {name: 16 * len(group) for name, group in loads}

        def full(t):
            return t[tuple(slice(None) for _ in t.shape)]

        block = ctx.enter_context(nc.Block())

        @block.sync
        def _(sp):
            for name, group in loads:
                for dst, src in group:
                    sp.dma_start(full(dst), src).then_inc(s(name), 16)
            sp.wait_ge(s("b3"), 3)
            for b in range(B):
                for k in range(3):
                    sp.dma_start(brow[32 * b + k:32 * b + k + 1, :], b3[:, k, :]).then_inc(s("brow"), 16)
            sp.wait_ge(s("fraw_zero"), 1)
            sp.wait_ge(s("gtap_mu"), 1)
            for e4 in range(4):
                if e4 >= 2:
                    sp.wait_ge(s("ftap"), e4 - 1)
                for r in range(PH):
                    sp.dma_start(fraw[32 * r:32 * r + 32, e4 % 2, :, r:N],
                                 gtap[32 * e4:32 * e4 + 32, :, 0:N - r]).then_inc(s("fraw%d" % (e4 % 2)), 16)
            sp.wait_ge(s("x_out"), 1)
            sp.dma_start(out, x_out[:, :]).then_inc(s("out"), 16)
            sp.wait_ge(s("out"), 16)

        @block.gpsimd
        def _(pool):
            g = nc.gpsimd
            g.memset(vaug[:, :, :, C:C + 1], 1.0).then_inc(s("vaug_one"), 1)
            g.memset(nmhl[:, :, :, :], 0.0).then_inc(s("nmhl_zero"), 1)
            g.memset(ones_bf[:, :], 1.0).then_inc(s("ones_bf"), 1)
            g.memset(r3[:, :, :, :], 0.0).then_inc(s("r3_zero"), 1)
            g.memset(fraw[:, :, :, 0:TAPS], 0.0).then_inc(s("fraw_zero"), 1)
            pool.wait_ge(s("in_b"), landed["in_b"])
            g.tensor_copy(ident_bf[:, :], ident).then_inc(s("ident_bf"), 1)
            pool.wait_ge(s("in_c"), landed["in_c"])
            g.tensor_copy(causal_bf[:, :, :], part(c2_sb, P2, "causal").rearrange("p (a n) -> p a n", a=2)
                          ).then_inc(s("causal_bf"), 1)
            g.tensor_copy(selr_bf[:, :, :], part(c3_sb, P3, "selr").rearrange("p (a n) -> p a n", a=HG)
                          ).then_inc(s("selr_bf"), 1)
            pool.wait_ge(s("in_d"), landed["in_d"])
            g.tensor_tensor(phi_sb[:, :], phi_sb[:, :], sign_sb[:, :], ALU.mult).then_inc(s("phi"), 1)
            pool.wait_ge(s("in_f"), landed["in_f"])
            g.tensor_tensor(b3f[:, :], bias3_sb[:, :], biasone_sb[:, :], ALU.add).then_inc(s("b3f"), 1)
            pool.wait_ge(s("b3f"), 1)
            g.tensor_copy(b3[:, 0, :], b3f[:, :]).then_inc(s("b3"), 1)
            pool.wait_ge(s("b3"), 1)
            g.tensor_tensor(b3r[:, :], b3f[:, :], b3[:, 0, :], ALU.subtract).then_inc(s("b3f"), 1)
            pool.wait_ge(s("b3f"), 2)
            g.tensor_copy(b3[:, 1, :], b3r[:, :]).then_inc(s("b3"), 1)
            pool.wait_ge(s("b3"), 2)
            g.tensor_tensor(b3f[:, :], b3r[:, :], b3[:, 1, :], ALU.subtract).then_inc(s("b3f"), 1)
            pool.wait_ge(s("b3f"), 3)
            g.tensor_copy(b3[:, 2, :], b3f[:, :]).then_inc(s("b3"), 1)
            pool.wait_ge(s("y_pad"), 5)
            for dx in (-1, 1):
                g.tensor_tensor(prod[:, 1, 1 + dx, :], shifted(y3, 0, 0), shifted(y3, 0, dx), ALU.mult
                                ).then_inc(s("prod_side"), 1)
            for e4 in range(4):
                pool.wait_ge(s("fraw%d" % (e4 % 2)), 64 * (e4 // 2 + 1))
                g.tensor_copy(ftap[:, :, e4::4], fraw[:, e4 % 2, :, :].rearrange("p g t -> p t g")
                              ).then_inc(s("ftap"), 1)

        @block.scalar
        def _(act):
            a = nc.scalar

            def ln_tail(nth, center_ps, var_ps):
                act.wait_ge(s("ln_center"), 2 * nth - 1)
                a.activation(sq[:, :], center_ps, ACT.Square).then_inc(s("ln_sq"), 1)
                act.wait_ge(s("ln_var"), nth)
                act.wait_ge(s("eps_ready"), 1)
                a.activation(rstd[:, :], var_ps, ACT.Ln, bias=wl[:, 31:32]).then_inc(s("ln_ln"), 1)
                act.wait_ge(s("ln_ln"), nth)
                a.activation(rstd[:, :], rstd[:, :], ACT.Exp, scale=-0.5).then_inc(s("ln_rstd"), 1)

            act.wait_ge(s("in_a"), landed["in_a"])
            act.wait_ge(s("qk0"), 2)
            a.activation(k0[:, :], bank(7, 0, N), ACT.Identity, bias=col[:, COL_BK:COL_BK + 1]).then_inc(s("k0"), 1)
            act.wait_ge(s("abd_ps"), 1)
            a.activation(abd[:, :], bank(6, 0, P), ACT.Copy, scale=float(C) ** -0.5).then_inc(s("abd"), 1)
            act.wait_ge(s("v0_ps"), 1)
            for h in range(NH):
                a.activation(vaug[:, h, :, 0:C], bank(5, 128 * h, 128 * h + 128).rearrange("p (b c) -> p b c", b=B),
                             ACT.Copy).then_inc(s("v0"), 1)
            act.wait_ge(s("gbv"), 1)
            a.activation(xg[:, :], x_cl[:, :], ACT.Identity, bias=wl[:, 30:31]).then_inc(s("xg"), 1)
            a.activation(wl[:, 16:17], col[:, COL_SIGMA:COL_SIGMA + 1], ACT.Ln).then_inc(s("sig"), 1)
            act.wait_ge(s("sig"), 1)
            a.activation(wl[:, 17:18], wl[:, 16:17], ACT.Exp, scale=0.25).then_inc(s("sig"), 1)
            act.wait_ge(s("lmax"), 1)
            a.activation(wl[:, 4:8], wl[:, 0:4], ACT.Exp, bias=wl[:, 8:9]).then_inc(s("lexp"), 1)
            act.wait_ge(s("ms_ps"), 2)
            for k in range(2):
                a.activation(ms[:, 512 * k:512 * k + 512], ps[0:2 * KF, 6 + k, :], ACT.Copy).then_inc(s("ms"), 1)
            for b in range(B):
                act.wait_ge(s("sT0"), b + 1)
                a.activation(pT[:, b, :, :], sc_bank[:, b, :, :], ACT.Exp).then_inc(s("pT0"), 1)
            act.wait_ge(s("gn_stat"), 1)
            act.wait_ge(s("eps_ready"), 1)
            a.activation(rs[:, 0:1], st2[:, 1:2], ACT.Ln, bias=wl[:, 31:32]).then_inc(s("gn_ln"), 1)
            act.wait_ge(s("gn_ln"), 1)
            a.activation(rs[:, 1:2], rs[:, 0:1], ACT.Exp, scale=-0.5).then_inc(s("gn_rstd"), 1)
            for k in (0, 1):
                act.wait_ge(s("gtap_ps"), k + 1)
                a.activation(gtap[:, 2 * k:2 * k + 2, :].rearrange("p g t -> p (g t)"), bank(k), ACT.Copy
                             ).then_inc(s("gtap"), 1)
            act.wait_ge(s("y_pad"), 6)
            a.activation(sq3[:, :, :, :], y3[:, :, :, :], ACT.Square).then_inc(s("ysq"), 1)
            for k in (2, 3):
                act.wait_ge(s("gtap_ps"), k + 1)
                a.activation(gtap[:, 2 * k:2 * k + 2, :].rearrange("p g t -> p (g t)"), bank(k), ACT.Copy
                             ).then_inc(s("gtap"), 1)
            act.wait_ge(s("lap_ps"), 1)
            a.activation(absd[:, :], ps[0:B, 5, 0:N], ACT.Abs).then_inc(s("absd"), 1)
            act.wait_ge(s("n2"), 1)
            a.activation(nt[:, :, :], n2[:, :, :], ACT.Ln, scale=float(2 ** 40)).then_inc(s("n2_ln"), 1)
            act.wait_ge(s("n2_ln"), 1)
            a.activation(rn[:, :, :], nt[:, :, :], ACT.Exp, scale=-0.5, bias=wl[:, 29:30]).then_inc(s("rn0"), 1)
            act.wait_ge(s("gvar"), 1)
            a.activation(gmu[:, 3:4], gmu[:, 2:3], ACT.Ln, bias=wl[:, 31:32]).then_inc(s("gln"), 1)
            act.wait_ge(s("gln"), 1)
            a.activation(gmu[:, 4:5], gmu[:, 3:4], ACT.Exp, scale=-0.5).then_inc(s("grstd"), 1)
            act.wait_ge(s("sim"), 1)
            a.activation(wts[:, :, :], sim[:, :, :], ACT.Exp).then_inc(s("simexp"), 1)
            act.wait_ge(s("gab"), 1)
            a.activation(gy[:, :], shifted(y3, 0, 0), ACT.Identity,
                         scale=gmu[:, 5:6], bias=gmu[:, 7:8]).then_inc(s("gy"), 1)
            act.wait_ge(s("hid_ps"), 1)
            act.wait_ge(s("in_e"), landed["in_e"])
            a.activation(hid[:, 0, :], bank(4, 0, N), ACT.Relu, bias=col[:, COL_B1:COL_B1 + 1]).then_inc(s("hid_a"), 1)
            ln_tail(1, bank(6, 0, N), bank(6, 256, 512))
            act.wait_ge(s("v2_ps"), 1)
            for h in range(NH):
                a.activation(vaug[:, h, :, 0:C], bank(4, 128 * h, 128 * h + 128).rearrange("p (b c) -> p b c", b=B),
                             ACT.Copy).then_inc(s("v2"), 1)
            for b in range(B):
                act.wait_ge(s("sT2"), b + 1)
                a.activation(pT[:, b, :, :].rearrange("p h n -> p (h n)")[:, 0:384], bank(b, 0, 384), ACT.Exp
                             ).then_inc(s("pT2"), 1)
            ln_tail(2, bank(6, 0, N), bank(6, 256, 512))
            act.wait_ge(s("u4_ps"), 2)
            a.activation(u4[:, :, :].rearrange("p b (h a) -> p h b a", h=2),
                         bank(7, 0, 256).rearrange("p (h b a) -> p h b a", h=2, b=B), ACT.Copy).then_inc(s("u4"), 1)
            ln_tail(3, bank(6, 0, N), bank(6, 256, 512))
            for t in range(16):
                act.wait_ge(s("qk3_ps"), t + 1)
                if t >= 4:
                    act.wait_ge(s("qk3"), t - 3)
                a.activation(ee[:, t % 4, :], bank(t % 4), ACT.Exp, bias=wl[:, 28:29]).then_inc(s("qk3_exp"), 1)
                if t in (8, 10, 12, 14):
                    b = (t - 8) // 2
                    act.wait_ge(s("kxt_ps"), b + 1)
                    a.activation(kxt[:, b, :], ps[0:XA, 4 + b % 2, :], ACT.Copy).then_inc(s("kxt"), 1)
            for b in range(B):
                act.wait_ge(s("kvd_ps"), b + 1)
                a.activation(kvd[:, b, :, :], bank(6 + b % 2, 0, HG * 66).rearrange("p (g n) -> p g n", g=HG), ACT.Copy
                             ).then_inc(s("kvd"), 1)
            act.wait_ge(s("rT_ps"), 4)
            a.activation(rT[:, :, :].rearrange("p c (h n) -> p c h n", h=NH),
                         bank(5, 0, 256).bitcast(BF16).rearrange("p (c h n) -> p c h n", c=2, h=NH), ACT.Copy
                         ).then_inc(s("rT"), 1)
            act.wait_ge(s("xc4"), 1)
            a.activation(sq4[:, :, :], xc4[:, :, :], ACT.Square).then_inc(s("sq4"), 1)
            act.wait_ge(s("var4"), 1)
            a.activation(rs4[:, :], rs4[:, :], ACT.Ln, scale=1.0 / C, bias=wl[:, 31:32]).then_inc(s("ln4"), 1)
            act.wait_ge(s("ln4"), 1)
            a.activation(rs4[:, :], rs4[:, :], ACT.Exp, scale=-0.5).then_inc(s("rs4"), 1)
            act.wait_ge(s("xl4_ps"), 2)
            a.activation(xl4[:, :], bank(7, 0, 256), ACT.Copy).then_inc(s("xl4"), 1)
            act.wait_ge(s("lx0"), 1)
            a.activation(lx[:, :, :], lx[:, :, :], ACT.Exp).then_inc(s("lexp4"), 1)
            act.wait_ge(s("fin_ps"), 1)
            a.activation(x_out[:, :], bank(4, 0, 256), ACT.Copy).then_inc(s("x_out"), 1)

        @block.vector
        def _(dve):
            v = nc.vector
            chain_count = [0]

            def small(ins):
                chain_count[0] += 1
                ins.then_inc(s("small"), 1)
                dve.wait_ge(s("small"), chain_count[0])

            def ln_apply(nth, out_ap):
                dve.wait_ge(s("ln_center"), 2 * nth)
                dve.wait_ge(s("ln_rstd"), nth)
                v.tensor_tensor(out_ap, bank(5, 0, N), rstd[:, :], ALU.mult).then_inc(s("ln_xln"), 1)

            v.memset(wl[:, 31:32], 1e-5)
            v.memset(wl[:, 29:30], 20.0 * LN2)
            v.memset(wl[:, 28:29], -1.0).then_inc(s("eps_ready"), 1)
            dve.wait_ge(s("in_a"), landed["in_a"])
            v.tensor_tensor(wl[:, 30:31], col[:, COL_GAMMA:COL_GAMMA + 1], col[:, COL_BV:COL_BV + 1], ALU.mult
                            ).then_inc(s("gbv"), 1)
            dve.wait_ge(s("qk0"), 1)
            v.tensor_scalar(q0[:, :], bank(4, 0, N), col[:, COL_BQ:COL_BQ + 1], float(C) ** -0.5, ALU.add, ALU.mult
                            ).then_inc(s("q0"), 1)
            small(v.tensor_tensor(wl[:, 0:4], col[:, COL_LOGW:COL_LOGW + 4], col[:, COL_GUMBEL:COL_GUMBEL + 4], ALU.add))
            v.tensor_reduce(wl[:, 8:9], wl[:, 0:4], AX, ALU.max, negate=True).then_inc(s("lmax"), 1)
            dve.wait_ge(s("lexp"), 1)
            small(v.tensor_reduce(wl[:, 9:10], wl[:, 4:8], AX, ALU.add))
            small(v.reciprocal(wl[:, 10:11], wl[:, 9:10]))
            small(v.tensor_scalar(wl[:, 4:8], wl[:, 4:8], wl[:, 10:11], None, ALU.mult))
            small(v.tensor_reduce(wl[:, 11:12], wl[:, 4:8], AX, ALU.max))
            small(v.tensor_scalar(wl[:, 0:4], wl[:, 4:8], wl[:, 11:12], None, ALU.is_equal))
            small(v.tensor_scalar(wl[:, 12:13], wl[:, 0:1], -1.0, 1.0, ALU.mult, ALU.add))
            for i in range(1, NRES):
                small(v.tensor_tensor(wl[:, i:i + 1], wl[:, i:i + 1], wl[:, 12:13], ALU.mult))
                small(v.tensor_tensor(wl[:, 12:13], wl[:, 12:13], wl[:, i:i + 1], ALU.subtract))
            small(v.tensor_tensor(wl[:, 20:24], wl[:, 0:4], wl[:, 4:8], ALU.subtract))
            small(v.tensor_tensor(wl[:, 20:24], wl[:, 20:24], wl[:, 4:8], ALU.add))
            small(v.tensor_tensor(wl[:, 24:28], wl[:, 20:24], col[:, COL_RES:COL_RES + 4], ALU.mult))
            small(v.tensor_reduce(wl[:, 13:14], wl[:, 24:28], AX, ALU.add))
            dve.wait_ge(s("sig"), 2)
            small(v.tensor_tensor(wl[:, 14:15], wl[:, 13:14], wl[:, 17:18], ALU.mult))
            dve.wait_ge(s("in_c"), landed["in_c"])
            v.tensor_scalar(mixw[:, :], ksel, wl[:, 14:15], None, ALU.mult).then_inc(s("mixw"), 1)
            for k in range(2):
                dve.wait_ge(s("s0"), k + 1)
                v.tensor_reduce(nmax[:, :, 2 * k:2 * k + 2].rearrange("p h b -> p b h"), sc_bank[:, 2 * k:2 * k + 2, :, :],
                                AX, ALU.max, negate=True).then_inc(s("max0"), 1)

            def split_max(nth):
                v.tensor_copy(nmb[:, :, :], nmax[:, :, :]).then_inc(s("max_nmb"), 1)
                dve.wait_ge(s("max_nmb"), nth)
                if nth == 1:
                    dve.wait_ge(s("nmhl_zero"), 1)
                v.tensor_copy(nmhl[:, :, :, 0], nmb[:, :, :])
                v.tensor_tensor(nmhl[:, :, :, 1], nmax[:, :, :], nmb[:, :, :], ALU.subtract).then_inc(s("max_nm"), 1)
                dve.wait_ge(s("max_nmT"), 2 * nth)
                v.tensor_copy(nmt[:, :], bank(4, 256, 512)).then_inc(s("max_nmt"), 1)

            dve.wait_ge(s("max0"), 2)
            split_max(1)
            dve.wait_ge(s("o0"), 1)
            small(v.reciprocal(orec[:, :].rearrange("p (h b) -> p h b", h=NH), o_ps[:, :, :, C]))
            v.tensor_tensor(onorm[:, :, :].rearrange("p h (b c) -> p (h b) c", b=B),
                            o_ps.rearrange("p h b c -> p (h b) c")[:, :, 0:C],
                            orec[:, :, None].broadcast_to([P, NH * B, C]), ALU.mult).then_inc(s("onorm0"), 1)
            dve.wait_ge(s("oT0"), 2)
            dve.wait_ge(s("xg"), 1)
            small(v.scalar_tensor_tensor(out=x0[:, :], in0=bank(7, 0, N), scalar=col[:, COL_GAMMA:COL_GAMMA + 1],
                                         in1=xg[:, :], op0=ALU.mult, op1=ALU.add))
            small(v.bn_stats(st6[:, :], x0[:, :]))
            v.bn_aggr(st2[:, :], st6[:, :]).then_inc(s("gn_stat"), 1)
            dve.wait_ge(s("gn_stat"), 1)
            dve.wait_ge(s("gn_rstd"), 1)
            v.tensor_scalar(shifted(y3, 0, 0), x0[:, :], st2[:, 0:1], rs[:, 1:2], ALU.subtract, ALU.mult
                            ).then_inc(s("y_pad"), 1)
            dve.wait_ge(s("y_pad"), 1)
            img = y3[:, 1, 1:1 + HW, :]
            v.tensor_copy(y3[:, 0, 1:1 + HW, 1:HW], img[:, :, 0:HW - 1]).then_inc(s("y_pad"), 1)
            v.tensor_copy(y3[:, 2, 1:1 + HW, 0:HW - 1], img[:, :, 1:HW]).then_inc(s("y_pad"), 1)
            v.tensor_copy(y3[:, 0, 1:1 + HW, 0:1], img[:, :, 1:2]).then_inc(s("y_pad"), 1)
            v.tensor_copy(y3[:, 2, 1:1 + HW, HW - 1:HW], img[:, :, HW - 2:HW - 1]).then_inc(s("y_pad"), 1)
            dve.wait_ge(s("y_pad"), 5)
            v.tensor_copy(y3[:, :, 0::PAD - 1, :], y3[:, :, 2::PAD - 5, :]).then_inc(s("y_pad"), 1)
            dve.wait_ge(s("y_pad"), 6)
            for dy in (-1, 1):
                v.tensor_tensor(prod[:, 1 + dy, :, :],
                                y3[:, 1:2, 1:1 + HW, :].rearrange("p d r c -> p d (r c)").broadcast_to([P, 3, N]),
                                y3[:, :, 1 + dy:1 + dy + HW, :].rearrange("p d r c -> p d (r c)"), ALU.mult
                                ).then_inc(s("prod"), 1)
            dve.wait_ge(s("av_ps"), 1)
            v.tensor_scalar(av[:, :, :], av_ps, 1.0 / C, None, ALU.mult).then_inc(s("av"), 1)
            small(v.bn_stats(gst6[:, :], shifted(y3, 0, 0)))
            small(v.bn_aggr(gst[:, :], gst6[:, :]))
            v.tensor_copy(gme[:, 0:1], gst[:, 0:1])
            v.scalar_tensor_tensor(out=gme[:, 1:2], in0=gst[:, 0:1], scalar=gst[:, 0:1], in1=gst[:, 1:2],
                                   op0=ALU.mult, op1=ALU.add).then_inc(s("gme"), 1)
            dve.wait_ge(s("absd"), 1)
            v.tensor_reduce(dstat[:, 0:1], absd[:, :], AX, ALU.max)
            small(v.tensor_reduce(dstat[:, 1:2], absd[:, :], AX, ALU.min))
            small(v.tensor_tensor(dstat[:, 2:3], dstat[:, 0:1], dstat[:, 1:2], ALU.subtract))
            small(v.tensor_scalar(dstat[:, 3:4], dstat[:, 2:3], 1e-8, None, ALU.add))
            small(v.reciprocal(dstat[:, 4:5], dstat[:, 3:4]))
            small(v.tensor_scalar(cnt[:, :], absd[:, :], dstat[:, 1:2], dstat[:, 4:5], ALU.subtract, ALU.mult))
            v.tensor_scalar(cnt[:, :], cnt[:, :], 7.0, MAGIC, ALU.mult, ALU.add).then_inc(s("cnt"), 1)
            dve.wait_ge(s("sim_ps"), 1)
            v.tensor_scalar(n2[:, :, :], n2_ps.rearrange("p k h b -> p k (h b)"), 1e-24, None, ALU.max).then_inc(s("n2"), 1)
            dve.wait_ge(s("gpair_ps"), 1)
            small(v.tensor_copy(gmu[:, 0:2], bank(7, 0, 2)))
            small(v.tensor_tensor(gmu[:, 6:7], gmu[:, 0:1], gmu[:, 0:1], ALU.mult))
            v.tensor_tensor(gmu[:, 2:3], gmu[:, 1:2], gmu[:, 6:7], ALU.subtract).then_inc(s("gvar"), 1)
            dve.wait_ge(s("cntT_ps"), 1)
            small(v.tensor_scalar(wsum[:, :], bank(5, 256, 264), -MAGIC, None, ALU.add))
            small(v.tensor_tensor(rk[:, :, :], wsum[:, None, :].broadcast_to([P, KN, NH * B]),
                                  rankoff[:, 0:KN, None].broadcast_to([P, KN, NH * B]), ALU.add))
            dve.wait_ge(s("rn0"), 1)
            small(v.scalar_tensor_tensor(out=nt[:, :, :], in0=n2[:, :, :], scalar=-0.5, in1=rn[:, :, :],
                                         op0=ALU.mult, op1=ALU.mult))
            small(v.tensor_tensor(nt[:, :, :], nt[:, :, :], rn[:, :, :], ALU.mult))
            small(v.scalar_tensor_tensor(out=n2[:, :, :], in0=nt[:, :, :], scalar=1.5, in1=rn[:, :, :],
                                         op0=ALU.add, op1=ALU.mult))
            small(v.tensor_tensor(sim[:, :, :], sim_ps.rearrange("p k h b -> p k (h b)"), n2[:, :, :], ALU.mult))
            v.tensor_tensor(sim[:, :, :], sim[:, :, :], n2[:, 4:5, :].broadcast_to([P, KN, NH * B]), ALU.mult
                            ).then_inc(s("sim"), 1)
            dve.wait_ge(s("sim"), 1)
            shape = [P, KN, KN, NH * B]
            small(v.tensor_tensor(ge[:, :, :, :], sim[:, :, None, :].broadcast_to(shape),
                                  sim[:, None, :, :].broadcast_to(shape), ALU.is_ge))
            small(v.tensor_tensor(ge[:, :, :, :], ge[:, :, :, :], lower[:, :, :, None].broadcast_to(shape), ALU.mult))
            small(v.tensor_tensor(gd[:, :, :, :], ge[:, :, :, :], ge[:, :, :, :].rearrange("p j k g -> p k j g"),
                                  ALU.subtract))
            dve.wait_ge(s("grstd"), 1)
            small(v.tensor_tensor(gmu[:, 5:6], gmu[:, 4:5], col[:, COL_GNW:COL_GNW + 1], ALU.mult))
            small(v.tensor_tensor(gmu[:, 6:7], gmu[:, 0:1], gmu[:, 5:6], ALU.mult))
            v.tensor_tensor(gmu[:, 7:8], col[:, COL_GNB:COL_GNB + 1], gmu[:, 6:7], ALU.subtract).then_inc(s("gab"), 1)
            small(v.tensor_reduce(rank[:, :, :], gd[:, :, :, :].rearrange("p j k g -> p k g j"), AX, ALU.add))
            small(v.tensor_tensor(rank[:, :, :], rank[:, :, :], rk[:, :, :], ALU.is_le))
            dve.wait_ge(s("simexp"), 1)
            small(v.tensor_tensor(wts[:, :, :], wts[:, :, :], rank[:, :, :], ALU.mult))
            small(v.tensor_reduce(wsum[:, :], wts[:, :, :].rearrange("p k g -> p g k"), AX, ALU.add))
            small(v.reciprocal(wsum[:, :], wsum[:, :]))
            small(v.tensor_tensor(wts[:, :, :], wts[:, :, :], wsum[:, None, :].broadcast_to([P, KN, NH * B]), ALU.mult))
            dve.wait_ge(s("pt_ps"), KN)
            dve.wait_ge(s("gtap_ps"), 4)
            for k in range(KN):
                src = pt_a[:, k, :, :] if k < 8 else pt_b
                v.tensor_tensor(wprod[:, k, :, :].rearrange("p h (b c) -> p (h b) c", b=B),
                                src.rearrange("p h (b c) -> p (h b) c", b=B),
                                wts[:, k, :, None].broadcast_to([P, NH * B, C]), ALU.mult).then_inc(s("wprod"), 1)
            dve.wait_ge(s("att1_ps"), 1)
            dve.wait_ge(s("gy"), 1)
            v.tensor_tensor(enh[:, :], bank(7, 0, N), gy[:, :], ALU.add).then_inc(s("enh"), 1)
            dve.wait_ge(s("enh"), 1)
            small(v.tensor_tensor(xe[:, :], enh[:, :], x0[:, :], ALU.add))
            dve.wait_ge(s("hid_ps"), 2)
            v.tensor_scalar(hid[:, 1, :], bank(0, 0, N), col[:, COL_B1:COL_B1 + 1], 0.0, ALU.add, ALU.max
                            ).then_inc(s("hid_b"), 1)
            dve.wait_ge(s("mlp_ps"), 1)
            v.scalar_tensor_tensor(out=x1[:, :], in0=bank(5, 0, N), scalar=col[:, COL_B2:COL_B2 + 1], in1=xe[:, :],
                                   op0=ALU.add, op1=ALU.add).then_inc(s("x1"), 1)
            dve.wait_ge(s("in_d"), landed["in_d"])
            small(v.tensor_scalar(mumix[:, :], mu_sb[:, 0, :], wl[:, 20:21], None, ALU.mult))
            for i in range(1, NRES):
                small(v.scalar_tensor_tensor(out=mumix[:, :], in0=mu_sb[:, i, :], scalar=wl[:, 20 + i:21 + i],
                                             in1=mumix[:, :], op0=ALU.mult, op1=ALU.add))
            dve.wait_ge(s("gtap"), 4)
            v.tensor_tensor(gtap[:, :, 0:TAPS], gtap[:, :, 0:TAPS],
                            mumix[:, :].rearrange("p (g l) -> p g l", g=8), ALU.add).then_inc(s("gtap_mu"), 1)
            small(v.tensor_scalar(segm[:, :], seg[:, 0, :], wl[:, 0:1], None, ALU.mult))
            for i in range(1, NRES):
                small(v.scalar_tensor_tensor(out=segm[:, :], in0=seg[:, i, :], scalar=wl[:, i:i + 1], in1=segm[:, :],
                                             op0=ALU.mult, op1=ALU.add))
            dve.wait_ge(s("w2h_ps"), 1)
            w2p = ps[0:XA, 1, :].rearrange("p (h e) -> p h e", h=HEADS)
            v.tensor_scalar(w2h[:, :, 0:C], w2p, col[0:XA, COL_MCOS:COL_MCOS + 1], None, ALU.mult)
            v.tensor_scalar(w2h[:, :, C:2 * C], w2p, col[0:XA, COL_MSIN:COL_MSIN + 1], None, ALU.mult)
            v.tensor_copy(w2h[:, :, 2 * C:2 * C + 2], kone_sb[:, None, :].broadcast_to([XA, HEADS, 2])).then_inc(s("w2h"), 1)
            ln_apply(1, xln[:, :])
            dve.wait_ge(s("gq_ps"), 1)
            v.tensor_copy(gq[:, :], bank(7, 0, N)).then_inc(s("gq"), 1)
            dve.wait_ge(s("s2"), 1)
            v.tensor_reduce(nmax[:, 0, :], ps[:, 0:4, 0:128], AX, ALU.max, negate=True)
            v.tensor_reduce(nmax[:, 1, :], ps[:, 0:4, 128:384], AX, ALU.max, negate=True).then_inc(s("max2"), 1)
            dve.wait_ge(s("max2"), 1)
            split_max(2)
            o2 = bank(6, 0, NH * B * (C + 1)).rearrange("p (h b c) -> p h b c", h=NH, b=B)
            dve.wait_ge(s("o2"), 1)
            small(v.reciprocal(orec[:, :].rearrange("p (h b) -> p h b", h=NH), o2[:, :, :, C]))
            v.tensor_tensor(onorm[:, :, :].rearrange("p h (b c) -> p (h b) c", b=B),
                            o2.rearrange("p h b c -> p (h b) c")[:, :, 0:C],
                            orec[:, :, None].broadcast_to([P, NH * B, C]), ALU.mult).then_inc(s("onorm2"), 1)
            dve.wait_ge(s("oT2"), 2)
            v.tensor_tensor(t2[:, :], x1[:, :], bank(5, 0, N), ALU.add).then_inc(s("t2"), 1)
            ln_apply(2, xln[:, :])
            dve.wait_ge(s("ln_xln"), 2)
            v.transpose(xtr[:, :, :, :], xln[:, :].rearrange("p (h a r) -> p h r a", h=2, r=PH)).then_inc(s("xtr"), 1)
            dve.wait_ge(s("y_ps"), 1)
            v.tensor_tensor(ys[:, :, :, :], bank(0, 0, N).rearrange("p (b h a) -> p h b a", b=B, h=2),
                            segm[:, :].rearrange("p (h a) -> p h a", h=2)[:, :, None, :].broadcast_to([P, 2, B, NA // 2]),
                            ALU.mult).then_inc(s("ys"), 1)
            dve.wait_ge(s("z_ps"), 2)
            small(v.transpose(ych[:, :].rearrange("p (h r a) -> p h r a", h=2, r=PH),
                              bank(1, 0, N).rearrange("p (h r a) -> p h r a", h=2, r=PH)))
            v.tensor_tensor(t3[:, :].rearrange("p (h a r) -> p h a r", h=2, r=PH),
                            t2[:, :].rearrange("p (h a r) -> p h a r", h=2, r=PH),
                            ych[:, :].rearrange("p (h r a) -> p h a r", h=2, r=PH), ALU.add).then_inc(s("t3"), 1)
            ln_apply(3, xln[:, :])
            dve.wait_ge(s("xT3"), 2)
            for h in range(NH):
                src = bank(7, 128 * h, 128 * h + 128).rearrange("p (b c) -> p b c", b=B)
                v.tensor_scalar(xa[:, h, :, 0:C], src, col[:, COL_COS + h:COL_COS + h + 1], None, ALU.mult)
                v.tensor_scalar(xa[:, h, :, C + 1:2 * C + 1], src, col[:, COL_SIN + h:COL_SIN + h + 1], None, ALU.mult)
                v.tensor_copy(xa[:, h, :, C], col[:, COL_COS + h:COL_COS + h + 1].broadcast_to([P, B]))
                v.tensor_copy(xa[:, h, :, 2 * C + 1], col[:, COL_SIN + h:COL_SIN + h + 1].broadcast_to([P, B])
                              ).then_inc(s("xa"), 1)
            dve.wait_ge(s("t3T"), 2)
            v.tensor_tensor(t3b[:, :, :], bank(4, 0, 256).rearrange("p (h n) -> p h n", h=NH),
                            denseb_sb[:, None, :].broadcast_to([P, NH, P]), ALU.add).then_inc(s("t3b"), 1)
            for t in range(16):
                dve.wait_ge(s("qk3_exp"), t + 1)
                if t < 8:
                    dst, z, e = kf[:, t // 2, t % 2, :], bank(t % 4), ee[:, t % 4, :]
                else:
                    g0 = 2 * (t % 2)
                    dst = qf[:, g0:g0 + 2, (t - 8) // 2, :]
                    z = bank(t % 4).rearrange("p (g n) -> p g n", g=2)
                    e = ee[:, t % 4, :].rearrange("p (g n) -> p g n", g=2)
                v.scalar_tensor_tensor(out=dst, in0=e, scalar=1.0, in1=z, op0=ALU.min, op1=ALU.max
                                       ).then_inc(s("qk3"), 1)
            dve.wait_ge(s("kvd"), 4)
            v.tensor_tensor(ksb[:, :, :, :],
                            kvd[:, :, :, 64:66].rearrange("p b g t -> p (b g) t")[:, :, None, :].broadcast_to(
                                [P, B * HG, 4, 2]),
                            col[:, None, COL_KVM:COL_KVM + 4, None].broadcast_to([P, B * HG, 4, 2]), ALU.mult
                            ).then_inc(s("ksb"), 1)
            dve.wait_ge(s("den_ps"), 1)
            dps = bank(4, 0, 256).rearrange("p (h g t) -> p h g t", h=NH, t=2)
            for h in range(NH):
                v.tensor_scalar(den[:, h, :], dps[:, h, :, 0], col[:, COL_COS + h:COL_COS + h + 1], 1e-5,
                                ALU.mult, ALU.add).then_inc(s("den_c"), 1)
            dve.wait_ge(s("den_c"), 2)
            for h in range(NH):
                v.scalar_tensor_tensor(out=den[:, h, :], in0=dps[:, h, :, 1], scalar=col[:, COL_SIN + h:COL_SIN + h + 1],
                                       in1=den[:, h, :], op0=ALU.mult, op1=ALU.add).then_inc(s("den_c"), 1)
            dve.wait_ge(s("den_c"), 4)
            small(v.reciprocal(den[:, :, :], den[:, :, :]))
            dv = den[:, :, :].rearrange("p h (b k) -> p (h b) k", b=B)

            def r3v(k):
                return r3[:, :, :, :].rearrange("p h b n -> p (h b) n")[:, :, 16 * k:16 * k + 16]

            dve.wait_ge(s("r3_zero"), 1)
            small(v.tensor_copy(r3v(0), dv))
            small(v.tensor_tensor(dv, dv, r3v(0), ALU.subtract))
            small(v.tensor_copy(r3v(1), dv))
            small(v.tensor_tensor(dv, dv, r3v(1), ALU.subtract))
            v.tensor_copy(r3v(2), dv).then_inc(s("r3"), 1)
            for t in range(8):
                dve.wait_ge(s("rb_ps"), t + 1)
                b, gp = t // 2, t % 2
                dst = qf[:, 2 * gp:2 * gp + 2, b, :]
                v.tensor_tensor(dst, dst, bank(t % 4).rearrange("p (g n) -> p g n", g=2), ALU.mult).then_inc(s("qs"), 1)
            dve.wait_ge(s("y3_ps"), 1)
            yp = bank(6).rearrange("p (h b n) -> p h b n", h=NH, b=B)
            for h in range(NH):
                v.scalar_tensor_tensor(out=t4a[:, h, :].rearrange("p (b c) -> p b c", b=B), in0=yp[:, h, :, 0:C],
                                       scalar=col[:, COL_COS + h:COL_COS + h + 1],
                                       in1=t3b[:, h, :].rearrange("p (b c) -> p b c", b=B),
                                       op0=ALU.mult, op1=ALU.add).then_inc(s("t4a"), 1)
            dve.wait_ge(s("t4a"), 2)
            for h in range(NH):
                v.scalar_tensor_tensor(out=t4[:, h, :].rearrange("p (b c) -> p b c", b=B), in0=yp[:, h, :, C:2 * C],
                                       scalar=col[:, COL_SIN + h:COL_SIN + h + 1],
                                       in1=t4a[:, h, :].rearrange("p (b c) -> p b c", b=B),
                                       op0=ALU.mult, op1=ALU.add).then_inc(s("t4"), 1)
            dve.wait_ge(s("t4"), 2)
            t4g = t4[:, :, :].rearrange("p h (b c) -> p (h b) c", b=B)
            small(v.tensor_reduce(mn4[:, :], t4g, AX, ALU.add))
            small(v.tensor_scalar(mn4[:, :], mn4[:, :], 1.0 / C, None, ALU.mult))
            v.tensor_tensor(xc4[:, :, :], t4g, mn4[:, :, None].broadcast_to([P, NH * B, C]), ALU.subtract
                            ).then_inc(s("xc4"), 1)
            dve.wait_ge(s("sq4"), 1)
            v.tensor_reduce(rs4[:, :], sq4[:, :, :], AX, ALU.add).then_inc(s("var4"), 1)
            dve.wait_ge(s("rs4"), 1)
            dve.wait_ge(s("xc4"), 1)
            v.tensor_tensor(xl4t[:, :, :].rearrange("p h (b c) -> p (h b) c", b=B), xc4[:, :, :],
                            rs4[:, :, None].broadcast_to([P, NH * B, C]), ALU.mult).then_inc(s("xl4t"), 1)
            dve.wait_ge(s("rout_ps"), 1)
            dve.wait_ge(s("in_g"), landed["in_g"])
            small(v.tensor_tensor(lg[:, :, :].rearrange("p g e -> p (g e)"), bank(5, 0, 64), routb_sb[:, :], ALU.add))
            small(v.tensor_reduce(lm[:, :], lg[:, :, :], AX, ALU.max))
            v.tensor_tensor(lx[:, :, :], lg[:, :, :], lm[:, :, None].broadcast_to([P, NH * B, NE]), ALU.subtract
                            ).then_inc(s("lx0"), 1)
            shape4 = [P, NH * B, NE, NE]
            small(v.tensor_tensor(ge4[:, :, :, :], lg[:, :, :, None].broadcast_to(shape4),
                                  lg[:, :, None, :].broadcast_to(shape4), ALU.is_ge))
            small(v.tensor_tensor(ge4[:, :, :, :], ge4[:, :, :, :],
                                  lower[:, None, 0:NE, 0:NE].broadcast_to(shape4), ALU.mult))
            small(v.tensor_tensor(gd4[:, :, :, :], ge4[:, :, :, :].rearrange("p g j k -> p g k j"), ge4[:, :, :, :],
                                  ALU.subtract))
            small(v.tensor_reduce(rank4[:, :, :], gd4[:, :, :, :], AX, ALU.add))
            small(v.tensor_tensor(rank4[:, :, :], rank4[:, :, :],
                                  rankoff[:, None, 2:2 + NE].broadcast_to([P, NH * B, NE]), ALU.is_le))
            dve.wait_ge(s("lexp4"), 1)
            small(v.tensor_tensor(lx[:, :, :], lx[:, :, :], rank4[:, :, :], ALU.mult))
            small(v.tensor_reduce(lm[:, :], lx[:, :, :], AX, ALU.add))
            small(v.reciprocal(lm[:, :], lm[:, :]))
            small(v.tensor_tensor(lx[:, :, :], lx[:, :, :], lm[:, :, None].broadcast_to([P, NH * B, NE]), ALU.mult))
            dve.wait_ge(s("exp_ps"), 1)
            for h in range(NH):
                for b in range(B):
                    src = sc_bank[:, b, h, :].rearrange("p (e c) -> p e c", e=NE)
                    v.tensor_tensor(eprod[:, :, h, C * b:C * b + C], src,
                                    lx[:, B * h + b, :, None].broadcast_to([P, NE, C]), ALU.mult).then_inc(s("eprod"), 1)

        @block.tensor
        def _(pe):
            t = nc.tensor

            def strip(tile, b, lo=0, hi=N, rows=32):
                return tile[32 * b:32 * b + rows, lo:hi]

            def ln_matmuls(nth, src):
                for k in (6, 5):
                    t.matmul(bank(k, 0, N), center, src, start=True, stop=True).then_inc(s("ln_center"), 1)
                pe.wait_ge(s("ln_sq"), nth)
                t.matmul(bank(6, 256, 512), meanw, sq[:, :], start=True, stop=True).then_inc(s("ln_var"), 1)

            def max_rows(nth):
                pe.wait_ge(s("max_nm"), nth)
                for h in range(NH):
                    t.transpose(bank(4, 256 + 128 * h, 384 + 128 * h),
                                nmhl[:, h, :, :].rearrange("p b c -> p (b c)"), ident).then_inc(s("max_nmT"), 1)
                pe.wait_ge(s("max_nmt"), nth)

            pe.wait_ge(s("in_a"), landed["in_a"])
            for k in range(2):
                t.matmul(bank(4 + 3 * k, 0, N), w0_sb[:, k, :], x_cl[:, :], start=True, stop=True
                         ).then_inc(s("qk0"), 1)
            for h in range(NH):
                mm = t.matmul(bank(5, 128 * h, 128 * h + 128), x_cl[:, 128 * h:128 * h + 128], w0_sb[:, 2, :],
                              start=True, stop=True)
            mm.then_inc(s("v0_ps"), 1)
            pe.wait_ge(s("q0"), 1)
            pe.wait_ge(s("k0"), 1)
            for b in range(B):
                for h in range(NH):
                    mm = t.matmul(sc_bank[:, b, h, :], strip(q0, b, 128 * h, 128 * h + 128, 4), strip(k0, b, rows=4),
                                  start=True, stop=True)
                if b % 2:
                    mm.then_inc(s("s0"), 1)
            pe.wait_ge(s("in_d"), landed["in_d"])
            t.matmul(bank(6, 0, P), wl2_sb[:, 0, :], wl2_sb[:, 1, :], start=True, stop=True).then_inc(s("abd_ps"), 1)
            pe.wait_ge(s("mixw"), 1)
            pe.wait_ge(s("abd"), 1)
            pe.wait_ge(s("k0"), 1)
            for k in range(2):
                t.matmul(ps[0:2 * KF, 6 + k, :], mixw[:, :], mstu_sb[:, 512 * k:512 * k + 512], start=True, stop=True
                         ).then_inc(s("ms_ps"), 1)
            pe.wait_ge(s("in_b"), landed["in_b"])
            max_rows(1)
            pe.wait_ge(s("ones_bf"), 1)
            for b in range(B):
                for h in range(NH):
                    t.matmul(sc_bank[:, b, h, :], strip(k0, b, 128 * h, 128 * h + 128, 4), strip(q0, b, rows=4),
                             start=True, stop=False)
                    mm = t.matmul(sc_bank[:, b, h, :], strip(ones_bf, b, 0, P, 2), strip(nmt, b, rows=2), start=False, stop=True)
                mm.then_inc(s("sT0"), 1)
            pe.wait_ge(s("v0"), 2)
            pe.wait_ge(s("vaug_one"), 1)
            pe.wait_ge(s("ms"), 2)
            for b in range(B):
                pe.wait_ge(s("pT0"), b + 1)
                for h in range(NH):
                    for m in range(NH):
                        mm = t.matmul(o_ps[:, h, b, :], pT[:, b, m, 128 * h:128 * h + 128], vaug[:, m, b, :],
                                      start=(m == 0), stop=(m == NH - 1))
            mm.then_inc(s("o0"), 1)
            pe.wait_ge(s("onorm0"), 1)
            for h in range(NH):
                t.transpose(bank(7, 128 * h, 128 * h + 128), onorm[:, h, :], ident).then_inc(s("oT0"), 1)

            pe.wait_ge(s("phi"), 1)
            for eg in range(8):
                mm = t.matmul(bank(eg // 2, 256 * (eg % 2), 256 * (eg % 2) + 256), ms[:, 128 * eg:128 * eg + 128],
                              phi_sb[:, :], start=True, stop=True)
                if eg % 2:
                    mm.then_inc(s("gtap_ps"), 1)

            pe.wait_ge(s("y_pad"), 1)
            for h in range(NH):
                mm = t.matmul(av_ps[:, h, :], shifted(y3, 0, 0, h), bo, start=True, stop=True)
            mm.then_inc(s("av_ps"), 1)
            pe.wait_ge(s("y_pad"), 6)
            pe.wait_ge(s("ysq"), 1)
            pe.wait_ge(s("prod"), 2)
            pe.wait_ge(s("prod_side"), 2)
            for k, (dy, dx) in enumerate(nbr):
                for h in range(NH):
                    t.matmul(n2_ps[:, k, h, :], shifted(sq3, dy, dx, h), bo, start=True, stop=True)
                    pair = (prod[:, 1 + dy, 1 + dx, 128 * h:128 * h + 128] if (dy, dx) != (0, 0)
                            else shifted(sq3, 0, 0, h))
                    mm = t.matmul(sim_ps[:, k, h, :], pair, bo, start=True, stop=True)
            mm.then_inc(s("sim_ps"), 1)
            pe.wait_ge(s("av"), 1)
            pe.wait_ge(s("in_c"), landed["in_c"])
            for h in range(NH):
                mm = t.matmul(ps[0:B, 5, 0:N], av[:, h, :], lap[:, h, :], start=(h == 0), stop=(h == NH - 1))
            mm.then_inc(s("lap_ps"), 1)
            pe.wait_ge(s("gme"), 1)
            t.matmul(bank(7, 0, 2), pairw, gme[:, :], start=True, stop=True).then_inc(s("gpair_ps"), 1)
            pe.wait_ge(s("gtap"), 4)
            for k, (dy, dx) in enumerate(nbr):
                for h in range(NH):
                    mm = t.transpose(pt_a[:, k, h, :] if k < 8 else pt_b[:, h, :], shifted(y3, dy, dx, h), ident)
                mm.then_inc(s("pt_ps"), 1)
            pe.wait_ge(s("cnt"), 1)
            for h in range(NH):
                mm = t.transpose(bank(5, 256 + B * h, 260 + B * h), cnt[:, 128 * h:128 * h + 128], ident[0:B, 0:B])
            mm.then_inc(s("cntT_ps"), 1)
            for k in range(KN):
                pe.wait_ge(s("wprod"), k + 1)
                for h in range(NH):
                    mm = t.matmul(bank(7, 128 * h, 128 * h + 128), wprod[:, k, h, :], ident, start=(k == 0 and h == 0),
                                  stop=(k == KN - 1), skip_group_check=True)
            mm.then_inc(s("att1_ps"), 1)
            pe.wait_ge(s("in_e"), landed["in_e"])
            pe.wait_ge(s("enh"), 1)
            for j in range(2):
                t.matmul(bank(4 - 4 * j, 0, N), wmlp1_sb[:, j, :], enh[:, :], start=True, stop=True
                         ).then_inc(s("hid_ps"), 1)
            pe.wait_ge(s("hid_a"), 1)
            t.matmul(bank(5, 0, N), wmlp2_sb[:, 0, :], hid[:, 0, :], start=True, stop=False)
            pe.wait_ge(s("hid_b"), 1)
            t.matmul(bank(5, 0, N), wmlp2_sb[:, 1, :], hid[:, 1, :], start=False, stop=True).then_inc(s("mlp_ps"), 1)
            pe.wait_ge(s("in_f"), landed["in_f"])
            for g in range(HG):
                mm = t.matmul(ps[0:XA, 1, 128 * g:128 * g + 128], wva_sb[:, g, :], dwbd_sb[:, g, :], start=True, stop=True)
            mm.then_inc(s("w2h_ps"), 1)

            pe.wait_ge(s("x1"), 1)
            ln_matmuls(1, x1[:, :])
            pe.wait_ge(s("ln_xln"), 1)
            t.matmul(bank(7, 0, N), abd[:, :], xln[:, :], start=True, stop=True).then_inc(s("gq_ps"), 1)
            for h in range(NH):
                mm = t.matmul(bank(4, 128 * h, 128 * h + 128), xln[:, 128 * h:128 * h + 128], wl2_sb[:, 2, :],
                              start=True, stop=True)
            mm.then_inc(s("v2_ps"), 1)
            pe.wait_ge(s("gq"), 1)
            pe.wait_ge(s("causal_bf"), 1)
            pe.wait_ge(s("ident_bf"), 1)
            for b in range(B):
                t.matmul(bank(b, 0, 128), strip(gq, b, 0, 128), strip(xln, b, 0, 128), start=True, stop=False)
                t.matmul(bank(b, 0, 128), ident_bf[:, :], causal_bf[:, 0, :], start=False, stop=True)
                t.matmul(bank(b, 128, 384), strip(gq, b, 128, 256), strip(xln, b), start=True, stop=False)
                mm = t.matmul(bank(b, 256, 384), ident_bf[:, :], causal_bf[:, 0, :], start=False, stop=True)
            mm.then_inc(s("s2"), 1)
            pe.wait_ge(s("v2"), 2)
            max_rows(2)
            for b in range(B):
                t.matmul(bank(b, 0, 256), strip(xln, b, 0, 128), strip(gq, b), start=True, stop=False)
                t.matmul(bank(b, 0, 128), ident_bf[:, :], causal_bf[:, 1, :], start=False, stop=False)
                t.matmul(bank(b, 0, 256), strip(ones_bf, b, 0, P, 2), strip(nmt, b, rows=2), start=False, stop=True)
                t.matmul(bank(b, 256, 384), strip(xln, b, 128, 256), strip(gq, b, 128, 256), start=True, stop=False)
                t.matmul(bank(b, 256, 384), ident_bf[:, :], causal_bf[:, 1, :], start=False, stop=False)
                t.matmul(bank(b, 256, 384), strip(ones_bf, b, 0, P, 2), strip(nmt, b, 128, 256, 2), start=False, stop=True
                         ).then_inc(s("sT2"), 1)
            pe.wait_ge(s("v2"), 2)
            o2 = bank(6, 0, NH * B * (C + 1)).rearrange("p (h b c) -> p h b c", h=NH, b=B)
            for b in range(B):
                pe.wait_ge(s("pT2"), b + 1)
                pb = pT[:, b, :, :].rearrange("p h n -> p (h n)")
                t.matmul(o2[:, 0, b, :], pb[:, 0:128], vaug[:, 0, b, :], start=True, stop=True)
                t.matmul(o2[:, 1, b, :], pb[:, 128:256], vaug[:, 0, b, :], start=True, stop=False)
                mm = t.matmul(o2[:, 1, b, :], pb[:, 256:384], vaug[:, 1, b, :], start=False, stop=True)
            mm.then_inc(s("o2"), 1)
            pe.wait_ge(s("onorm2"), 1)
            for h in range(NH):
                t.transpose(bank(5, 128 * h, 128 * h + 128), onorm[:, h, :], ident).then_inc(s("oT2"), 1)

            pe.wait_ge(s("t2"), 1)
            ln_matmuls(2, t2[:, :])
            pe.wait_ge(s("xtr"), 1)
            for h in range(2):
                t.transpose(bank(7, 128 * h, 128 * h + 128), xtr[:, h, :, :].rearrange("p r d -> p (r d)"), ident
                            ).then_inc(s("u4_ps"), 1)
            pe.wait_ge(s("u4"), 1)
            pe.wait_ge(s("ftap"), 4)
            yv = bank(0, 0, N).rearrange("p (b a) -> p b a", b=B)
            for j in range(NA):
                mm = t.matmul(yv[:, :, j:NA], ftap[:, PH * j:PH * j + PH, :].rearrange("p r e -> p (r e)"),
                              u4[:, :, 0:NA - j], start=(j == 0), stop=(j == NA - 1))
            mm.then_inc(s("y_ps"), 1)
            pe.wait_ge(s("ys"), 1)
            for h in range(2):
                t.transpose(bank(1, 128 * h, 128 * h + 128), ys[:, h, :, :].rearrange("p b a -> p (b a)"), ident).then_inc(s("z_ps"), 1)

            pe.wait_ge(s("t3"), 1)
            ln_matmuls(3, t3[:, :])
            for h in range(NH):
                t.transpose(bank(4, 128 * h, 128 * h + 128), t3[:, 128 * h:128 * h + 128], ident
                            ).then_inc(s("t3T"), 1)
            pe.wait_ge(s("ln_xln"), 3)
            for h in range(NH):
                t.transpose(bank(7, 128 * h, 128 * h + 128), xln[:, 128 * h:128 * h + 128], ident).then_inc(s("xT3"), 1)
            pe.wait_ge(s("in_g"), landed["in_g"])
            pe.wait_ge(s("brow"), 16 * 3 * B)
            pe.wait_ge(s("ones_bf"), 1)

            def key_values(b):
                for h in range(NH):
                    pe.wait_ge(s("qk3"), 2 * b + h + 1)
                    if b == 0:
                        pe.wait_ge(s("xa"), h + 1)
                        pe.wait_ge(s("t3b"), 1)
                    if b >= 2 and h == 0:
                        pe.wait_ge(s("kxt"), b - 1)
                    mm = t.matmul(ps[0:XA, 4 + b % 2, :], xa[:, h, b, :], kf[:, b, h, :], start=(h == 0),
                                  stop=(h == NH - 1))
                mm.then_inc(s("kxt_ps"), 1)

            for n in range(16):
                if n >= 4:
                    pe.wait_ge(s("qk3"), n - 3)
                if n < 8:
                    b, h = n // 2, n % 2
                    t.matmul(bank(n % 4), strip(xln, b, 128 * h, 128 * h + 128), wk3_sb[32 * b:32 * b + 32, :],
                             start=True, stop=False)
                    t.matmul(bank(n % 4), strip(ones_bf, b, 0, P, 3), strip(brow, b, 512, 1024, 3), start=False, stop=True
                             ).then_inc(s("qk3_ps"), 1)
                else:
                    b, gp = (n - 8) // 2, n % 2
                    for g in (2 * gp, 2 * gp + 1):
                        o = bank(n % 4, 256 * (g % 2), 256 * (g % 2) + 256)
                        t.matmul(o, wq3_sb[32 * b:32 * b + 32, 128 * g:128 * g + 128], strip(xln, b),
                                 start=True, stop=False)
                        mm = t.matmul(o, strip(brow, b, 128 * g, 128 * g + 128, 3), strip(ones_bf, b, rows=3),
                                      start=False, stop=True)
                    mm.then_inc(s("qk3_ps"), 1)
                if n in (5, 7, 9, 11):
                    key_values((n - 5) // 2)
            pe.wait_ge(s("w2h"), 1)
            for b in range(B):
                pe.wait_ge(s("kxt"), b + 1)
                if b >= 2:
                    pe.wait_ge(s("kvd"), b - 1)
                for hd in range(HEADS):
                    q = 32 * (hd % 4)
                    mm = t.matmul(ps[q:q + 32, 6 + b % 2, 66 * (hd // 4):66 * (hd // 4) + 66],
                                  kxt[:, b, 32 * hd:32 * hd + 32], w2h[:, hd, :], start=True, stop=True,
                                  tile_position=(0, q))
                mm.then_inc(s("kvd_ps"), 1)
            pe.wait_ge(s("ksb"), 1)
            pe.wait_ge(s("qk3"), 16)
            for h in range(NH):
                for b in range(B):
                    for g in range(HG):
                        c0 = 128 * h + 32 * b + 8 * g
                        mm = t.matmul(bank(4, c0, c0 + 8), qf[:, g, b, 128 * h:128 * h + 128],
                                      ksb[:, HG * b + g, :, :].rearrange("p k t -> p (k t)"), start=True, stop=True)
            mm.then_inc(s("den_ps"), 1)
            pe.wait_ge(s("r3"), 1)
            pe.wait_ge(s("selr_bf"), 1)
            for bp in range(2):
                for h in range(NH):
                    o = ps[:, 5, 128 * bp + 64 * h:128 * bp + 64 * h + 64].bitcast(BF16)
                    t.transpose(o, r3[:, h, 2 * bp:2 * bp + 2, :].rearrange("p b n -> p (b n)"), ident_bf[:, :]
                                ).then_inc(s("rT_ps"), 1)
            pe.wait_ge(s("rT"), 1)
            yo = bank(6).rearrange("p (h b n) -> p h b n", h=NH, b=B)

            def spread(n):
                b, gp = n // 2, n % 2
                if n >= 4:
                    pe.wait_ge(s("qs"), n - 3)
                q = 64 * (b % 2)
                for g in (2 * gp, 2 * gp + 1):
                    mm = t.matmul(bank(n % 4, 256 * (g % 2), 256 * (g % 2) + 256), selr_bf[q:q + 48, g, :],
                                  rT[q:q + 48, b // 2, :], start=True, stop=True)
                mm.then_inc(s("rb_ps"), 1)

            for n in range(4):
                spread(n)
            for b in range(B):
                pe.wait_ge(s("qs"), 2 * b + 2)
                for h in range(NH):
                    for g in range(HG):
                        mm = t.matmul(yo[:, h, b, :], qf[:, g, b, 128 * h:128 * h + 128], kvd[:, b, g, 0:64],
                                      start=(g == 0), stop=(g == HG - 1))
                if b == B - 1:
                    mm.then_inc(s("y3_ps"), 1)
                for n in (2 * b + 4, 2 * b + 5):
                    if n < 8:
                        spread(n)

            pe.wait_ge(s("xl4t"), 1)
            for h in range(NH):
                t.transpose(bank(7, 128 * h, 128 * h + 128), xl4t[:, h, :], ident).then_inc(s("xl4_ps"), 1)
            pe.wait_ge(s("xl4"), 1)
            for h in range(NH):
                mm = t.matmul(bank(5, 32 * h, 32 * h + 32), xl4[:, 128 * h:128 * h + 128], wrout_sb[:, :],
                              start=True, stop=True)
            mm.then_inc(s("rout_ps"), 1)
            for h in range(NH):
                for b in range(B):
                    t.matmul(sc_bank[:, b, h, :], strip(xl4, b, 128 * h, 128 * h + 128),
                             wexp_sb[32 * b:32 * b + 32, :], start=True, stop=False)
                    mm = t.matmul(sc_bank[:, b, h, :], strip(ones_bf, b, 0, P, 3), strip(brow, b, 1024, 1280, 3), start=False, stop=True)
            mm.then_inc(s("exp_ps"), 1)
            for h in range(NH):
                t.matmul(bank(4, 128 * h, 128 * h + 128), t4[:, h, :], ident, start=True, stop=False)
                pe.wait_ge(s("eprod"), 4 * h + 4)
                for e in range(NE):
                    mm = t.matmul(bank(4, 128 * h, 128 * h + 128), eprod[:, e, h, :], ident, start=False,
                                  stop=(e == NE - 1))
            mm.then_inc(s("fin_ps"), 1)


def blocks(m):
    m = np.asarray(m)
    r, c = m.shape
    o = np.zeros((4 * r, 4 * c), m.dtype)
    for b in range(4):
        o[b * r:(b + 1) * r, b * c:(b + 1) * c] = m
    return o


def constants():
    f = np.float32
    eye = np.eye(P, dtype=f)
    ones = np.kron(np.eye(4, dtype=f), np.ones((32, 32), f))
    c1 = np.concatenate([eye, eye - ones / f(C), ones / f(C), np.kron(np.eye(4, dtype=f), np.ones((32, 1), f))], 1)
    lap = np.zeros((N, N), f)
    for r in range(HW):
        for c in range(HW):
            lap[r * HW + c, r * HW + c] = 4
            for dr, dc in ((0, 1), (0, -1), (1, 0), (-1, 0)):
                if 0 <= r + dr < HW and 0 <= c + dc < HW:
                    lap[(r + dr) * HW + c + dc, r * HW + c] = -1
    lower = (np.arange(KN)[:, None] < np.arange(KN)[None, :]).astype(f)
    rankoff = np.arange(NE + 2, dtype=f) - 8
    pair = np.kron(np.eye(64, dtype=f), np.full((2, 2), 0.5, f))
    i = np.arange(P)
    c2 = np.concatenate([
        lap.reshape(NH, P, N).transpose(1, 0, 2).reshape(P, -1),
        np.broadcast_to(lower.reshape(1, -1), (P, KN * KN)),
        np.broadcast_to(rankoff, (P, NE + 2)), pair,
        np.where(i[None, :] > i[:, None], MASKED, 0).astype(f),
        np.where(i[:, None] > i[None, :], MASKED, 0).astype(f)], 1)
    seg = np.stack([(np.arange(NA) < NA >> k) for k in range(NRES)]).astype(f)
    selr = np.zeros((2, 64, HG, 4, 32), f)
    for k in range(3):
        for hd in range(HEADS):
            selr[:, 16 * k + hd, hd // 4, hd % 4, :] = 1
    ksel = np.tile(np.eye(2 * KF, dtype=f), (NRES, 1))
    c3 = np.concatenate([np.broadcast_to(seg.reshape(1, -1), (P, NRES * NA)), selr.reshape(P, -1), ksel], 1)
    pos = f(1.57) * np.arange(N, dtype=f) / f(N)
    rows = np.arange(P)
    kone = np.zeros((XA, 2), f)
    kone[C, 0] = kone[2 * C + 1, 1] = 1
    biasone = np.concatenate([np.ones(1024, f), np.zeros(256, f)]).reshape(P, 10)
    return dict(
        c1=c1, c2=c2, c3=c3,
        sign=np.concatenate([np.ones((KF, N), f), np.tile(np.where(np.arange(N) % 2, -1, 1).astype(f), (KF, 1))]),
        kone=kone, biasone=biasone,
        cols=dict(cos=np.cos(pos).reshape(NH, P).T, sin=np.sin(pos).reshape(NH, P).T,
                  res=(rows[:, None] // 32 == np.arange(4)).astype(f),
                  mcos=(rows < C + 1).astype(f)[:, None], msin=((rows > C) & (rows < XA)).astype(f)[:, None],
                  kvm=(rows[:, None] // 32 == np.arange(4)).astype(f)))


def kernel(**inputs):
    import numpy as _np
    import concourse.bacc as _bacc
    from concourse import mybir as _mybir
    from concourse.bass_utils import run_bass_kernel_spmd as _run

    f = _np.float32
    a = {k: _np.asarray(v) for k, v in inputs.items()}
    k = constants()
    kc = k.pop("cols")

    def strips(v):
        return _np.tile(v, 4)[:, None]

    def qpad(v):
        o = _np.zeros(32, v.dtype)
        o[:v.shape[0]] = v
        return o

    def wpad(m):
        o = _np.zeros((C, 32), m.dtype)
        o[:, :m.shape[0]] = m.T
        return o

    def row(v):
        return _np.broadcast_to(v.reshape(1, -1), (P, v.size))

    cols = _np.concatenate([
        strips(qpad(a["L0_conv_bq"])), strips(qpad(a["L0_conv_bk"])), row(a["L0_conv_gamma"]),
        strips(a["L0_conv_bv"]), strips(a["L1_conv_gn_weight"]), strips(a["L1_conv_gn_bias"]),
        _np.tile(a["L1_conv_b1"], 2)[:, None], strips(a["L1_conv_b2"]),
        _np.tile(a["L2_ffn_sigma"], 8)[:, None], kc["cos"], kc["sin"],
        row(a["L2_ffn_log_weights"]), row(a["L2_ffn_gumbel"]), kc["res"], kc["mcos"], kc["msin"], kc["kvm"]], 1)
    w0 = _np.stack([blocks(wpad(a["L0_conv_wq"])), blocks(wpad(a["L0_conv_wk"])), blocks(a["L0_conv_wv"].T)], 1)
    wl2 = _np.stack([blocks(a["L2_attn_Wk"]), blocks(a["L2_attn_Wq"]), blocks(a["L2_attn_Wv"].T)], 1)
    wl2[:, 0], wl2[:, 1] = blocks(a["L2_attn_Wq"]), blocks(a["L2_attn_Wk"])
    m1, m2 = blocks(a["L1_conv_w1"].T), blocks(a["L1_conv_w2"].T)
    mstu = _np.stack([a["L2_ffn_M_phi_plus"], a["L2_ffn_M_phi_minus"]], 1)
    mstu = mstu.transpose(0, 1, 2, 4, 3).reshape(P, C * C)
    phi = _np.tile(a["L2_ffn_phi"][:N].T, (2, 1))
    mu = a["L2_ffn_M_u"].reshape(NRES, TAPS, C, 8, 4).transpose(4, 2, 0, 3, 1).reshape(P, NRES, 8 * TAPS)
    wv = _np.concatenate([a["L3_attn_wv_w"], a["L3_attn_wv_b"][:, None]], 1)
    wva = _np.concatenate([wv, wv], 1).reshape(HG, P, XA).transpose(1, 0, 2)
    dw = a["L3_attn_dense_w"].T.reshape(HG, 4, 32, C)
    dwbd = _np.zeros((4, 32, HG, 4, C), f)
    for h in range(4):
        dwbd[h, :, :, h] = dw[:, h].transpose(1, 0, 2)
    arrays = dict(
        x=a["x"].reshape(P, N), w0=w0, cols=cols, c1=k["c1"], c2=k["c2"], c3=k["c3"], wl2=wl2,
        wmlp1=m1.reshape(P, 2, P), wmlp2=m2.reshape(2, P, P).transpose(1, 0, 2), mstu=mstu, phi=phi, sign=k["sign"],
        mu=mu, bias3=_np.concatenate([a["L3_attn_wq_b"], a["L3_attn_wk_b"], a["L3_ffn_expert_b"].reshape(-1)]
                                     ).reshape(P, 10),
        biasone=k["biasone"], wq3=_np.tile(a["L3_attn_wq_w"].T, (4, 1)), wk3=_np.tile(a["L3_attn_wk_w"].T, (4, 1)),
        wva=wva, dwbd=dwbd.reshape(P, HG, P), kone=k["kone"],
        denseb=row(_np.tile(a["L3_attn_dense_b"], 4)), wrout=blocks(a["L3_ffn_router_w"]),
        routb=row(_np.tile(a["L3_ffn_router_b"], NH * B)),
        wexp=_np.tile(a["L3_ffn_expert_w"].transpose(1, 0, 2).reshape(C, NE * C), (4, 1)))

    nc = _bacc.Bacc("TRN2", target_bir_lowering=False, num_devices=1)
    feeds, args = {}, {}
    for name, v in arrays.items():
        v = _np.ascontiguousarray(v)
        feeds["in_" + name] = v
        args[name] = nc.dram_tensor("in_" + name, v.shape, _mybir.dt.from_np(v.dtype), kind="ExternalInput").ap()
    o = nc.dram_tensor("out_0", (P, N), _mybir.dt.float32, kind="ExternalOutput").ap()
    build(nc, out=o, **args)
    r = _run(nc, [feeds], core_ids=[0])
    return r.results[0]["out_0"].reshape(B, C, HW, HW)
```

```python
from contextlib import ExitStack

import numpy as np

import concourse.bass as bass
from concourse import mybir

B, C, HW = 4, 32, 16
N = HW * HW
P = 128
NH = N // P
PAD = HW + 2
KN = 9
HEADS = 16
HG = HEADS // 4
KF = 16
NRES = 4
NE = 8
XA = 2 * (C + 1)
TAPS = 3
PH = 4
NA = N // PH

F32 = mybir.dt.float32
BF16 = mybir.dt.bfloat16
F16 = mybir.dt.float16
DQ = C // 8
ALU = mybir.AluOpType
ACT = mybir.ActivationFunctionType
AX = mybir.AxisListType.X
MAGIC = 12582912.0
MASKED = -1e30
LN2 = 0.6931471805599453

(COL_BQ, COL_BK, COL_GAMMA, COL_BV, COL_GNW, COL_GNB, COL_B1, COL_B2, COL_SIGMA,
 COL_COS, COL_SIN, COL_LOGW, COL_GUMBEL, COL_RES, COL_MCOS, COL_MSIN, COL_KVM, COL_QS, COL_QL, COL_KS, COL_KL, COL_WS, COL_WL, NCOL) = (
    0, 1, 2, 3, 4, 5, 6, 7, 8, 9, 11, 13, 17, 21, 25, 26, 27, 31, 32, 33, 34, 35, 36, 37)

C1 = dict(ident=128, center=128, mean=128, bo=4)
C2 = dict(lap=NH * N, lower=KN * KN, rankoff=NE + 2, pair=128, causal=2 * 128)
C4 = dict(csd=N, csy=N, seld=HEADS, sely=2 * C)
C3 = dict(seg=NRES * NA, selr=HG * 128, ksel=32)


def places(parts):
    at, out = 0, {}
    for name, width in parts.items():
        out[name] = (at, at + width)
        at += width
    return out, at


P1, W1 = places(C1)
P2, W2 = places(C2)
P3, W3 = places(C3)
P4, W4 = places(C4)
WQ, WK, WE, WR, W3S = 0, 512, 1024, 1024 + NE * C, 1024 + NE * C + NE


def build(nc, x, w0, cols, c1, c2, c3, wqk2, wv2, wmlp1, wmlp2, mstu, phi, sign, mu, bias3, biasone,
          wva, dwbd, kone, denseb, routb, w3, c4, out):
    KC = [5, 1, 10, 4, 4, 4, 3, 3, 3, 3, 8]
    with ExitStack() as ctx:
        def sb(name, shape, dt=F32):
            return ctx.enter_context(nc.sbuf_tensor(name, shape, dt))

        sems = {}

        def s(name):
            if name not in sems:
                sems[name] = ctx.enter_context(nc.semaphore(name))
            return sems[name]

        x_cl = sb("x_cl", [P, N])
        w0_sb = sb("w0_sb", [P, 3, P])
        col = sb("col", [P, NCOL])
        c1_sb = sb("c1_sb", [P, W1])
        c2_sb = sb("c2_sb", [P, W2])
        c3_sb = sb("c3_sb", [P, W3])
        c4_sb = sb("c4_sb", [P, W4])
        wqk2_sb = sb("wqk2_sb", [C, 2, P])
        wmlp1_sb = sb("wmlp1_sb", [P, 2, P])
        wmlp2_sb = sb("wmlp2_sb", [P, 2, P])
        mstu_sb = sb("mstu_sb", [P, C * C])
        phi_sb = sb("phi_sb", [2 * KF, N])
        sign_sb = sb("sign_sb", [2 * KF, N])
        mu_sb = sb("mu_sb", [P, NRES, 8 * TAPS])
        bias3_sb = sb("bias3_sb", [P, 10])
        biasone_sb = sb("biasone_sb", [P, 10])
        wva_sb = sb("wva_sb", [P, HG, XA])
        dwbd_sb = sb("dwbd_sb", [P, HG, P])
        kone_sb = sb("kone_sb", [XA, 2])
        denseb_sb = sb("denseb_sb", [P, P])
        routb_sb = sb("routb_sb", [P, NH * B * NE])
        w3_sb = sb("w3_sb", [P, W3S])

        def part(tile, table, name):
            return tile[:, table[name][0]:table[name][1]]

        ident = part(c1_sb, P1, "ident")
        center = part(c1_sb, P1, "center")
        meanw = part(c1_sb, P1, "mean")
        bo = part(c1_sb, P1, "bo")
        lap = part(c2_sb, P2, "lap").rearrange("p (h n) -> p h n", h=NH)
        lower = part(c2_sb, P2, "lower").rearrange("p (j k) -> p j k", j=KN)
        rankoff = part(c2_sb, P2, "rankoff")
        pairw = part(c2_sb, P2, "pair")
        seg = part(c3_sb, P3, "seg").rearrange("p (i a) -> p i a", i=NRES)
        ksel = part(c3_sb, P3, "ksel")
        csd = part(c4_sb, P4, "csd")
        csy = part(c4_sb, P4, "csy")
        seld = part(c4_sb, P4, "seld")
        sely = part(c4_sb, P4, "sely")

        ident_bf = sb("ident_bf", [P, P], BF16)
        ident_hf = sb("ident_hf", [P, P], F16)
        causal_bf = sb("causal_bf", [P, 2, P], BF16)
        selr_bf = sb("selr_bf", [P, HG, P], BF16)
        ones_bf = sb("ones_bf", [P, 512], BF16)

        ones_f = sb("ones_f", [P, C])

        qhi = sb("qhi", [P, N], F16)
        q0 = sb("q0", [P, N], F16)
        khi = sb("khi", [P, N], F16)
        k0 = sb("k0", [P, N], F16)
        xg = sb("xg", [P, N])
        vtok = sb("vtok", [P, NH, B, C])
        nmax = sb("nmax", [P, NH, B])
        nmhl = sb("nmhl", [P, NH, B, 32])
        nmb = sb("nmb", [P, NH, B], BF16)
        nmt = sb("nmt", [P, N], BF16)
        pT = sb("pT", [P, B, NH, N])
        x0 = sb("x0", [P, N])
        st6 = sb("st6", [P, 6])
        st2 = sb("st2", [P, 2])
        rs = sb("rs", [P, 2])
        y3 = sb("y3", [P, 3, PAD, HW])
        sq3 = sb("sq3", [P, 3, PAD, HW])
        ptc = sb("ptc", [P, NH, P])
        prod = sb("prod", [P, 8, NH, P])
        qall = prod[:, 0, :, :].rearrange("p h n -> p (h n)")
        kall = prod[:, 1, :, :].rearrange("p h n -> p (h n)")
        gst6 = sb("gst6", [P, 6])
        gmv = sb("gmv", [P, 2])
        gme = sb("gme", [P, 2])
        gmu = sb("gmu", [P, 8])
        gy = sb("gy", [P, N])
        av = sb("av", [P, NH, B])
        absd = sb("absd", [B, N])
        dstat = sb("dstat", [B, 8])
        cnt = sb("cnt", [B, N])
        rk = sb("rk", [P, KN, NH * B])
        n2 = sb("n2", [P, KN, NH * B])
        rn = sb("rn", [P, KN, NH * B])
        nt = sb("nt", [P, KN, NH * B])
        sim = sb("sim", [P, KN, NH * B])
        dot = sb("dot", [P, KN, NH * B])
        ge = sb("ge", [P, KN, KN, NH * B])
        gd = sb("gd", [P, KN, KN, NH * B])
        rank = sb("rank", [P, KN, NH * B])
        wts = sb("wts", [P, KN, NH * B])
        wsum = sb("wsum", [P, NH * B])
        wprod = sb("wprod", [P, KN, NH, P])
        enh = sb("enh", [P, N])
        hid = sb("hid", [P, 2, N])
        xe = sb("xe", [P, N])
        x1 = sb("x1", [P, N])
        sq = sb("sq", [P, N])
        rstd = sb("rstd", [P, N])
        xln = sb("xln", [P, N])
        w2_sb = sb("w2_sb", [P, P + C])
        w2hi = sb("w2hi", [P, P + C], F16)
        w2st = sb("w2st", [P, P + C], F16)
        ghi = sb("ghi", [P, NH, B, P], F16)
        gst = sb("gst", [P, NH, B, P], F16)
        t2 = sb("t2", [P, N])
        wl = sb("wl", [P, 40])
        mixw = sb("mixw", [P, 2 * KF])
        ms = wprod[0:2 * KF, 0:4, :, :].rearrange("p k h n -> p (k h n)")
        mumix = sb("mumix", [P, 8 * TAPS])
        gtap = sb("gtap", [P, 8, N])
        fraw = sb("fraw", [P, 2, 8, N])
        big = sb("big", [P, 2 * HG * B * N])
        ftap = big[:, :].rearrange("p (t e) -> p t e", e=C)
        segm = sb("segm", [P, NA])
        xtr = sb("xtr", [P, 2, PH, C])
        u4 = sb("u4", [P, B, NA])
        ys = sb("ys", [P, 2, B, NA // 2])
        ych = sb("ych", [P, N])
        t3 = sb("t3", [P, N])
        b3f = sb("b3f", [P, 10])
        b3r = sb("b3r", [P, 10])
        b3 = sb("b3", [P, 3, 10], BF16)
        brow = sb("brow", [P, P * 10], BF16)
        xa = sb("xa", [P, NH, B, XA])
        ee = pT[:, :, :, :].rearrange("p b h n -> p b (h n)")
        qf = big[:, 0:HG * B * N].rearrange("p (g b n) -> p g b n", g=HG, b=B)
        kf = big[:, HG * B * N:].rearrange("p (b h n) -> p b h n", b=B, h=NH)
        w2h = sb("w2h", [XA, HEADS, 66])
        kxt = sb("kxt", [XA, B, 512])
        kvd = sb("kvd", [P, B, HG, 66])
        ksb = sb("ksb", [P, B * HG, 32])
        dcs = prod[:, 0:4, :, :].rearrange("p b h n -> p b (h n)")
        ycs = prod[:, 4:6, :, :].rearrange("p b h n -> p b (h n)")
        den = sb("den", [P, NH, B * HEADS])
        r3 = sb("r3", [P, NH, B, 64], BF16)
        rT = sb("rT", [P, 2, N], BF16)
        t4 = sb("t4", [P, NH, P])
        mn4 = sb("mn4", [P, NH * B])
        xc4 = sb("xc4", [P, NH * B, C])
        sq4 = sb("sq4", [P, NH * B, C])
        rs4 = sb("rs4", [P, NH * B])
        xlt = sb("xlt", [P, NH * B, C])
        xst = sb("xst", [P, NH * B, 4, C], F16)
        xs = sb("xs", [P, NH, B, P], F16)
        whi = sb("whi", [P, W3S], F16)
        wst = sb("wst", [P, W3S], F16)
        lg = sb("lg", [P, NH * B, NE])
        lm = sb("lm", [P, NH * B])
        lx = sb("lx", [P, NH * B, NE])
        ge4 = sb("ge4", [P, NH * B, NE, NE])
        gd4 = gd[:, :, :, :].rearrange("p j k g -> p (j k g)")[:, 0:NH * B * NE * NE].rearrange(
            "p (g j k) -> p g j k", j=NE, k=NE)
        rank4 = sb("rank4", [P, NH * B, NE])
        eprod = wprod[:, 0:NE]
        esum = sb("esum", [P, P])
        t5 = sb("t5", [P, P])
        x_out = sb("x_out", [P, N])

        ps = ctx.enter_context(nc.psum_tensor("ps", [P, 8, 512], F32))

        def bank(i, lo=0, hi=512):
            return ps[:, i, lo:hi]

        sc_bank = ps[:, 0:4, :].rearrange("p b (h n) -> p b h n", h=NH)
        n2_ps = bank(5, 256, 328).rearrange("p (k h b) -> p k h b", k=KN, h=NH)
        av_ps = bank(4, 256, 264).rearrange("p (h b) -> p h b", h=NH)
        pt = ps[:, 0:4, :].rearrange("p b (k n) -> p (b k) n", k=4).rearrange("p (k h) n -> p k h n", h=NH)
        nbr = [(dy, dx) for dy in (-1, 0, 1) for dx in (-1, 0, 1)]

        def shifted(tile, dy, dx, h=None):
            rows = slice(1 + dy, 1 + dy + HW) if h is None else slice(1 + dy + 8 * h, 9 + dy + 8 * h)
            return tile[:, 1 + dx, rows, :].rearrange("p r c -> p (r c)")

        loads = [
            ("in_cols", [(col, cols)]),
            ("in_a", [(x_cl, x), (w0_sb, w0)]),
            ("in_b", [(c1_sb, c1)]),
            ("in_c", [(c2_sb, c2), (mstu_sb, mstu), (c3_sb, c3)]),
            ("in_d", [(wqk2_sb, wqk2), (w2_sb[:, P:P + C], wv2), (phi_sb, phi), (sign_sb, sign), (mu_sb, mu)]),
            ("in_e", [(wmlp1_sb, wmlp1), (wmlp2_sb, wmlp2)]),
            ("in_f", [(bias3_sb, bias3), (biasone_sb, biasone), (wva_sb, wva), (dwbd_sb, dwbd), (kone_sb, kone)]),
            ("in_g", [(w3_sb, w3), (c4_sb, c4), (denseb_sb, denseb), (routb_sb, routb)]),
        ]
        landed = {name: 16 * len(group) for name, group in loads}

        order = ["ones_bf", "ones_f", "nmhl", "ge", "ge4", "ksb", "brow", "r3", "fraw", "ident_bf", "ident_hf",
                 "xa0", "xa", "causal_bf", "selr_bf"]
        filled = {name: n + 1 for n, name in enumerate(order)}

        def full(t):
            return t[tuple(slice(None) for _ in t.shape)]

        block = ctx.enter_context(nc.Block())

        @block.sync
        def _(sp):
            for name, group in loads:
                for dst, src in group:
                    sp.dma_start(full(dst), src).then_inc(s(name), 16)
            sp.wait_ge(s("b3"), 3)
            sp.wait_ge(s("filled"), filled["brow"])
            for k in range(3):
                sp.dma_start(brow[k:k + 1, :], b3[:, k, :]).then_inc(s("brow"), 16)
            sp.wait_ge(s("filled"), filled["fraw"])
            sp.wait_ge(s("gtap_mu"), 1)
            for e4 in range(4):
                if e4 >= 2:
                    sp.wait_ge(s("ftap"), e4 - 1)
                for r in range(PH):
                    sp.dma_start(fraw[32 * r:32 * r + 32, e4 % 2, :, r:N],
                                 gtap[32 * e4:32 * e4 + 32, :, 0:N - r]).then_inc(s("fraw%d" % (e4 % 2)), 16)
            sp.wait_ge(s("x_out"), NH)
            sp.dma_start(out, x_out[:, :]).then_inc(s("out"), 16)
            sp.wait_ge(s("out"), 16)

        @block.gpsimd
        def _(pool):
            g = nc.gpsimd
            g.memset(ones_bf[:, :], 1.0).then_inc(s("filled"), 1)
            g.memset(ones_f[:, :], 1.0).then_inc(s("filled"), 1)
            g.memset(nmhl[:, :, :, :], 0.0).then_inc(s("filled"), 1)
            g.memset(ge[:, :, :, :], 0.0).then_inc(s("filled"), 1)
            g.memset(ge4[:, :, :, :], 0.0).then_inc(s("filled"), 1)
            g.memset(ksb[:, :, :], 0.0).then_inc(s("filled"), 1)
            g.memset(brow[:, :], 0.0).then_inc(s("filled"), 1)
            g.memset(r3[:, :, :, :], 0.0).then_inc(s("filled"), 1)
            g.memset(fraw[:, :, :, 0:TAPS], 0.0).then_inc(s("filled"), 1)
            pool.wait_ge(s("in_b"), landed["in_b"])
            pool.wait_ge(s("in_cols"), landed["in_cols"])
            g.tensor_copy(ident_bf[:, :], ident).then_inc(s("filled"), 1)
            g.tensor_copy(ident_hf[:, :], ident).then_inc(s("filled"), 1)
            for h in range(NH):
                g.tensor_copy(xa[:, h, :, C], col[:, COL_COS + h:COL_COS + h + 1].broadcast_to([P, B]))
                g.tensor_copy(xa[:, h, :, 2 * C + 1], col[:, COL_SIN + h:COL_SIN + h + 1].broadcast_to([P, B])
                              ).then_inc(s("filled"), 1)
            pool.wait_ge(s("in_c"), landed["in_c"])
            g.tensor_copy(causal_bf[:, :, :], part(c2_sb, P2, "causal").rearrange("p (a n) -> p a n", a=2)
                          ).then_inc(s("filled"), 1)
            g.tensor_copy(selr_bf[:, :, :], part(c3_sb, P3, "selr").rearrange("p (a n) -> p a n", a=HG)
                          ).then_inc(s("filled"), 1)
            pool.wait_ge(s("in_d"), landed["in_d"])
            g.tensor_tensor(phi_sb[:, :], phi_sb[:, :], sign_sb[:, :], ALU.mult).then_inc(s("phi"), 1)
            pool.wait_ge(s("in_f"), landed["in_f"])
            g.tensor_tensor(b3f[:, :], bias3_sb[:, :], biasone_sb[:, :], ALU.add).then_inc(s("b3f"), 1)
            pool.wait_ge(s("b3f"), 1)
            g.tensor_copy(b3[:, 0, :], b3f[:, :]).then_inc(s("b3"), 1)
            pool.wait_ge(s("b3"), 1)
            g.tensor_tensor(b3r[:, :], b3f[:, :], b3[:, 0, :], ALU.subtract).then_inc(s("b3f"), 1)
            pool.wait_ge(s("b3f"), 2)
            g.tensor_copy(b3[:, 1, :], b3r[:, :]).then_inc(s("b3"), 1)
            pool.wait_ge(s("b3"), 2)
            g.tensor_tensor(b3f[:, :], b3r[:, :], b3[:, 1, :], ALU.subtract).then_inc(s("b3f"), 1)
            pool.wait_ge(s("b3f"), 3)
            g.tensor_copy(b3[:, 2, :], b3f[:, :]).then_inc(s("b3"), 1)
            pool.wait_ge(s("dstat"), 1)
            g.tensor_scalar(cnt[:, :], absd[:, :], dstat[:, 1:2], dstat[:, 4:5], ALU.subtract, ALU.mult
                            ).then_inc(s("cnt"), 1)
            pool.wait_ge(s("cnt"), 1)
            g.tensor_scalar(cnt[:, :], cnt[:, :], 7.0, MAGIC, ALU.mult, ALU.add).then_inc(s("cnt"), 1)
            for e4 in range(3):
                pool.wait_ge(s("fraw%d" % (e4 % 2)), 64 * (e4 // 2 + 1))
                g.tensor_copy(ftap[:, :, e4::4], fraw[:, e4 % 2, :, :].rearrange("p g t -> p t g")
                              ).then_inc(s("ftap"), 1)
            for h in range(NH):
                pool.wait_ge(s("xlt"), NH + h + 1)
                src = xlt[:, B * h:B * h + B, :]
                g.tensor_scalar(xa[:, h, :, 0:C], src, col[:, COL_COS + h:COL_COS + h + 1], None, ALU.mult)
                g.tensor_scalar(xa[:, h, :, C + 1:2 * C + 1], src, col[:, COL_SIN + h:COL_SIN + h + 1], None, ALU.mult
                                ).then_inc(s("xa"), 1)

        @block.scalar
        def _(act):
            a = nc.scalar
            step_count = [0]

            def step(ins):
                step_count[0] += 1
                ins.then_inc(s("act_step"), 1)
                act.wait_ge(s("act_step"), step_count[0])

            def ln_tail(nth, center_ps, var_ps):
                act.wait_ge(s("ln_center"), 2 * nth - 1)
                a.activation(sq[:, :], center_ps, ACT.Square).then_inc(s("ln_sq"), 1)
                act.wait_ge(s("ln_var"), nth)
                act.wait_ge(s("eps_ready"), 1)
                step(a.activation(rstd[:, :], var_ps, ACT.Ln, bias=wl[:, 31:32]))
                a.activation(rstd[:, :], rstd[:, :], ACT.Exp, scale=-0.5).then_inc(s("ln_rstd"), 1)

            def token_rstd(nth, centred):
                a.activation(sq4[:, :, :], centred, ACT.Square).then_inc(s("sq4"), 1)
                act.wait_ge(s("var4"), nth)
                step(a.activation(rs4[:, :], rs4[:, :], ACT.Ln, scale=1.0 / C, bias=wl[:, 31:32]))
                a.activation(rs4[:, :], rs4[:, :], ACT.Exp, scale=-0.5).then_inc(s("rs4"), 1)

            def stack_high(nth):
                for h in range(NH):
                    act.wait_ge(s("xlt"), 2 * nth - 1 + h)
                    a.activation(xst[:, B * h:B * h + B, 0::2, :],
                                 xlt[:, B * h:B * h + B, None, :].broadcast_to([P, B, 2, C]), ACT.Copy
                                 ).then_inc(s("x_high"), 1)
                act.wait_ge(s("xs_ps"), 2 * nth - 1)
                a.activation(xs[:, 0, :, :].rearrange("p b n -> p (b n)"), bank(7).bitcast(F16)[:, 0:512], ACT.Copy
                             ).then_inc(s("xs_a"), 1)

            a.preload_act_table_set("natural_log_exp_and_others")
            act.wait_ge(s("in_cols"), landed["in_cols"])
            a.activation(wl[:, 16:17], col[:, COL_SIGMA:COL_SIGMA + 1], ACT.Ln).then_inc(s("sig"), 1)
            act.wait_ge(s("sig"), 1)
            a.activation(wl[:, 17:18], wl[:, 16:17], ACT.Exp, scale=0.25).then_inc(s("sig"), 1)
            act.wait_ge(s("lmax"), 1)
            a.activation(wl[:, 4:8], wl[:, 0:4], ACT.Exp, bias=wl[:, 8:9]).then_inc(s("lexp"), 1)
            act.wait_ge(s("in_cols"), landed["in_cols"])
            act.wait_ge(s("qk0"), 2)
            a.activation(khi[:, :], bank(7, 0, N), ACT.Identity, bias=col[:, COL_BK:COL_BK + 1]).then_inc(s("khi"), 1)
            act.wait_ge(s("gbv"), 2)
            a.activation(kall[:, :], bank(7, 0, N), ACT.Identity, bias=wl[:, 32:33], scale=col[:, COL_KL:COL_KL + 1]
                         ).then_inc(s("khi"), 1)
            act.wait_ge(s("w2_ps"), 1)
            a.activation(w2_sb[:, 0:P], bank(6, 0, P), ACT.Copy, scale=float(C) ** -0.5).then_inc(s("w2"), 1)
            act.wait_ge(s("v0_ps"), 1)
            for h in range(NH):
                a.activation(vtok[:, h, :, :], bank(5, 128 * h, 128 * h + 128).rearrange("p (b c) -> p b c", b=B),
                             ACT.Copy).then_inc(s("v0"), 1)
            act.wait_ge(s("gbv"), 1)
            a.activation(xg[:, :], x_cl[:, :], ACT.Identity, bias=wl[:, 30:31]).then_inc(s("xg"), 1)
            for b in range(B):
                act.wait_ge(s("sT0"), b + 1)
                a.activation(pT[:, b, :, :], sc_bank[:, b, :, :], ACT.Exp).then_inc(s("pT0"), 1)
            act.wait_ge(s("in_d"), landed["in_d"])
            act.wait_ge(s("w2"), 1)
            a.activation(w2hi[:, :], w2_sb[:, :], ACT.Copy, scale=col[:, COL_WS:COL_WS + 1]).then_inc(s("w2"), 1)
            act.wait_ge(s("gn_stat"), 1)
            act.wait_ge(s("eps_ready"), 1)
            step(a.activation(rs[:, 0:1], st2[:, 1:2], ACT.Ln, bias=wl[:, 31:32]))
            a.activation(rs[:, 1:2], rs[:, 0:1], ACT.Exp, scale=-0.5).then_inc(s("gn_rstd"), 1)
            act.wait_ge(s("ptc_ps"), 1)
            a.activation(ptc[:, :, :].rearrange("p h n -> p (h n)"), bank(5, 0, N), ACT.Copy).then_inc(s("ptc"), 1)
            act.wait_ge(s("ms_ps"), 2)
            for k in range(2):
                a.activation(ms[:, 512 * k:512 * k + 512], ps[0:2 * KF, 7 - 4 * k, :], ACT.Copy).then_inc(s("ms"), 1)
            act.wait_ge(s("y_pad"), 6)
            a.activation(sq3[:, :, :, :], y3[:, :, :, :], ACT.Square).then_inc(s("ysq"), 1)
            act.wait_ge(s("lap_ps"), 1)
            a.activation(absd[:, :], ps[0:B, 4, 0:N], ACT.Abs).then_inc(s("absd"), 1)
            act.wait_ge(s("n2"), 1)
            step(a.activation(nt[:, :, :], n2[:, :, :], ACT.Ln, scale=float(2 ** 40)))
            a.activation(rn[:, :, :], nt[:, :, :], ACT.Exp, scale=-0.5, bias=wl[:, 29:30]).then_inc(s("rn0"), 1)
            act.wait_ge(s("gvar"), 1)
            step(a.activation(gmu[:, 3:4], gmu[:, 2:3], ACT.Ln, bias=wl[:, 31:32]))
            a.activation(gmu[:, 4:5], gmu[:, 3:4], ACT.Exp, scale=-0.5).then_inc(s("grstd"), 1)

            def taps_out(k):
                act.wait_ge(s("gtap_ps"), k + 1)
                a.activation(gtap[:, 2 * k:2 * k + 2, :].rearrange("p g t -> p (g t)"), bank(7 - k % 2), ACT.Copy
                             ).then_inc(s("gtap"), 1)

            taps_out(0)
            taps_out(1)
            act.wait_ge(s("sim"), 1)
            a.activation(wts[:, :, :], sim[:, :, :], ACT.Exp).then_inc(s("simexp"), 1)
            act.wait_ge(s("gab"), 1)
            a.activation(gy[:, :], shifted(y3, 0, 0), ACT.Identity,
                         scale=gmu[:, 5:6], bias=gmu[:, 7:8]).then_inc(s("gy"), 1)
            taps_out(2)
            taps_out(3)
            act.wait_ge(s("hid_ps"), 1)
            act.wait_ge(s("in_e"), landed["in_e"])
            a.activation(hid[:, 0, :], bank(4, 0, N), ACT.Relu, bias=col[:, COL_B1:COL_B1 + 1]).then_inc(s("hid_a"), 1)
            act.wait_ge(s("tc_ps"), 2)
            token_rstd(1, bank(6, 0, N).rearrange("p (g c) -> p g c", c=C))
            stack_high(1)
            for h in range(NH):
                act.wait_ge(s("gq_ps"), h + 1)
                a.activation(ghi[:, h, :, :].rearrange("p b n -> p (b n)"), bank(h), ACT.Copy,
                             scale=col[:, COL_WS:COL_WS + 1]).then_inc(s("ghi"), 1)
            act.wait_ge(s("v2_ps"), 1)
            for h in range(NH):
                a.activation(vtok[:, h, :, :], bank(4, 128 * h, 128 * h + 128).rearrange("p (b c) -> p b c", b=B),
                             ACT.Copy).then_inc(s("v2"), 1)
            for b in range(B):
                act.wait_ge(s("sT2"), b + 1)
                a.activation(pT[:, b, :, :].rearrange("p h n -> p (h n)")[:, 0:384], bank(b, 0, 384), ACT.Exp
                             ).then_inc(s("pT2"), 1)
            act.wait_ge(s("fraw1"), 64 * 2)
            a.activation(ftap[:, :, 3::4], fraw[:, 1, :, :].rearrange("p g t -> p t g"), ACT.Copy
                         ).then_inc(s("ftap_a"), 1)
            ln_tail(1, bank(6, 0, N), bank(6, 256, 512))
            act.wait_ge(s("u4_ps"), 2)
            a.activation(u4[:, :, :].rearrange("p b (h a) -> p h b a", h=2),
                         bank(7, 0, 256).rearrange("p (h b a) -> p h b a", h=2, b=B), ACT.Copy).then_inc(s("u4"), 1)
            act.wait_ge(s("in_g"), landed["in_g"])
            a.activation(whi[:, :], w3_sb[:, :], ACT.Copy, scale=col[:, COL_WS:COL_WS + 1]).then_inc(s("whi"), 1)

            act.wait_ge(s("tc_ps"), 6)
            token_rstd(2, bank(6, 0, N).rearrange("p (g c) -> p g c", c=C))
            stack_high(2)
            for t in range(16):
                act.wait_ge(s("qk3_ps"), t + 1)
                if t >= 4:
                    act.wait_ge(s("qk3"), t - 3)
                a.activation(ee[:, t % 4, :], bank(t % 4), ACT.Exp, bias=wl[:, 28:29]).then_inc(s("qk3_exp"), 1)
                if t in (5, 7, 9, 11):
                    b = (t - 5) // 2
                    act.wait_ge(s("kxt_ps"), b + 1)
                    a.activation(kxt[:, b, :], ps[0:XA, 4 + b % 2, :], ACT.Copy).then_inc(s("kxt"), 1)
            for b in range(B):
                act.wait_ge(s("kvd_ps"), b + 1)
                a.activation(kvd[:, b, :, :], bank(6 + b % 2, 0, HG * 66).rearrange("p (g n) -> p g n", g=HG), ACT.Copy
                             ).then_inc(s("kvd"), 1)
            for bp in range(2):
                act.wait_ge(s("rT_ps"), 2 * bp + 2)
                a.activation(rT[:, bp, :], bank(4 + bp, 0, 128).bitcast(BF16), ACT.Copy).then_inc(s("rT"), 1)
            act.wait_ge(s("xc4"), 1)
            token_rstd(3, xc4[:, :, :])
            stack_high(3)
            act.wait_ge(s("lx0"), 1)
            a.activation(lx[:, :, :], lx[:, :, :], ACT.Exp).then_inc(s("lexp4"), 1)
            for h in range(NH):
                act.wait_ge(s("fin_ps"), h + 1)
                a.activation(x_out[:, 128 * h:128 * h + 128], bank(4 + h, 0, 128), ACT.Copy).then_inc(s("x_out"), 1)

        @block.vector
        def _(dve):
            v = nc.vector
            chain_count = [0]

            def small(ins):
                chain_count[0] += 1
                ins.then_inc(s("small"), 1)
                dve.wait_ge(s("small"), chain_count[0])

            def ln_apply(nth, out_ap):
                dve.wait_ge(s("ln_center"), 2 * nth)
                dve.wait_ge(s("ln_rstd"), nth)
                v.tensor_tensor(out_ap, bank(5, 0, N), rstd[:, :], ALU.mult).then_inc(s("ln_xln"), 1)

            def normalise_stack(nth, centred):
                dve.wait_ge(s("sq4"), nth)
                v.tensor_reduce(rs4[:, :], sq4[:, :, :], AX, ALU.add).then_inc(s("var4"), 1)
                dve.wait_ge(s("rs4"), nth)
                for h in range(NH):
                    gs = slice(B * h, B * h + B)
                    v.tensor_tensor(xlt[:, gs, :], centred[:, gs, :], rs4[:, gs, None].broadcast_to([P, B, C]), ALU.mult
                                    ).then_inc(s("xlt"), 1)
                for h in range(NH):
                    gs = slice(B * h, B * h + B)
                    dve.wait_ge(s("x_high"), 2 * nth - 1 + h)
                    v.tensor_tensor(xst[:, gs, 1::2, :], xlt[:, gs, None, :].broadcast_to([P, B, 2, C]),
                                    xst[:, gs, 0::2, :], ALU.subtract).then_inc(s("x_low"), 1)

            def stack_second(nth):
                dve.wait_ge(s("xs_ps"), 2 * nth)
                v.tensor_copy(xs[:, 1, :, :].rearrange("p b n -> p (b n)"), bank(6).bitcast(F16)[:, 0:512]
                              ).then_inc(s("xs_b"), 1)

            v.memset(wl[:, 31:32], 1e-5)
            v.memset(wl[:, 29:30], 20.0 * LN2)
            v.memset(wl[:, 28:29], -1.0).then_inc(s("eps_ready"), 1)
            dve.wait_ge(s("in_cols"), landed["in_cols"])
            v.tensor_tensor(wl[:, 30:31], col[:, COL_GAMMA:COL_GAMMA + 1], col[:, COL_BV:COL_BV + 1], ALU.mult
                            ).then_inc(s("gbv"), 1)
            v.tensor_tensor(wl[:, 32:33], col[:, COL_BK:COL_BK + 1], col[:, COL_KL:COL_KL + 1], ALU.mult
                            ).then_inc(s("gbv"), 1)
            small(v.tensor_tensor(wl[:, 0:4], col[:, COL_LOGW:COL_LOGW + 4], col[:, COL_GUMBEL:COL_GUMBEL + 4], ALU.add))
            v.tensor_reduce(wl[:, 8:9], wl[:, 0:4], AX, ALU.max, negate=True).then_inc(s("lmax"), 1)
            dve.wait_ge(s("lexp"), 1)
            small(v.tensor_reduce(wl[:, 9:10], wl[:, 4:8], AX, ALU.add))
            small(v.reciprocal(wl[:, 10:11], wl[:, 9:10]))
            small(v.tensor_scalar(wl[:, 4:8], wl[:, 4:8], wl[:, 10:11], None, ALU.mult))
            dve.wait_ge(s("qk0"), 1)
            v.tensor_scalar(qhi[:, :], bank(4, 0, N), col[:, COL_BQ:COL_BQ + 1], float(C) ** -0.5, ALU.add, ALU.mult)
            small(v.tensor_scalar(qall[:, :], bank(4, 0, N), col[:, COL_BQ:COL_BQ + 1], col[:, COL_QL:COL_QL + 1],
                                  ALU.add, ALU.mult))
            v.scalar_tensor_tensor(out=q0[:, :], in0=qhi[:, :], scalar=col[:, COL_QS:COL_QS + 1], in1=qall[:, :],
                                   op0=ALU.mult, op1=ALU.add).then_inc(s("q0"), 1)
            dve.wait_ge(s("khi"), 2)
            v.scalar_tensor_tensor(out=k0[:, :], in0=khi[:, :], scalar=col[:, COL_KS:COL_KS + 1], in1=kall[:, :],
                                   op0=ALU.mult, op1=ALU.add).then_inc(s("k0"), 1)
            for b in range(B):
                dve.wait_ge(s("s0"), b + 1)
                reduced = v.tensor_reduce(nmax[:, :, b], sc_bank[:, b, :, :], AX, ALU.max, negate=True)
            small(reduced)

            def split_max(nth):
                small(v.tensor_copy(nmb[:, :, :], nmax[:, :, :]))
                if nth == 1:
                    dve.wait_ge(s("filled"), filled["nmhl"])
                v.tensor_copy(nmhl[:, :, :, 0], nmb[:, :, :])
                v.tensor_tensor(nmhl[:, :, :, 1], nmax[:, :, :], nmb[:, :, :], ALU.subtract).then_inc(s("max_nm"), 1)
                dve.wait_ge(s("max_nmT"), 2 * nth)
                v.tensor_copy(nmt[:, :], bank(4, 256, 512)).then_inc(s("max_nmt"), 1)

            split_max(1)
            small(v.tensor_reduce(wl[:, 11:12], wl[:, 4:8], AX, ALU.max))
            small(v.tensor_scalar(wl[:, 0:4], wl[:, 4:8], wl[:, 11:12], None, ALU.is_equal))
            small(v.tensor_scalar(wl[:, 12:13], wl[:, 0:1], -1.0, 1.0, ALU.mult, ALU.add))
            for i in range(1, NRES):
                small(v.tensor_tensor(wl[:, i:i + 1], wl[:, i:i + 1], wl[:, 12:13], ALU.mult))
                small(v.tensor_tensor(wl[:, 12:13], wl[:, 12:13], wl[:, i:i + 1], ALU.subtract))
            small(v.tensor_tensor(wl[:, 20:24], wl[:, 0:4], wl[:, 4:8], ALU.subtract))
            small(v.tensor_tensor(wl[:, 20:24], wl[:, 20:24], wl[:, 4:8], ALU.add))
            small(v.tensor_tensor(wl[:, 24:28], wl[:, 20:24], col[:, COL_RES:COL_RES + 4], ALU.mult))
            small(v.tensor_reduce(wl[:, 13:14], wl[:, 24:28], AX, ALU.add))
            dve.wait_ge(s("sig"), 2)
            small(v.tensor_tensor(wl[:, 14:15], wl[:, 13:14], wl[:, 17:18], ALU.mult))
            dve.wait_ge(s("in_c"), landed["in_c"])
            v.tensor_scalar(mixw[:, :], ksel, wl[:, 14:15], None, ALU.mult).then_inc(s("mixw"), 1)
            dve.wait_ge(s("in_d"), landed["in_d"])
            small(v.tensor_scalar(mumix[:, :], mu_sb[:, 0, :], wl[:, 20:21], None, ALU.mult))
            for i in range(1, NRES):
                small(v.scalar_tensor_tensor(out=mumix[:, :], in0=mu_sb[:, i, :], scalar=wl[:, 20 + i:21 + i],
                                             in1=mumix[:, :], op0=ALU.mult, op1=ALU.add))
            small(v.tensor_scalar(segm[:, :], seg[:, 0, :], wl[:, 0:1], None, ALU.mult))
            for i in range(1, NRES):
                small(v.scalar_tensor_tensor(out=segm[:, :], in0=seg[:, i, :], scalar=wl[:, i:i + 1], in1=segm[:, :],
                                             op0=ALU.mult, op1=ALU.add))
            dve.wait_ge(s("w2"), 2)
            v.scalar_tensor_tensor(out=w2st[:, :], in0=w2_sb[:, :], scalar=col[:, COL_WL:COL_WL + 1], in1=w2hi[:, :],
                                   op0=ALU.mult, op1=ALU.add).then_inc(s("w2st"), 1)
            dve.wait_ge(s("sum0"), 1)
            small(v.reciprocal(gy[:, :], bank(5, 0, N)))
            dve.wait_ge(s("o0"), 1)
            small(v.tensor_tensor(gy[:, :], bank(6, 0, N), gy[:, :], ALU.mult))
            dve.wait_ge(s("xg"), 1)
            small(v.scalar_tensor_tensor(out=x0[:, :], in0=gy[:, :], scalar=col[:, COL_GAMMA:COL_GAMMA + 1],
                                         in1=xg[:, :], op0=ALU.mult, op1=ALU.add))
            small(v.bn_stats(st6[:, :], x0[:, :]))
            v.bn_aggr(st2[:, :], st6[:, :]).then_inc(s("gn_stat"), 1)
            dve.wait_ge(s("gn_stat"), 1)
            dve.wait_ge(s("gn_rstd"), 1)
            v.tensor_scalar(shifted(y3, 0, 0), x0[:, :], st2[:, 0:1], rs[:, 1:2], ALU.subtract, ALU.mult
                            ).then_inc(s("y_pad"), 1)
            dve.wait_ge(s("y_pad"), 1)
            img = y3[:, 1, 1:1 + HW, :]
            v.tensor_copy(y3[:, 0, 1:1 + HW, 1:HW], img[:, :, 0:HW - 1]).then_inc(s("y_pad"), 1)
            v.tensor_copy(y3[:, 2, 1:1 + HW, 0:HW - 1], img[:, :, 1:HW]).then_inc(s("y_pad"), 1)
            v.tensor_copy(y3[:, 0, 1:1 + HW, 0:1], img[:, :, 1:2]).then_inc(s("y_pad"), 1)
            v.tensor_copy(y3[:, 2, 1:1 + HW, HW - 1:HW], img[:, :, HW - 2:HW - 1]).then_inc(s("y_pad"), 1)
            dve.wait_ge(s("y_pad"), 5)
            v.tensor_copy(y3[:, :, 0::PAD - 1, :], y3[:, :, 2::PAD - 5, :]).then_inc(s("y_pad"), 1)
            dve.wait_ge(s("y_pad"), 6)
            dve.wait_ge(s("av_ps"), 1)
            v.tensor_scalar(av[:, :, :], av_ps, 1.0 / C, None, ALU.mult).then_inc(s("av"), 1)
            small(v.bn_stats(gst6[:, :], shifted(y3, 0, 0)))
            small(v.bn_aggr(gmv[:, :], gst6[:, :]))
            v.tensor_copy(gme[:, 0:1], gmv[:, 0:1])
            v.scalar_tensor_tensor(out=gme[:, 1:2], in0=gmv[:, 0:1], scalar=gmv[:, 0:1], in1=gmv[:, 1:2],
                                   op0=ALU.mult, op1=ALU.add).then_inc(s("gme"), 1)
            dve.wait_ge(s("ptc"), 1)
            for j in range(4):
                dve.wait_ge(s("pt_ps"), 2 * j + 2)
                v.tensor_tensor(prod[:, 2 * j:2 * j + 2, :, :].rearrange("p k h n -> p k (h n)"),
                                pt[:, 2 * j:2 * j + 2, :, :].rearrange("p k h n -> p k (h n)"),
                                ptc[:, :, :].rearrange("p h n -> p (h n)")[:, None, :].broadcast_to([P, 2, N]), ALU.mult
                                ).then_inc(s("prod"), 1)
            prodc = prod[:, :, :, :].rearrange("p k h (b c) -> p (k h b) c", b=B)
            for j in (0, 1):
                dve.wait_ge(s("prod"), 2 * j + 2)
                v.tensor_reduce(dot[:, 5 * j:5 * j + 4, :].rearrange("p k g -> p (k g)"),
                                prodc[:, 32 * j:32 * j + 32, :], AX, ALU.add).then_inc(s("dot"), 1)
            dve.wait_ge(s("absd"), 1)
            v.tensor_reduce(dstat[:, 0:1], absd[:, :], AX, ALU.max)
            small(v.tensor_reduce(dstat[:, 1:2], absd[:, :], AX, ALU.min))
            small(v.tensor_tensor(dstat[:, 2:3], dstat[:, 0:1], dstat[:, 1:2], ALU.subtract))
            small(v.tensor_scalar(dstat[:, 3:4], dstat[:, 2:3], 1e-8, None, ALU.add))
            v.reciprocal(dstat[:, 4:5], dstat[:, 3:4]).then_inc(s("dstat"), 1)
            dve.wait_ge(s("n2_ps"), 1)
            n2p = n2_ps.rearrange("p k h b -> p k (h b)")
            v.tensor_scalar(n2[:, :, :], n2p, 1e-24, None, ALU.max).then_inc(s("n2"), 1)
            v.tensor_copy(dot[:, 4, :], n2p[:, 4, :]).then_inc(s("dot"), 1)
            dve.wait_ge(s("gpair_ps"), 1)
            small(v.tensor_copy(gmu[:, 0:2], bank(4, 272, 274)))
            small(v.tensor_tensor(gmu[:, 6:7], gmu[:, 0:1], gmu[:, 0:1], ALU.mult))
            v.tensor_tensor(gmu[:, 2:3], gmu[:, 1:2], gmu[:, 6:7], ALU.subtract).then_inc(s("gvar"), 1)
            dve.wait_ge(s("rn0"), 1)
            small(v.scalar_tensor_tensor(out=nt[:, :, :], in0=n2[:, :, :], scalar=-0.5, in1=rn[:, :, :],
                                         op0=ALU.mult, op1=ALU.mult))
            small(v.tensor_tensor(nt[:, :, :], nt[:, :, :], rn[:, :, :], ALU.mult))
            small(v.scalar_tensor_tensor(out=n2[:, :, :], in0=nt[:, :, :], scalar=1.5, in1=rn[:, :, :],
                                         op0=ALU.add, op1=ALU.mult))
            dve.wait_ge(s("dot"), 3)
            small(v.tensor_tensor(sim[:, :, :], dot[:, :, :], n2[:, :, :], ALU.mult))
            v.tensor_tensor(sim[:, :, :], sim[:, :, :], n2[:, 4:5, :].broadcast_to([P, KN, NH * B]), ALU.mult
                            ).then_inc(s("sim"), 1)
            dve.wait_ge(s("sim"), 1)
            dve.wait_ge(s("filled"), filled["ge"])
            for d in range(1, KN):
                pairs = ge[:, :, :, :].rearrange("p j k g -> p (j k) g")[:, d:(KN - d) * KN:KN + 1, :]
                compare = v.tensor_tensor(pairs, sim[:, 0:KN - d, :], sim[:, d:KN, :], ALU.is_ge)
            small(compare)
            small(v.tensor_tensor(gd[:, :, :, :], ge[:, :, :, :], ge[:, :, :, :].rearrange("p j k g -> p k j g"),
                                  ALU.subtract))
            dve.wait_ge(s("grstd"), 1)
            small(v.tensor_tensor(gmu[:, 5:6], gmu[:, 4:5], col[:, COL_GNW:COL_GNW + 1], ALU.mult))
            small(v.tensor_tensor(gmu[:, 6:7], gmu[:, 0:1], gmu[:, 5:6], ALU.mult))
            v.tensor_tensor(gmu[:, 7:8], col[:, COL_GNB:COL_GNB + 1], gmu[:, 6:7], ALU.subtract).then_inc(s("gab"), 1)
            small(v.tensor_reduce(rank[:, :, :], gd[:, :, :, :].rearrange("p j k g -> p k g j"), AX, ALU.add))
            dve.wait_ge(s("cntT_ps"), 1)
            small(v.tensor_scalar(wsum[:, :], bank(4, 256, 264), -MAGIC, None, ALU.add))
            small(v.tensor_tensor(rk[:, :, :], wsum[:, None, :].broadcast_to([P, KN, NH * B]),
                                  rankoff[:, 0:KN, None].broadcast_to([P, KN, NH * B]), ALU.add))
            small(v.tensor_tensor(rank[:, :, :], rank[:, :, :], rk[:, :, :], ALU.is_le))
            dve.wait_ge(s("simexp"), 1)
            small(v.tensor_tensor(wts[:, :, :], wts[:, :, :], rank[:, :, :], ALU.mult))
            small(v.tensor_reduce(wsum[:, :], wts[:, :, :].rearrange("p k g -> p g k"), AX, ALU.add))
            small(v.reciprocal(wsum[:, :], wsum[:, :]))
            small(v.tensor_tensor(wts[:, :, :], wts[:, :, :], wsum[:, None, :].broadcast_to([P, KN, NH * B]), ALU.mult))
            dve.wait_ge(s("gtap"), 4)
            v.tensor_tensor(gtap[:, :, 0:TAPS], gtap[:, :, 0:TAPS],
                            mumix[:, :].rearrange("p (g l) -> p g l", g=8), ALU.add).then_inc(s("gtap_mu"), 1)
            dve.wait_ge(s("gtap_ps"), 4)
            for k in range(KN):
                src = ptc if k == 4 else pt[:, k - (k > 4), :, :]
                v.tensor_tensor(wprod[:, k, :, :].rearrange("p h (b c) -> p (h b) c", b=B),
                                src[:, :, :].rearrange("p h (b c) -> p (h b) c", b=B),
                                wts[:, k, :, None].broadcast_to([P, NH * B, C]), ALU.mult).then_inc(s("wprod"), 1)
            dve.wait_ge(s("att1_ps"), 1)
            dve.wait_ge(s("gy"), 1)
            v.tensor_tensor(enh[:, :], bank(7, 0, N), gy[:, :], ALU.add).then_inc(s("enh"), 1)
            dve.wait_ge(s("enh"), 1)
            small(v.tensor_tensor(xe[:, :], enh[:, :], x0[:, :], ALU.add))
            dve.wait_ge(s("hid_ps"), 2)
            v.tensor_scalar(hid[:, 1, :], bank(0, 0, N), col[:, COL_B1:COL_B1 + 1], 0.0, ALU.add, ALU.max
                            ).then_inc(s("hid_b"), 1)
            dve.wait_ge(s("mlp_ps"), 1)
            v.scalar_tensor_tensor(out=x1[:, :], in0=bank(5, 0, N), scalar=col[:, COL_B2:COL_B2 + 1], in1=xe[:, :],
                                   op0=ALU.add, op1=ALU.add).then_inc(s("x1"), 1)
            dve.wait_ge(s("tc_ps"), 4)
            normalise_stack(1, bank(5, 0, N).rearrange("p (g c) -> p g c", c=C))
            stack_second(1)
            for h in range(NH):
                dve.wait_ge(s("ghi"), h + 1)
                v.scalar_tensor_tensor(out=gst[:, h, :, :].rearrange("p b n -> p (b n)"), in0=bank(h),
                                       scalar=col[:, COL_WL:COL_WL + 1],
                                       in1=ghi[:, h, :, :].rearrange("p b n -> p (b n)"), op0=ALU.mult, op1=ALU.add
                                       ).then_inc(s("gst"), 1)
            for b in range(B):
                dve.wait_ge(s("s2"), b + 1)
                v.tensor_reduce(nmax[:, 0, b:b + 1], bank(b, 0, 128), AX, ALU.max, negate=True)
                reduced = v.tensor_reduce(nmax[:, 1, b:b + 1], bank(b, 128, 384), AX, ALU.max, negate=True)
            small(reduced)
            split_max(2)
            dve.wait_ge(s("sum2"), 1)
            small(v.reciprocal(gy[:, :], bank(5, 0, N)))
            dve.wait_ge(s("o2"), 1)
            small(v.tensor_tensor(gy[:, :], bank(6, 0, N), gy[:, :], ALU.mult))
            v.tensor_tensor(t2[:, :], x1[:, :], gy[:, :], ALU.add).then_inc(s("t2"), 1)
            ln_apply(1, xln[:, :])
            dve.wait_ge(s("ln_xln"), 1)
            v.transpose(xtr[:, :, :, :], xln[:, :].rearrange("p (h a r) -> p h r a", h=2, r=PH)).then_inc(s("xtr"), 1)
            dve.wait_ge(s("whi"), 1)
            v.scalar_tensor_tensor(out=wst[:, :], in0=w3_sb[:, :], scalar=col[:, COL_WL:COL_WL + 1], in1=whi[:, :],
                                   op0=ALU.mult, op1=ALU.add).then_inc(s("wst"), 1)
            dve.wait_ge(s("w2h_ps"), 1)
            w2p = ps[0:XA, 1, :].rearrange("p (h e) -> p h e", h=HEADS)
            v.tensor_scalar(w2h[:, :, 0:C], w2p, col[0:XA, COL_MCOS:COL_MCOS + 1], None, ALU.mult)
            v.tensor_scalar(w2h[:, :, C:2 * C], w2p, col[0:XA, COL_MSIN:COL_MSIN + 1], None, ALU.mult)
            v.tensor_copy(w2h[:, :, 2 * C:2 * C + 2], kone_sb[:, None, :].broadcast_to([XA, HEADS, 2])).then_inc(s("w2h"), 1)
            dve.wait_ge(s("y_ps"), 1)
            v.tensor_tensor(ys[:, :, :, :], bank(0, 0, N).rearrange("p (b h a) -> p h b a", b=B, h=2),
                            segm[:, :].rearrange("p (h a) -> p h a", h=2)[:, :, None, :].broadcast_to([P, 2, B, NA // 2]),
                            ALU.mult).then_inc(s("ys"), 1)
            dve.wait_ge(s("z_ps"), 2)
            small(v.transpose(ych[:, :].rearrange("p (h r a) -> p h r a", h=2, r=PH),
                              bank(1, 0, N).rearrange("p (h r a) -> p h r a", h=2, r=PH)))
            v.tensor_tensor(t3[:, :].rearrange("p (h a r) -> p h a r", h=2, r=PH),
                            t2[:, :].rearrange("p (h a r) -> p h a r", h=2, r=PH),
                            ych[:, :].rearrange("p (h r a) -> p h a r", h=2, r=PH), ALU.add).then_inc(s("t3"), 1)
            dve.wait_ge(s("tc_ps"), 8)
            normalise_stack(2, bank(5, 0, N).rearrange("p (g c) -> p g c", c=C))
            stack_second(2)
            for t in range(16):
                dve.wait_ge(s("qk3_exp"), t + 1)
                if t < 8:
                    dst, z, e = kf[:, t // 2, t % 2, :], bank(t % 4), ee[:, t % 4, :]
                else:
                    g0 = 2 * (t % 2)
                    dst = qf[:, g0:g0 + 2, (t - 8) // 2, :]
                    z = bank(t % 4).rearrange("p (g n) -> p g n", g=2)
                    e = ee[:, t % 4, :].rearrange("p (g n) -> p g n", g=2)
                v.scalar_tensor_tensor(out=dst, in0=e, scalar=1.0, in1=z, op0=ALU.min, op1=ALU.max
                                       ).then_inc(s("qk3"), 1)
            dve.wait_ge(s("filled"), filled["ksb"])
            for bp in range(2):
                dve.wait_ge(s("kvd"), 2 * bp + 2)
                v.tensor_tensor(ksb[:, 2 * HG * bp:2 * HG * bp + 2 * HG, 0:8].rearrange("p g (k t) -> p g k t", t=2),
                                kvd[:, 2 * bp:2 * bp + 2, :, 64:66].rearrange("p b g t -> p (b g) t")[
                                    :, :, None, :].broadcast_to([P, 2 * HG, 4, 2]),
                                col[:, None, COL_KVM:COL_KVM + 4, None].broadcast_to([P, 2 * HG, 4, 2]), ALU.mult
                                ).then_inc(s("ksb"), 1)
            dve.wait_ge(s("in_g"), landed["in_g"])
            for bp in range(2):
                dve.wait_ge(s("den_ps"), bp + 1)
                v.tensor_tensor(dcs[:, 2 * bp:2 * bp + 2, :], bank(4 + bp).rearrange("p (b n) -> p b n", b=2),
                                csd[:, None, :].broadcast_to([P, 2, N]), ALU.mult).then_inc(s("dcs"), 1)
            dve.wait_ge(s("filled"), filled["r3"])
            for bp in range(2):
                dve.wait_ge(s("dent_ps"), bp + 1)
                dv = den[:, :, 2 * HEADS * bp:2 * HEADS * bp + 2 * HEADS].rearrange("p h (b k) -> p h b k", b=2)
                parts = [r3[:, :, 2 * bp:2 * bp + 2, HEADS * k:HEADS * k + HEADS] for k in range(3)]
                small(v.tensor_scalar(den[:, :, 2 * HEADS * bp:2 * HEADS * bp + 2 * HEADS],
                                      bank(7 - bp, 0, 4 * HEADS).rearrange("p (h k) -> p h k", h=NH), 1e-5, None, ALU.add))
                small(v.reciprocal(den[:, :, 2 * HEADS * bp:2 * HEADS * bp + 2 * HEADS],
                                   den[:, :, 2 * HEADS * bp:2 * HEADS * bp + 2 * HEADS]))
                small(v.tensor_copy(parts[0], dv))
                small(v.tensor_tensor(dv, dv, parts[0], ALU.subtract))
                small(v.tensor_copy(parts[1], dv))
                small(v.tensor_tensor(dv, dv, parts[1], ALU.subtract))
                v.tensor_copy(parts[2], dv).then_inc(s("r3"), 1)
            for t in range(8):
                dve.wait_ge(s("rb_ps"), t + 1)
                b, gp = t // 2, t % 2
                dst = qf[:, 2 * gp:2 * gp + 2, b, :]
                v.tensor_tensor(dst, dst, bank(t % 4).rearrange("p (g n) -> p g n", g=2), ALU.mult).then_inc(s("qs"), 1)
            for bp in range(2):
                dve.wait_ge(s("y3_ps"), bp + 1)
                v.tensor_tensor(ycs[:, bp, :], bank(6 + bp, 0, N), csy, ALU.mult).then_inc(s("ycs"), 1)
            dve.wait_ge(s("t4_ps"), 1)
            small(v.tensor_tensor(t4[:, :, :], bank(4, 0, N).rearrange("p (h n) -> p h n", h=NH),
                                  denseb_sb[:, None, :].broadcast_to([P, NH, P]), ALU.add))
            t4g = t4[:, :, :].rearrange("p h (b c) -> p (h b) c", b=B)
            small(v.tensor_reduce(mn4[:, :], t4g, AX, ALU.add))
            v.scalar_tensor_tensor(out=xc4[:, :, :], in0=mn4[:, :, None].broadcast_to([P, NH * B, C]),
                                   scalar=-1.0 / C, in1=t4g, op0=ALU.mult, op1=ALU.add).then_inc(s("xc4"), 1)
            dve.wait_ge(s("xc4"), 1)
            normalise_stack(3, xc4)
            stack_second(3)
            dve.wait_ge(s("rout_ps"), 1)
            dve.wait_ge(s("in_g"), landed["in_g"])
            small(v.tensor_tensor(lg[:, :, :].rearrange("p g e -> p (g e)"), bank(5, 0, 64), routb_sb[:, :], ALU.add))
            small(v.tensor_reduce(lm[:, :], lg[:, :, :], AX, ALU.max))
            v.tensor_tensor(lx[:, :, :], lg[:, :, :], lm[:, :, None].broadcast_to([P, NH * B, NE]), ALU.subtract
                            ).then_inc(s("lx0"), 1)
            dve.wait_ge(s("filled"), filled["ge4"])
            for d in range(1, NE):
                pairs = ge4[:, :, :, :].rearrange("p g j k -> p g (j k)")[:, :, d:(NE - d) * NE:NE + 1]
                compare = v.tensor_tensor(pairs, lg[:, :, 0:NE - d], lg[:, :, d:NE], ALU.is_ge)
            small(compare)
            small(v.tensor_tensor(gd4[:, :, :, :], ge4[:, :, :, :].rearrange("p g j k -> p g k j"), ge4[:, :, :, :],
                                  ALU.subtract))
            small(v.tensor_reduce(rank4[:, :, :], gd4[:, :, :, :], AX, ALU.add))
            small(v.tensor_tensor(rank4[:, :, :], rank4[:, :, :],
                                  rankoff[:, None, 2:2 + NE].broadcast_to([P, NH * B, NE]), ALU.is_le))
            dve.wait_ge(s("lexp4"), 1)
            small(v.tensor_tensor(lx[:, :, :], lx[:, :, :], rank4[:, :, :], ALU.mult))
            small(v.tensor_reduce(lm[:, :], lx[:, :, :], AX, ALU.add))
            small(v.reciprocal(lm[:, :], lm[:, :]))
            small(v.tensor_tensor(lx[:, :, :], lx[:, :, :], lm[:, :, None].broadcast_to([P, NH * B, NE]), ALU.mult))
            dve.wait_ge(s("exp_ps"), 1)
            for h in range(NH):
                for b in range(B):
                    src = sc_bank[:, b, h, :].rearrange("p (e c) -> p e c", e=NE)
                    v.tensor_tensor(eprod[:, :, h, C * b:C * b + C], src,
                                    lx[:, B * h + b, :, None].broadcast_to([P, NE, C]), ALU.mult).then_inc(s("eprod"), 1)
            dve.wait_ge(s("eprod"), NH * B)
            small(v.tensor_reduce(esum[:, :], eprod[:, :, 1, :].rearrange("p e n -> p n e"), AX, ALU.add))
            v.tensor_tensor(t5[:, :], esum[:, :], t4[:, 1, :], ALU.add).then_inc(s("t5"), 1)

        @block.tensor
        def _(pe):
            t = nc.tensor

            def keep_clock(n, free):
                for _ in range(n):
                    t.matmul(bank(free), ones_bf[:, 0:P], ones_bf[:, :], start=True, stop=True)

            def strip(tile, b, lo=0, hi=N, rows=32):
                return tile[32 * b:32 * b + rows, lo:hi]

            def ln_matmuls(nth, src):
                for k in (6, 5):
                    t.matmul(bank(k, 0, N), center, src, start=True, stop=True).then_inc(s("ln_center"), 1)
                pe.wait_ge(s("ln_sq"), nth)
                t.matmul(bank(6, 256, 512), meanw, sq[:, :], start=True, stop=True).then_inc(s("ln_var"), 1)

            def max_rows(nth, n):
                pe.wait_ge(s("max_nm"), nth)
                for h in range(NH):
                    t.transpose(bank(4, 256 + 128 * h, 384 + 128 * h),
                                nmhl[:, h, :, :].rearrange("p b c -> p (b c)"), ident).then_inc(s("max_nmT"), 1)
                keep_clock(n, 7)
                pe.wait_ge(s("max_nmt"), nth)

            def turn_stack(nth):
                for h in range(NH):
                    pe.wait_ge(s("x_low"), 2 * nth - 1 + h)
                    for b in range(B):
                        g = B * h + b
                        mm = t.transpose(bank(7 - h).bitcast(F16)[:, 128 * b:128 * b + 128],
                                         xst[:, g, :, :].rearrange("p k c -> p (k c)"), ident_hf[:, :])
                    mm.then_inc(s("xs_ps"), 1)
                pe.wait_ge(s("xs_a"), nth)

            def centre_tokens(src):
                for k in (6, 5):
                    for h in range(NH):
                        t.matmul(bank(k, 128 * h, 128 * h + 128), src[:, 128 * h:128 * h + 128], center,
                                 start=True, stop=True).then_inc(s("tc_ps"), 1)

            pe.wait_ge(s("filled"), filled["ones_bf"])
            keep_clock(6, 0)
            pe.wait_ge(s("in_a"), landed["in_a"])
            for k in range(2):
                t.matmul(bank(4 + 3 * k, 0, N), w0_sb[:, k, :], x_cl[:, :], start=True, stop=True
                         ).then_inc(s("qk0"), 1)
            for h in range(NH):
                mm = t.matmul(bank(5, 128 * h, 128 * h + 128), x_cl[:, 128 * h:128 * h + 128], w0_sb[:, 2, :],
                              start=True, stop=True)
            mm.then_inc(s("v0_ps"), 1)
            keep_clock(KC[6], 0)
            pe.wait_ge(s("q0"), 1)
            pe.wait_ge(s("k0"), 1)
            for b in range(B):
                for h in range(NH):
                    mm = t.matmul(sc_bank[:, b, h, :], strip(q0, b, 128 * h, 128 * h + 128, 4 * DQ), strip(k0, b, rows=4 * DQ),
                                  start=True, stop=True)
                mm.then_inc(s("s0"), 1)
            pe.wait_ge(s("in_d"), landed["in_d"])
            t.matmul(bank(6, 0, P), wqk2_sb[:, 0, :], wqk2_sb[:, 1, :], start=True, stop=True).then_inc(s("w2_ps"), 1)
            pe.wait_ge(s("in_b"), landed["in_b"])
            keep_clock(KC[5], 7)
            max_rows(1, KC[8])
            for b in range(B):
                for h in range(NH):
                    t.matmul(sc_bank[:, b, h, :], strip(k0, b, 128 * h, 128 * h + 128, 4 * DQ), strip(q0, b, rows=4 * DQ),
                             start=True, stop=False)
                    mm = t.matmul(sc_bank[:, b, h, :], strip(ones_bf, b, 0, P, 2), strip(nmt, b, rows=2), start=False, stop=True)
                mm.then_inc(s("sT0"), 1)
            pe.wait_ge(s("v0"), 2)
            pe.wait_ge(s("filled"), filled["ones_f"])
            pe.wait_ge(s("w2"), 1)

            def attend0(b, k, weights, m):
                return t.matmul(ps[32 * b:32 * b + 32, k, 0:N], weights, pT[:, b, m, :],
                                start=(m == 0), stop=(m == 1), tile_position=(0, 32 * b))

            for b in range(B):
                pe.wait_ge(s("pT0"), b + 1)
                attend0(b, 6, vtok[:, 0, b, :], 0)
            for m in range(NH):
                for b in range(B):
                    mm = attend0(b, 5, ones_f[:, :], m)
            mm.then_inc(s("sum0"), 1)
            for b in range(B):
                mm = attend0(b, 6, vtok[:, 1, b, :], 1)
            mm.then_inc(s("o0"), 1)
            pe.wait_ge(s("mixw"), 1)
            for k in range(2):
                t.matmul(ps[0:2 * KF, 7 - 4 * k, :], mixw[:, :], mstu_sb[:, 512 * k:512 * k + 512],
                         start=True, stop=True).then_inc(s("ms_ps"), 1)

            pe.wait_ge(s("y_pad"), 1)
            for h in range(NH):
                mm = t.transpose(bank(5, 128 * h, 128 * h + 128), shifted(y3, 0, 0, h), ident)
            mm.then_inc(s("ptc_ps"), 1)
            for h in range(NH):
                mm = t.matmul(av_ps[:, h, :], shifted(y3, 0, 0, h), bo, start=True, stop=True)
            mm.then_inc(s("av_ps"), 1)
            pe.wait_ge(s("y_pad"), 6)
            for k, (dy, dx) in enumerate(nbr[:4] + nbr[5:]):
                if k == 6:
                    pe.wait_ge(s("ms"), 2)
                for h in range(NH):
                    mm = t.transpose(pt[:, k, h, :], shifted(y3, dy, dx, h), ident)
                mm.then_inc(s("pt_ps"), 1)
            pe.wait_ge(s("av"), 1)
            pe.wait_ge(s("in_c"), landed["in_c"])
            for h in range(NH):
                mm = t.matmul(ps[0:B, 4, 0:N], av[:, h, :], lap[:, h, :], start=(h == 0), stop=(h == NH - 1))
            mm.then_inc(s("lap_ps"), 1)
            pe.wait_ge(s("ysq"), 1)
            pe.wait_ge(s("ptc"), 1)
            for k, (dy, dx) in enumerate(nbr):
                for h in range(NH):
                    mm = t.matmul(n2_ps[:, k, h, :], shifted(sq3, dy, dx, h), bo, start=True, stop=True)
            mm.then_inc(s("n2_ps"), 1)
            pe.wait_ge(s("gme"), 1)
            pe.wait_ge(s("absd"), 1)
            t.matmul(bank(4, 272, 274), pairw, gme[:, :], start=True, stop=True).then_inc(s("gpair_ps"), 1)

            def spectral_taps(k):
                for eg in (2 * k, 2 * k + 1):
                    mm = t.matmul(bank(7 - k % 2, 256 * (eg % 2), 256 * (eg % 2) + 256),
                                  ms[:, 128 * eg:128 * eg + 128], phi_sb[:, :], start=True, stop=True)
                mm.then_inc(s("gtap_ps"), 1)

            pe.wait_ge(s("phi"), 1)
            spectral_taps(0)
            spectral_taps(1)
            for k in (2, 3):
                pe.wait_ge(s("gtap"), k - 1)
                spectral_taps(k)
                if k == 2:
                    pe.wait_ge(s("cnt"), 2)
                    pe.wait_ge(s("gvar"), 1)
                    for h in range(NH):
                        mm = t.transpose(bank(4, 256 + B * h, 260 + B * h), cnt[:, 128 * h:128 * h + 128], ident[0:B, 0:B])
                    mm.then_inc(s("cntT_ps"), 1)
            keep_clock(KC[7], 5)
            pe.wait_ge(s("gtap"), 4)
            for k in range(KN):
                pe.wait_ge(s("wprod"), k + 1)
                for h in range(NH):
                    mm = t.matmul(bank(7, 128 * h, 128 * h + 128), wprod[:, k, h, :], ident, start=(k == 0 and h == 0),
                                  stop=(k == KN - 1), skip_group_check=True)
            mm.then_inc(s("att1_ps"), 1)
            pe.wait_ge(s("in_e"), landed["in_e"])
            pe.wait_ge(s("enh"), 1)
            for j in range(2):
                t.matmul(bank(4 - 4 * j, 0, N), wmlp1_sb[:, j, :], enh[:, :], start=True, stop=True
                         ).then_inc(s("hid_ps"), 1)
            pe.wait_ge(s("hid_a"), 1)
            t.matmul(bank(5, 0, N), wmlp2_sb[:, 0, :], hid[:, 0, :], start=True, stop=False)
            pe.wait_ge(s("hid_b"), 1)
            t.matmul(bank(5, 0, N), wmlp2_sb[:, 1, :], hid[:, 1, :], start=False, stop=True).then_inc(s("mlp_ps"), 1)

            pe.wait_ge(s("x1"), 1)
            centre_tokens(x1)
            keep_clock(KC[10], 0)
            pe.wait_ge(s("filled"), filled["ident_hf"])
            turn_stack(1)
            pe.wait_ge(s("w2st"), 1)
            for h in range(NH):
                if h == 1:
                    pe.wait_ge(s("xs_b"), 1)
                t.matmul(bank(h), w2st[:, 0:P], xs[:, h, :, :].rearrange("p b n -> p (b n)"), start=True, stop=True
                         ).then_inc(s("gq_ps"), 1)
            for h in range(NH):
                for b in range(B):
                    mm = t.matmul(bank(4, 128 * h + C * b, 128 * h + C * b + C), xs[:, h, b, :], w2st[:, P:P + C],
                                  start=True, stop=True)
            mm.then_inc(s("v2_ps"), 1)
            keep_clock(5, 7)
            pe.wait_ge(s("gst"), 2)
            pe.wait_ge(s("filled"), filled["causal_bf"])
            pe.wait_ge(s("filled"), filled["ident_bf"])
            for b in range(B):
                t.matmul(bank(b, 0, 128), gst[:, 0, b, :], xs[:, 0, b, :], start=True, stop=False)
                t.matmul(bank(b, 0, 128), ident_bf[:, :], causal_bf[:, 0, :], start=False, stop=True)
                t.matmul(bank(b, 128, 384), gst[:, 1, b, :], xs[:, :, b, :], start=True, stop=False)
                t.matmul(bank(b, 256, 384), ident_bf[:, :], causal_bf[:, 0, :], start=False, stop=True
                         ).then_inc(s("s2"), 1)
            pe.wait_ge(s("v2"), 2)
            keep_clock(KC[4], 7)
            max_rows(2, KC[9])
            for b in range(B):
                t.matmul(bank(b, 0, 256), xs[:, 0, b, :], gst[:, :, b, :], start=True, stop=False)
                t.matmul(bank(b, 0, 128), ident_bf[:, :], causal_bf[:, 1, :], start=False, stop=False)
                t.matmul(bank(b, 0, 256), strip(ones_bf, b, 0, P, 2), strip(nmt, b, rows=2), start=False, stop=True)
                t.matmul(bank(b, 256, 384), xs[:, 1, b, :], gst[:, 1, b, :], start=True, stop=False)
                t.matmul(bank(b, 256, 384), ident_bf[:, :], causal_bf[:, 1, :], start=False, stop=False)
                t.matmul(bank(b, 256, 384), strip(ones_bf, b, 0, P, 2), strip(nmt, b, 128, 256, 2), start=False, stop=True
                         ).then_inc(s("sT2"), 1)
            pe.wait_ge(s("v2"), 2)
            pe.wait_ge(s("filled"), filled["ones_f"])

            def attend(b, k, weights, m):
                lo, p0 = (0, 0) if m == 0 else (128, 256)
                return t.matmul(ps[32 * b:32 * b + 32, k, lo:N], weights,
                                pT[:, b, :, :].rearrange("p h n -> p (h n)")[:, p0:p0 + N - lo],
                                start=(m == 0), stop=(m == 1), tile_position=(0, 32 * b))

            for b in range(B):
                pe.wait_ge(s("pT2"), b + 1)
                attend(b, 6, vtok[:, 0, b, :], 0)
            for m in range(2):
                for b in range(B):
                    mm = attend(b, 5, ones_f[:, :], m)
            mm.then_inc(s("sum2"), 1)
            for b in range(B):
                mm = attend(b, 6, vtok[:, 1, b, :], 1)
            mm.then_inc(s("o2"), 1)

            pe.wait_ge(s("t2"), 1)
            ln_matmuls(1, t2[:, :])
            pe.wait_ge(s("in_f"), landed["in_f"])
            for g in range(HG):
                mm = t.matmul(ps[0:XA, 1, 128 * g:128 * g + 128], wva_sb[:, g, :], dwbd_sb[:, g, :], start=True, stop=True)
            mm.then_inc(s("w2h_ps"), 1)
            keep_clock(KC[3], 2)
            pe.wait_ge(s("xtr"), 1)
            for h in range(2):
                t.transpose(bank(7, 128 * h, 128 * h + 128), xtr[:, h, :, :].rearrange("p r d -> p (r d)"), ident
                            ).then_inc(s("u4_ps"), 1)
            pe.wait_ge(s("u4"), 1)
            pe.wait_ge(s("ftap"), 3)
            pe.wait_ge(s("ftap_a"), 1)
            yv = bank(0, 0, N).rearrange("p (b a) -> p b a", b=B)
            for j in range(NA):
                mm = t.matmul(yv[:, :, j:NA], ftap[:, PH * j:PH * j + PH, :].rearrange("p r e -> p (r e)"),
                              u4[:, :, 0:NA - j], start=(j == 0), stop=(j == NA - 1))
            mm.then_inc(s("y_ps"), 1)
            keep_clock(2, 2)
            pe.wait_ge(s("ys"), 1)
            pe.wait_ge(s("w2h"), 1)
            for h in range(2):
                t.transpose(bank(1, 128 * h, 128 * h + 128), ys[:, h, :, :].rearrange("p b a -> p (b a)"), ident).then_inc(s("z_ps"), 1)

            keep_clock(4, 2)
            pe.wait_ge(s("t3"), 1)
            centre_tokens(t3)
            keep_clock(8, 2)
            turn_stack(2)
            pe.wait_ge(s("wst"), 1)
            pe.wait_ge(s("brow"), 16 * 3)
            pe.wait_ge(s("filled"), filled["ones_bf"])

            def key_values(b):
                for h in range(NH):
                    pe.wait_ge(s("qk3"), 2 * b + h + 1)
                    if b == 0:
                        pe.wait_ge(s("xa"), h + 1)
                        pe.wait_ge(s("filled"), filled["xa"])
                    if b >= 2 and h == 0:
                        pe.wait_ge(s("kxt"), b - 1)
                    mm = t.matmul(ps[0:XA, 4 + b % 2, :], xa[:, h, b, :], kf[:, b, h, :], start=(h == 0),
                                  stop=(h == NH - 1))
                mm.then_inc(s("kxt_ps"), 1)

            for n in range(16):
                if n >= 4:
                    pe.wait_ge(s("qk3"), n - 3)
                if n < 8:
                    b, h = n // 2, n % 2
                    if n == 1:
                        pe.wait_ge(s("xs_b"), 2)
                    t.matmul(bank(n % 4), xs[:, h, b, :], wst[:, WK:WE], start=True, stop=False)
                    t.matmul(bank(n % 4), ones_bf[:, 0:P], brow[:, WK:WE], start=False, stop=True
                             ).then_inc(s("qk3_ps"), 1)
                else:
                    b, gp = (n - 8) // 2, n % 2
                    for g in (2 * gp, 2 * gp + 1):
                        o = bank(n % 4, 256 * (g % 2), 256 * (g % 2) + 256)
                        t.matmul(o, wst[:, WQ + 128 * g:WQ + 128 * g + 128], xs[:, :, b, :], start=True, stop=False)
                        mm = t.matmul(o, brow[:, WQ + 128 * g:WQ + 128 * g + 128], ones_bf[:, 0:N], start=False, stop=True)
                    mm.then_inc(s("qk3_ps"), 1)
                if n in (5, 7, 9, 11):
                    key_values((n - 5) // 2)
            pe.wait_ge(s("w2h"), 1)
            for b in range(B):
                pe.wait_ge(s("kxt"), b + 1)
                if b >= 2:
                    pe.wait_ge(s("kvd"), b - 1)
                for hd in range(HEADS):
                    q = 32 * (hd % 4)
                    mm = t.matmul(ps[q:q + 32, 6 + b % 2, 66 * (hd // 4):66 * (hd // 4) + 66],
                                  kxt[:, b, 32 * hd:32 * hd + 32], w2h[:, hd, :], start=True, stop=True,
                                  tile_position=(0, q))
                mm.then_inc(s("kvd_ps"), 1)
            pe.wait_ge(s("qk3"), 16)
            for b in range(B):
                pe.wait_ge(s("ksb"), b // 2 + 1)
                for g in range(HG):
                    mm = t.matmul(ps[32 * g:32 * g + 32, 4 + b // 2, 256 * (b % 2):256 * (b % 2) + 256],
                                  ksb[:, HG * b + g, :], qf[:, g, b, :], start=True, stop=True,
                                  tile_position=(0, 32 * g))
                if b % 2:
                    mm.then_inc(s("den_ps"), 1)
            for bp in range(2):
                pe.wait_ge(s("dcs"), bp + 1)
                for h in range(NH):
                    for b in (2 * bp, 2 * bp + 1):
                        c0 = HEADS * (2 * h + b % 2)
                        mm = t.matmul(bank(7 - bp, c0, c0 + HEADS), dcs[:, b, 128 * h:128 * h + 128], seld,
                                      start=True, stop=True)
                mm.then_inc(s("dent_ps"), 1)
            keep_clock(KC[0], 0)

            def spread(n):
                b, gp = n // 2, n % 2
                if n >= 4:
                    pe.wait_ge(s("qs"), n - 3)
                q = 64 * (b % 2)
                for g in (2 * gp, 2 * gp + 1):
                    mm = t.matmul(bank(n % 4, 256 * (g % 2), 256 * (g % 2) + 256), selr_bf[q:q + 48, g, :],
                                  rT[q:q + 48, b // 2, :], start=True, stop=True)
                mm.then_inc(s("rb_ps"), 1)

            pe.wait_ge(s("filled"), filled["selr_bf"])
            for bp in range(2):
                pe.wait_ge(s("r3"), bp + 1)
                for h in range(NH):
                    o = ps[:, 4 + bp, 64 * h:64 * h + 64].bitcast(BF16)
                    t.transpose(o, r3[:, h, 2 * bp:2 * bp + 2, :].rearrange("p b n -> p (b n)"), ident_bf[:, :]
                                ).then_inc(s("rT_ps"), 1)
                if bp == 0:
                    pe.wait_ge(s("rT"), 1)
                    for n in range(4):
                        spread(n)
            keep_clock(KC[1], 6)
            pe.wait_ge(s("rT"), 2)
            for n in range(4, 8):
                spread(n)
            for bp in range(2):
                pe.wait_ge(s("qs"), 4 * bp + 4)
                for g in range(HG):
                    for b in (2 * bp, 2 * bp + 1):
                        q = 64 * (b % 2)
                        mm = t.matmul(ps[q:q + 64, 6 + bp, 0:N], kvd[:, b, g, 0:64], qf[:, g, b, :],
                                      start=(g == 0), stop=(g == HG - 1), tile_position=(0, q))
                mm.then_inc(s("y3_ps"), 1)
                if bp == 0:
                    for h in range(NH):
                        t.matmul(bank(4, 128 * h, 128 * h + 128), t3[:, 128 * h:128 * h + 128], ident,
                                 start=(h == 0), stop=False, skip_group_check=True)
            for bp in range(2):
                pe.wait_ge(s("ycs"), bp + 1)
                for h in range(NH):
                    c0 = 128 * h + 64 * bp
                    mm = t.matmul(bank(4, c0, c0 + 64), ycs[:, bp, 128 * h:128 * h + 128], sely, start=False, stop=True,
                                  skip_group_check=True)
            mm.then_inc(s("t4_ps"), 1)

            keep_clock(KC[2], 0)
            turn_stack(3)
            for h in range(NH):
                if h == 1:
                    pe.wait_ge(s("xs_b"), 3)
                for b in range(B):
                    g = B * h + b
                    mm = t.matmul(bank(5, NE * g, NE * g + NE), xs[:, h, b, :], wst[:, WR:W3S], start=True, stop=True)
            mm.then_inc(s("rout_ps"), 1)
            for h in range(NH):
                for b in range(B):
                    t.matmul(sc_bank[:, b, h, :], xs[:, h, b, :], wst[:, WE:WR], start=True, stop=False)
                    mm = t.matmul(sc_bank[:, b, h, :], ones_bf[:, 0:P], brow[:, WE:WR], start=False, stop=True)
            mm.then_inc(s("exp_ps"), 1)
            t.matmul(bank(4, 0, 128), t4[:, 0, :], ident, start=True, stop=False)
            keep_clock(8, 7)
            pe.wait_ge(s("eprod"), B)
            for e in range(NE):
                mm = t.matmul(bank(4, 0, 128), eprod[:, e, 0, :], ident, start=False, stop=(e == NE - 1))
            mm.then_inc(s("fin_ps"), 1)
            pe.wait_ge(s("t5"), 1)
            t.transpose(bank(5, 0, 128), t5[:, :], ident).then_inc(s("fin_ps"), 1)


def blocks(m):
    m = np.asarray(m)
    r, c = m.shape
    o = np.zeros((4 * r, 4 * c), m.dtype)
    for b in range(4):
        o[b * r:(b + 1) * r, b * c:(b + 1) * c] = m
    return o


def constants():
    f = np.float32
    eye = np.eye(P, dtype=f)
    ones = np.kron(np.eye(4, dtype=f), np.ones((32, 32), f))
    c1 = np.concatenate([eye, eye - ones / f(C), ones / f(C), np.kron(np.eye(4, dtype=f), np.ones((32, 1), f))], 1)
    lap = np.zeros((N, N), f)
    for r in range(HW):
        for c in range(HW):
            lap[r * HW + c, r * HW + c] = 4
            for dr, dc in ((0, 1), (0, -1), (1, 0), (-1, 0)):
                if 0 <= r + dr < HW and 0 <= c + dc < HW:
                    lap[(r + dr) * HW + c + dc, r * HW + c] = -1
    lower = (np.arange(KN)[:, None] < np.arange(KN)[None, :]).astype(f)
    rankoff = np.arange(NE + 2, dtype=f) - 8
    pair = np.kron(np.eye(64, dtype=f), np.full((2, 2), 0.5, f))
    i = np.arange(P)
    c2 = np.concatenate([
        lap.reshape(NH, P, N).transpose(1, 0, 2).reshape(P, -1),
        np.broadcast_to(lower.reshape(1, -1), (P, KN * KN)),
        np.broadcast_to(rankoff, (P, NE + 2)), pair,
        np.where(i[None, :] > i[:, None], MASKED, 0).astype(f),
        np.where(i[:, None] > i[None, :], MASKED, 0).astype(f)], 1)
    seg = np.stack([(np.arange(NA) < NA >> k) for k in range(NRES)]).astype(f)
    selr = np.zeros((2, 64, HG, 4, 32), f)
    for k in range(3):
        for hd in range(HEADS):
            selr[:, 16 * k + hd, hd // 4, hd % 4, :] = 1
    ksel = np.tile(np.eye(2 * KF, dtype=f), (NRES, 1))
    c3 = np.concatenate([np.broadcast_to(seg.reshape(1, -1), (P, NRES * NA)), selr.reshape(P, -1), ksel], 1)
    pos = f(1.57) * np.arange(N, dtype=f) / f(N)
    rows = np.arange(P)
    trig = np.stack([np.cos(pos), np.sin(pos)]).astype(f)
    strip = rows % 32
    csd = np.where((strip < 8)[:, None], trig[rows % 2], 0)
    csy = trig[rows // 32 % 2]
    seld = ((strip < 8)[:, None] & (rows[:, None] // 32 * 4 + strip[:, None] // 2 == np.arange(HEADS))).astype(f)
    sely = (rows[:, None] // 64 * C + strip[:, None] == np.arange(2 * C)).astype(f)
    c4 = np.concatenate([csd, csy, seld, sely], 1).astype(f)
    kone = np.zeros((XA, 2), f)
    kone[C, 0] = kone[2 * C + 1, 1] = 1
    biasone = np.concatenate([np.ones(1024, f), np.zeros(256, f)]).reshape(P, 10)
    return dict(
        c1=c1, c2=c2, c3=c3, c4=c4,
        sign=np.concatenate([np.ones((KF, N), f), np.tile(np.where(np.arange(N) % 2, -1, 1).astype(f), (KF, 1))]),
        kone=kone, biasone=biasone,
        cols=dict(cos=np.cos(pos).reshape(NH, P).T, sin=np.sin(pos).reshape(NH, P).T,
                  res=(rows[:, None] // 32 == np.arange(4)).astype(f),
                  mcos=(rows < C + 1).astype(f)[:, None], msin=((rows > C) & (rows < XA)).astype(f)[:, None],
                  kvm=(rows[:, None] // 32 == np.arange(4)).astype(f),
                  split=np.stack([
                      np.where(rows % 16 < 8, 1, -1), np.where(rows % 16 < 8, 0, C ** -0.5),
                      np.where(rows % 8 < 4, 1, -1), np.where(rows % 8 < 4, 0, 1),
                      np.where(rows < 64, 1, -1), np.where(rows < 64, 0, 1)], 1).astype(f)))


def kernel(**inputs):
    import numpy as _np
    import concourse.bacc as _bacc
    from concourse import mybir as _mybir
    from concourse.bass_utils import run_bass_kernel_spmd as _run

    f = _np.float32
    a = {k: _np.asarray(v) for k, v in inputs.items()}
    k = constants()
    kc = k.pop("cols")

    def strips(v):
        return _np.tile(v, 4)[:, None]

    def qpad(v):
        return _np.concatenate([_np.tile(v, 4), _np.zeros(32 - 4 * v.shape[0], v.dtype)])

    def wpad(m):
        return _np.concatenate([_np.tile(m.T, (1, 4)), _np.zeros((C, 32 - 4 * m.shape[0]), m.dtype)], 1)

    def row(v):
        return _np.broadcast_to(v.reshape(1, -1), (P, v.size))

    cols = _np.concatenate([
        strips(qpad(a["L0_conv_bq"])), strips(qpad(a["L0_conv_bk"])), row(a["L0_conv_gamma"]),
        strips(a["L0_conv_bv"]), strips(a["L1_conv_gn_weight"]), strips(a["L1_conv_gn_bias"]),
        _np.tile(a["L1_conv_b1"], 2)[:, None], strips(a["L1_conv_b2"]),
        _np.tile(a["L2_ffn_sigma"], 8)[:, None], kc["cos"], kc["sin"],
        row(a["L2_ffn_log_weights"]), row(a["L2_ffn_gumbel"]), kc["res"], kc["mcos"], kc["msin"], kc["kvm"], kc["split"]], 1)
    w0 = _np.stack([blocks(wpad(a["L0_conv_wq"])), blocks(wpad(a["L0_conv_wk"])), blocks(a["L0_conv_wv"].T)], 1)
    wqk2 = _np.stack([_np.tile(a["L2_attn_Wq"], (1, 4)), _np.tile(a["L2_attn_Wk"], (1, 4))], 1)
    m1, m2 = blocks(a["L1_conv_w1"].T), blocks(a["L1_conv_w2"].T)
    mstu = _np.stack([a["L2_ffn_M_phi_plus"], a["L2_ffn_M_phi_minus"]], 1)
    mstu = mstu.transpose(0, 1, 2, 4, 3).reshape(P, C * C)
    phi = _np.tile(a["L2_ffn_phi"][:N].T, (2, 1))
    mu = a["L2_ffn_M_u"].reshape(NRES, TAPS, C, 8, 4).transpose(4, 2, 0, 3, 1).reshape(P, NRES, 8 * TAPS)
    wv = _np.concatenate([a["L3_attn_wv_w"], a["L3_attn_wv_b"][:, None]], 1)
    wva = _np.concatenate([wv, wv], 1).reshape(HG, P, XA).transpose(1, 0, 2)
    dw = a["L3_attn_dense_w"].T.reshape(HG, 4, 32, C)
    dwbd = _np.zeros((4, 32, HG, 4, C), f)
    for h in range(4):
        dwbd[h, :, :, h] = dw[:, h].transpose(1, 0, 2)
    arrays = dict(
        x=a["x"].reshape(P, N), w0=w0, cols=cols, c1=k["c1"], c2=k["c2"], c3=k["c3"], c4=k["c4"], wqk2=wqk2,
        wv2=_np.tile(a["L2_attn_Wv"].T, (4, 1)),
        wmlp1=m1.reshape(P, 2, P), wmlp2=m2.reshape(2, P, P).transpose(1, 0, 2), mstu=mstu, phi=phi, sign=k["sign"],
        mu=mu, bias3=_np.concatenate([a["L3_attn_wq_b"], a["L3_attn_wk_b"], a["L3_ffn_expert_b"].reshape(-1)]
                                     ).reshape(P, 10),
        biasone=k["biasone"], wva=wva, dwbd=dwbd.reshape(P, HG, P), kone=k["kone"],
        denseb=row(_np.tile(a["L3_attn_dense_b"], 4)), routb=row(_np.tile(a["L3_ffn_router_b"], NH * B)),
        w3=_np.tile(_np.concatenate([
            a["L3_attn_wq_w"].T, a["L3_attn_wk_w"].T,
            a["L3_ffn_expert_w"].transpose(1, 0, 2).reshape(C, NE * C), a["L3_ffn_router_w"]], 1), (4, 1)))

    nc = _bacc.Bacc("TRN2", target_bir_lowering=False, num_devices=1)
    feeds, args = {}, {}
    for name, v in arrays.items():
        v = _np.ascontiguousarray(v)
        feeds["in_" + name] = v
        args[name] = nc.dram_tensor("in_" + name, v.shape, _mybir.dt.from_np(v.dtype), kind="ExternalInput").ap()
    o = nc.dram_tensor("out_0", (P, N), _mybir.dt.float32, kind="ExternalOutput").ap()
    build(nc, out=o, **args)
    r = _run(nc, [feeds], core_ids=[0])
    return r.results[0]["out_0"].reshape(B, C, HW, HW)
```

```python
from contextlib import ExitStack

import numpy as np

import concourse.bass as bass
from concourse import mybir

B, C, HW = 4, 32, 16
N = HW * HW
P = 128
NH = N // P
PAD = HW + 2
KN = 9
HEADS = 16
HG = HEADS // 4
KF = 16
NRES = 4
NE = 8
NE_SUM = 5
XA = 2 * (C + 1)
TAPS = 3
PH = 4
NA = N // PH

F32 = mybir.dt.float32
BF16 = mybir.dt.bfloat16
F16 = mybir.dt.float16
DQ = C // 8
ALU = mybir.AluOpType
ACT = mybir.ActivationFunctionType
AX = mybir.AxisListType.X
MAGIC = 12582912.0
MASKED = -1e30
TAP_SCALE = 1024.0
LN2 = 0.6931471805599453

(COL_BQ, COL_BK, COL_GAMMA, COL_BV, COL_GNW, COL_GNB, COL_B1, COL_B2, COL_SIGMA,
 COL_COS, COL_SIN, COL_LOGW, COL_GUMBEL, COL_RES, COL_MCOS, COL_MSIN, COL_KVM, COL_QS, COL_QL, COL_KS, COL_KL,
 COL_WS, COL_WL, COL_ONE, NCOL) = (
    0, 1, 2, 3, 4, 5, 6, 7, 8, 9, 11, 13, 17, 21, 25, 26, 27, 31, 32, 33, 34, 35, 36, 37, 38)

C1 = dict(ident=128, center=128, mean=128, bo=4)
C2 = dict(lap=NH * N, lower=KN * KN, rankoff=NE + 2, pair=128, causal=2 * 128)
C4 = dict(csd=N, csy=N, seld=HEADS, sely=2 * C)
C3 = dict(seg=NRES * NA, selr=HG * 128, ksel=32)


def places(parts):
    at, out = 0, {}
    for name, width in parts.items():
        out[name] = (at, at + width)
        at += width
    return out, at


P1, W1 = places(C1)
P2, W2 = places(C2)
P3, W3 = places(C3)
P4, W4 = places(C4)
WQ, WK, WE, WR, W3S = 0, 512, 1024, 1024 + NE * C, 1024 + NE * C + NE


def build(nc, x, w0, cols, c1, c2, c3, wqk2, wv2, wmlp1, wmlp2, mstu, phi, sign, mu,
          wva, dwbd, kone, denseb, w3, c4, out):
    with ExitStack() as ctx:
        def sb(name, shape, dt=F32):
            return ctx.enter_context(nc.sbuf_tensor(name, shape, dt))

        sems = {}

        def s(name):
            if name not in sems:
                sems[name] = ctx.enter_context(nc.semaphore(name))
            return sems[name]

        x_cl = sb("x_cl", [P, N])
        w0_sb = sb("w0_sb", [P, 3, P])
        col = sb("col", [P, NCOL])
        c1_sb = sb("c1_sb", [P, W1])
        c2_sb = sb("c2_sb", [P, W2])
        c3_sb = sb("c3_sb", [P, W3])
        c4_sb = sb("c4_sb", [P, W4])
        wqk2_sb = sb("wqk2_sb", [C, 2, P])
        wmlp1_sb = sb("wmlp1_sb", [P, 2, P])
        wmlp2_sb = sb("wmlp2_sb", [P, 2, P])
        mstu_sb = sb("mstu_sb", [P, C * C])
        phi_sb = sb("phi_sb", [2 * KF, N])
        sign_sb = sb("sign_sb", [2 * KF, N])
        mu_sb = sb("mu_sb", [P, NRES, 8 * TAPS])
        wva_sb = sb("wva_sb", [P, HG, XA])
        dwbd_sb = sb("dwbd_sb", [P, HG, P])
        kone_sb = sb("kone_sb", [XA, 2])
        denseb_sb = sb("denseb_sb", [P, P])
        w3_sb = sb("w3_sb", [P, W3S])

        def part(tile, table, name):
            return tile[:, table[name][0]:table[name][1]]

        ident = part(c1_sb, P1, "ident")
        center = part(c1_sb, P1, "center")
        meanw = part(c1_sb, P1, "mean")
        bo = part(c1_sb, P1, "bo")
        lap = part(c2_sb, P2, "lap").rearrange("p (h n) -> p h n", h=NH)
        lower = part(c2_sb, P2, "lower").rearrange("p (j k) -> p j k", j=KN)
        rankoff = part(c2_sb, P2, "rankoff")
        pairw = part(c2_sb, P2, "pair")
        seg = part(c3_sb, P3, "seg").rearrange("p (i a) -> p i a", i=NRES)
        ksel = part(c3_sb, P3, "ksel")
        csd = part(c4_sb, P4, "csd")
        csy = part(c4_sb, P4, "csy")
        seld = part(c4_sb, P4, "seld")
        sely = part(c4_sb, P4, "sely")

        ident_bf = sb("ident_bf", [P, P], BF16)
        ident_hf = sb("ident_hf", [P, P], F16)
        causal_bf = sb("causal_bf", [P, 2, P], BF16)
        selr_bf = sb("selr_bf", [P, HG, P], BF16)
        ones_bf = sb("ones_bf", [P, 512], BF16)

        ones_f = sb("ones_f", [P, C])

        qhi = sb("qhi", [P, N], F16)
        q0 = sb("q0", [P, N], F16)
        khi = sb("khi", [P, N], F16)
        k0 = sb("k0", [P, N], F16)
        xg = sb("xg", [P, N])
        vtok = sb("vtok", [P, NH, B, C])
        nmax = sb("nmax", [P, NH, B])
        nmhl = sb("nmhl", [P, NH, B, 32])
        nmb = sb("nmb", [P, NH, B], BF16)
        nmt = sb("nmt", [P, N], BF16)
        pT = sb("pT", [P, B, NH, N])
        x0 = sb("x0", [P, N])
        st6 = sb("st6", [P, 6])
        st2 = sb("st2", [P, 2])
        rs = sb("rs", [P, 2])
        y3 = sb("y3", [P, 3, PAD, HW])
        sq3 = sb("sq3", [P, 3, PAD, HW])
        ptc = sb("ptc", [P, NH, P])
        prod = sb("prod", [P, 8, NH, P])
        qall = prod[:, 0, :, :].rearrange("p h n -> p (h n)")
        kall = prod[:, 1, :, :].rearrange("p h n -> p (h n)")
        gst6 = sb("gst6", [P, 6])
        gmv = sb("gmv", [P, 2])
        gme = sb("gme", [P, 2])
        gmu = sb("gmu", [P, 8])
        gy = sb("gy", [P, N])
        av = sb("av", [P, NH, B])
        absd = sb("absd", [B, N])
        dstat = sb("dstat", [B, 8])
        cnt = sb("cnt", [B, N])
        rk = sb("rk", [P, KN, NH * B])
        n2 = sb("n2", [P, KN, NH * B])
        rn = sb("rn", [P, KN, NH * B])
        nt = sb("nt", [P, KN, NH * B])
        sim = sb("sim", [P, KN, NH * B])
        dot = sb("dot", [P, KN, NH * B])
        ge = sb("ge", [P, KN, KN, NH * B])
        gd = sb("gd", [P, KN, KN, NH * B])
        rank = sb("rank", [P, KN, NH * B])
        wts = sb("wts", [P, KN, NH * B])
        wsum = sb("wsum", [P, NH * B])
        wprod = sb("wprod", [P, KN, NH, P])
        enh = sb("enh", [P, N])
        hid = sb("hid", [P, 2, N])
        xe = sb("xe", [P, N])
        x1 = sb("x1", [P, N])
        sq = sb("sq", [P, N])
        rstd = sb("rstd", [P, N])
        xln = sb("xln", [P, N])
        w2_sb = sb("w2_sb", [P, P + C])
        w2hi = sb("w2hi", [P, P + C], F16)
        w2st = sb("w2st", [P, P + C], F16)
        ghi = sb("ghi", [P, NH, B, P], F16)
        gst = sb("gst", [P, NH, B, P], F16)
        t2 = sb("t2", [P, N])
        wl = sb("wl", [P, 40])
        mixw = sb("mixw", [P, 2 * KF])
        ms = wprod[0:2 * KF, 0:4, :, :].rearrange("p k h n -> p (k h n)")
        mumix = sb("mumix", [P, 8 * TAPS])
        gtap = sb("gtap", [P, 8, N])
        fraw = sb("fraw", [P, 2, 8, N])
        big = sb("big", [P, 2 * HG * B * N])
        ftap = big[:, :].bitcast(F16).rearrange("p (k t e) -> p k t e", k=2, e=C)
        segm = sb("segm", [P, NA])
        xtr = sb("xtr", [P, 2, PH, C])
        u4 = sb("u4", [P, 2, B, NA], F16)
        ys = sb("ys", [P, 2, B, NA // 2])
        ych = sb("ych", [P, N])
        t3 = sb("t3", [P, N])
        xa = sb("xa", [P, NH, B, XA])
        ee = pT[:, :, :, :].rearrange("p b h n -> p b (h n)")
        qf = big[:, 0:HG * B * N].rearrange("p (g b n) -> p g b n", g=HG, b=B)
        kf = big[:, HG * B * N:].rearrange("p (b h n) -> p b h n", b=B, h=NH)
        w2h = sb("w2h", [XA, HEADS, 66])
        kxt = sb("kxt", [XA, B, 512])
        kvd = sb("kvd", [P, B, HG, 66])
        ksb = sb("ksb", [P, B * HG, 32])
        dcs = prod[:, 0:4, :, :].rearrange("p b h n -> p b (h n)")
        ycs = prod[:, 4:6, :, :].rearrange("p b h n -> p b (h n)")
        den = sb("den", [P, NH, B * HEADS])
        r3 = sb("r3", [P, NH, B, 64], BF16)
        rT = sb("rT", [P, 2, N], BF16)
        t4 = sb("t4", [P, NH, P])
        mn4 = sb("mn4", [P, NH * B])
        xc4 = sb("xc4", [P, NH * B, C])
        sq4 = sb("sq4", [P, NH * B, C])
        rs4 = sb("rs4", [P, NH * B])
        xlt = sb("xlt", [P, NH * B, C])
        xst = sb("xst", [P, NH * B, 4, C], F16)
        xs = sb("xs", [P, NH, B, P], F16)
        whi = sb("whi", [P, W3S], F16)
        wst = sb("wst", [P, W3S], F16)
        lg = sb("lg", [P, NH * B, NE])
        lm = sb("lm", [P, NH * B])
        lx = sb("lx", [P, NH * B, NE])
        ge4 = sb("ge4", [P, NH * B, NE, NE])
        gd4 = gd[:, :, :, :].rearrange("p j k g -> p (j k g)")[:, 0:NH * B * NE * NE].rearrange(
            "p (g j k) -> p g j k", j=NE, k=NE)
        rank4 = sb("rank4", [P, NH * B, NE])
        eprod = wprod[:, 0:NE]
        esum = sb("esum", [P, P])
        x_out = sb("x_out", [P, N])

        ps = ctx.enter_context(nc.psum_tensor("ps", [P, 8, 512], F32))

        def bank(i, lo=0, hi=512):
            return ps[:, i, lo:hi]

        sc_bank = ps[:, 0:4, :].rearrange("p b (h n) -> p b h n", h=NH)
        n2_ps = bank(5, 256, 328).rearrange("p (k h b) -> p k h b", k=KN, h=NH)
        av_ps = bank(4, 256, 264).rearrange("p (h b) -> p h b", h=NH)
        pt = ps[:, 0:4, :].rearrange("p b (k n) -> p (b k) n", k=4).rearrange("p (k h) n -> p k h n", h=NH)
        nbr = [(dy, dx) for dy in (-1, 0, 1) for dx in (-1, 0, 1)]

        def shifted(tile, dy, dx, h=None):
            rows = slice(1 + dy, 1 + dy + HW) if h is None else slice(1 + dy + 8 * h, 9 + dy + 8 * h)
            return tile[:, 1 + dx, rows, :].rearrange("p r c -> p (r c)")

        loads = [
            ("in_cols", [(col, cols)]),
            ("in_a", [(x_cl, x), (w0_sb, w0)]),
            ("in_b", [(c1_sb, c1)]),
            ("in_c", [(c2_sb, c2), (mstu_sb, mstu), (c3_sb, c3)]),
            ("in_d", [(wqk2_sb, wqk2), (w2_sb[:, P:P + C], wv2), (phi_sb, phi), (sign_sb, sign), (mu_sb, mu)]),
            ("in_e", [(wmlp1_sb, wmlp1), (wmlp2_sb, wmlp2)]),
            ("in_f", [(wva_sb, wva), (dwbd_sb, dwbd), (kone_sb, kone)]),
            ("in_g", [(w3_sb, w3), (c4_sb, c4), (denseb_sb, denseb)]),
        ]
        landed = {name: 16 * len(group) for name, group in loads}

        order = ["ones_bf", "ones_f", "nmhl", "ge", "ge4", "ksb", "xst0", "xst", "r3", "fraw", "ident_bf", "ident_hf",
                 "xa0", "xa", "causal_bf", "selr_bf"]
        filled = {name: n + 1 for n, name in enumerate(order)}

        def quarter(c):
            dst = fraw[:, c % 3, :, :] if c % 3 < 2 else prod[:, :, :, :].rearrange("p g h n -> p g (h n)")
            return dst, dst.rearrange("p g t -> p t g")

        def taps_high(engine_copy, c):
            return engine_copy(ftap[:, 0, :, c::4], quarter(c)[1])

        def taps_low(subtract, c):
            return subtract(ftap[:, 1, :, c::4], quarter(c)[1], ftap[:, 0, :, c::4], ALU.subtract)

        def full(t):
            return t[tuple(slice(None) for _ in t.shape)]

        block = ctx.enter_context(nc.Block())

        @block.sync
        def _(sp):
            for name, group in loads:
                for dst, src in group:
                    sp.dma_start(full(dst), src).then_inc(s(name), 16)
            sp.wait_ge(s("filled"), filled["fraw"])
            sp.wait_ge(s("gtap_mu"), 1)
            for c in range(4):
                if c == 2:
                    sp.wait_ge(s("dot"), 4)
                if c == 3:
                    sp.wait_ge(s("taps_pool"), 1)
                for r in range(PH):
                    sp.dma_start(quarter(c)[0][32 * r:32 * r + 32, :, r:N],
                                 gtap[32 * c:32 * c + 32, :, 0:N - r]).then_inc(s("quarter%d" % (c % 3)), 16)
            sp.wait_ge(s("x_out"), NH)
            sp.dma_start(out, x_out[:, :]).then_inc(s("out"), 16)
            sp.wait_ge(s("out"), 16)

        @block.gpsimd
        def _(pool):
            g = nc.gpsimd
            g.memset(ones_bf[:, :], 1.0).then_inc(s("filled"), 1)
            g.memset(ones_f[:, :], 1.0).then_inc(s("filled"), 1)
            g.memset(nmhl[:, :, :, :], 0.0).then_inc(s("filled"), 1)
            g.memset(ge[:, :, :, :], 0.0).then_inc(s("filled"), 1)
            g.memset(ge4[:, :, :, :], 0.0).then_inc(s("filled"), 1)
            g.memset(ksb[:, :, :], 0.0).then_inc(s("filled"), 1)
            g.memset(xst[:, :, 3, 2:C], 0.0).then_inc(s("filled"), 1)
            g.memset(xst[:, :, 3, 0:2], 1.0).then_inc(s("filled"), 1)
            g.memset(r3[:, :, :, :], 0.0).then_inc(s("filled"), 1)
            g.memset(fraw[:, :, :, 0:TAPS], 0.0).then_inc(s("filled"), 1)
            pool.wait_ge(s("in_b"), landed["in_b"])
            pool.wait_ge(s("in_cols"), landed["in_cols"])
            g.tensor_copy(ident_bf[:, :], ident).then_inc(s("filled"), 1)
            g.tensor_copy(ident_hf[:, :], ident).then_inc(s("filled"), 1)
            for h in range(NH):
                g.tensor_copy(xa[:, h, :, C], col[:, COL_COS + h:COL_COS + h + 1].broadcast_to([P, B]))
                g.tensor_copy(xa[:, h, :, 2 * C + 1], col[:, COL_SIN + h:COL_SIN + h + 1].broadcast_to([P, B])
                              ).then_inc(s("filled"), 1)
            pool.wait_ge(s("in_c"), landed["in_c"])
            g.tensor_copy(causal_bf[:, :, :], part(c2_sb, P2, "causal").rearrange("p (a n) -> p a n", a=2)
                          ).then_inc(s("filled"), 1)
            g.tensor_copy(selr_bf[:, :, :], part(c3_sb, P3, "selr").rearrange("p (a n) -> p a n", a=HG)
                          ).then_inc(s("filled"), 1)
            pool.wait_ge(s("in_d"), landed["in_d"])
            g.tensor_tensor(phi_sb[:, :], phi_sb[:, :], sign_sb[:, :], ALU.mult).then_inc(s("phi"), 1)
            pool.wait_ge(s("in_g"), landed["in_g"])
            g.tensor_scalar(w3_sb[:, WQ:WE], w3_sb[:, WQ:WE], col[:, COL_ONE:COL_ONE + 1], None, ALU.add
                            ).then_inc(s("w3"), 1)
            pool.wait_ge(s("dstat"), 1)
            g.tensor_scalar(cnt[:, :], absd[:, :], dstat[:, 1:2], dstat[:, 4:5], ALU.subtract, ALU.mult
                            ).then_inc(s("cnt"), 1)
            pool.wait_ge(s("cnt"), 1)
            g.tensor_scalar(cnt[:, :], cnt[:, :], 7.0, MAGIC, ALU.mult, ALU.add).then_inc(s("cnt"), 1)
            pool.wait_ge(s("taps_act"), 1)
            taps_low(g.tensor_tensor, 0).then_inc(s("taps_pool"), 1)
            pool.wait_ge(s("taps_act"), 4)
            taps_low(g.tensor_tensor, 3).then_inc(s("taps_pool"), 1)
            for h in range(NH):
                pool.wait_ge(s("xlt"), NH + h + 1)
                src = xlt[:, B * h:B * h + B, :]
                g.tensor_scalar(xa[:, h, :, 0:C], src, col[:, COL_COS + h:COL_COS + h + 1], None, ALU.mult)
                g.tensor_scalar(xa[:, h, :, C + 1:2 * C + 1], src, col[:, COL_SIN + h:COL_SIN + h + 1], None, ALU.mult
                                ).then_inc(s("xa"), 1)

        @block.scalar
        def _(act):
            a = nc.scalar
            step_count = [0]

            def step(ins):
                step_count[0] += 1
                ins.then_inc(s("act_step"), 1)
                act.wait_ge(s("act_step"), step_count[0])

            def ln_tail(nth, center_ps, var_ps):
                act.wait_ge(s("ln_center"), 2 * nth - 1)
                a.activation(sq[:, :], center_ps, ACT.Square).then_inc(s("ln_sq"), 1)
                act.wait_ge(s("ln_var"), nth)
                act.wait_ge(s("eps_ready"), 1)
                step(a.activation(rstd[:, :], var_ps, ACT.Ln, bias=wl[:, 31:32]))
                a.activation(rstd[:, :], rstd[:, :], ACT.Exp, scale=-0.5).then_inc(s("ln_rstd"), 1)

            def token_rstd(nth, centred):
                a.activation(sq4[:, :, :], centred, ACT.Square).then_inc(s("sq4"), 1)
                act.wait_ge(s("var4"), nth)
                step(a.activation(rs4[:, :], rs4[:, :], ACT.Ln, scale=1.0 / C, bias=wl[:, 31:32]))
                a.activation(rs4[:, :], rs4[:, :], ACT.Exp, scale=-0.5).then_inc(s("rs4"), 1)

            def stack_high(nth):
                for h in range(NH):
                    act.wait_ge(s("xlt"), 2 * nth - 1 + h)
                    a.activation(xst[:, B * h:B * h + B, 0:3:2, :],
                                 xlt[:, B * h:B * h + B, None, :].broadcast_to([P, B, 2, C]), ACT.Copy
                                 ).then_inc(s("x_high"), 1)
                act.wait_ge(s("xs_ps"), 2 * nth - 1)
                a.activation(xs[:, 0, :, :].rearrange("p b n -> p (b n)"), bank(7).bitcast(F16)[:, 0:512], ACT.Copy
                             ).then_inc(s("xs_a"), 1)

            def copy_taps(dst, src):
                return a.activation(dst, src, ACT.Copy)

            a.preload_act_table_set("natural_log_exp_and_others")
            act.wait_ge(s("in_cols"), landed["in_cols"])
            a.activation(wl[:, 16:17], col[:, COL_SIGMA:COL_SIGMA + 1], ACT.Ln).then_inc(s("sig"), 1)
            act.wait_ge(s("sig"), 1)
            a.activation(wl[:, 17:18], wl[:, 16:17], ACT.Exp, scale=0.25).then_inc(s("sig"), 1)
            act.wait_ge(s("lmax"), 1)
            a.activation(wl[:, 4:8], wl[:, 0:4], ACT.Exp, bias=wl[:, 8:9]).then_inc(s("lexp"), 1)
            act.wait_ge(s("in_cols"), landed["in_cols"])
            act.wait_ge(s("qk0"), 2)
            a.activation(khi[:, :], bank(7, 0, N), ACT.Identity, bias=col[:, COL_BK:COL_BK + 1]).then_inc(s("khi"), 1)
            act.wait_ge(s("gbv"), 2)
            a.activation(kall[:, :], bank(7, 0, N), ACT.Identity, bias=wl[:, 32:33], scale=col[:, COL_KL:COL_KL + 1]
                         ).then_inc(s("khi"), 1)
            act.wait_ge(s("w2_ps"), 1)
            a.activation(w2_sb[:, 0:P], bank(6, 0, P), ACT.Copy, scale=float(C) ** -0.5).then_inc(s("w2"), 1)
            act.wait_ge(s("v0_ps"), 1)
            for h in range(NH):
                a.activation(vtok[:, h, :, :], bank(5, 128 * h, 128 * h + 128).rearrange("p (b c) -> p b c", b=B),
                             ACT.Copy).then_inc(s("v0"), 1)
            act.wait_ge(s("gbv"), 1)
            a.activation(xg[:, :], x_cl[:, :], ACT.Identity, bias=wl[:, 30:31]).then_inc(s("xg"), 1)
            for b in range(B):
                act.wait_ge(s("sT0"), b + 1)
                a.activation(pT[:, b, :, :], sc_bank[:, b, :, :], ACT.Exp).then_inc(s("pT0"), 1)
            act.wait_ge(s("in_d"), landed["in_d"])
            act.wait_ge(s("w2"), 1)
            a.activation(w2hi[:, :], w2_sb[:, :], ACT.Copy, scale=col[:, COL_WS:COL_WS + 1]).then_inc(s("w2"), 1)
            act.wait_ge(s("gn_stat"), 1)
            act.wait_ge(s("eps_ready"), 1)
            step(a.activation(rs[:, 0:1], st2[:, 1:2], ACT.Ln, bias=wl[:, 31:32]))
            a.activation(rs[:, 1:2], rs[:, 0:1], ACT.Exp, scale=-0.5).then_inc(s("gn_rstd"), 1)
            act.wait_ge(s("ptc_ps"), 1)
            a.activation(ptc[:, :, :].rearrange("p h n -> p (h n)"), bank(5, 0, N), ACT.Copy).then_inc(s("ptc"), 1)
            act.wait_ge(s("ms_ps"), 2)
            for k in range(2):
                a.activation(ms[:, 512 * k:512 * k + 512], ps[0:2 * KF, 7 - 4 * k, :], ACT.Copy).then_inc(s("ms"), 1)
            act.wait_ge(s("y_pad"), 6)
            a.activation(sq3[:, :, :, :], y3[:, :, :, :], ACT.Square).then_inc(s("ysq"), 1)
            act.wait_ge(s("lap_ps"), 1)
            a.activation(absd[:, :], ps[0:B, 4, 0:N], ACT.Abs).then_inc(s("absd"), 1)
            act.wait_ge(s("n2"), 1)
            step(a.activation(nt[:, :, :], n2[:, :, :], ACT.Ln, scale=float(2 ** 40)))
            a.activation(rn[:, :, :], nt[:, :, :], ACT.Exp, scale=-0.5, bias=wl[:, 29:30]).then_inc(s("rn0"), 1)
            act.wait_ge(s("gvar"), 1)
            step(a.activation(gmu[:, 3:4], gmu[:, 2:3], ACT.Ln, bias=wl[:, 31:32]))
            a.activation(gmu[:, 4:5], gmu[:, 3:4], ACT.Exp, scale=-0.5).then_inc(s("grstd"), 1)

            def taps_out(k):
                act.wait_ge(s("gtap_ps"), k + 1)
                a.activation(gtap[:, 2 * k:2 * k + 2, :].rearrange("p g t -> p (g t)"), bank(7 - k % 2), ACT.Copy, scale=TAP_SCALE
                             ).then_inc(s("gtap"), 1)

            taps_out(0)
            taps_out(1)
            act.wait_ge(s("sim"), 1)
            a.activation(wts[:, :, :], sim[:, :, :], ACT.Exp).then_inc(s("simexp"), 1)
            act.wait_ge(s("gab"), 1)
            a.activation(gy[:, :], shifted(y3, 0, 0), ACT.Identity,
                         scale=gmu[:, 5:6], bias=gmu[:, 7:8]).then_inc(s("gy"), 1)
            taps_out(2)
            taps_out(3)
            act.wait_ge(s("hid_ps"), 1)
            act.wait_ge(s("in_e"), landed["in_e"])
            a.activation(hid[:, 0, :], bank(4, 0, N), ACT.Relu, bias=col[:, COL_B1:COL_B1 + 1]).then_inc(s("hid_a"), 1)
            act.wait_ge(s("quarter0"), 64)
            taps_high(copy_taps, 0).then_inc(s("taps_act"), 1)
            act.wait_ge(s("tc_ps"), 2)
            token_rstd(1, bank(6, 0, N).rearrange("p (g c) -> p g c", c=C))
            stack_high(1)
            for h in range(NH):
                act.wait_ge(s("gq_ps"), h + 1)
                a.activation(ghi[:, h, :, :].rearrange("p b n -> p (b n)"), bank(h), ACT.Copy,
                             scale=col[:, COL_WS:COL_WS + 1]).then_inc(s("ghi"), 1)
            act.wait_ge(s("v2_ps"), 1)
            for h in range(NH):
                a.activation(vtok[:, h, :, :], bank(4, 128 * h, 128 * h + 128).rearrange("p (b c) -> p b c", b=B),
                             ACT.Copy).then_inc(s("v2"), 1)
            for c in (1, 2):
                act.wait_ge(s("quarter%d" % c), 64)
                taps_high(copy_taps, c).then_inc(s("taps_act"), 1)
            for b in range(B):
                act.wait_ge(s("sT2"), b + 1)
                a.activation(pT[:, b, :, :].rearrange("p h n -> p (h n)")[:, 0:384], bank(b, 0, 384), ACT.Exp
                             ).then_inc(s("pT2"), 1)
            act.wait_ge(s("quarter0"), 64 * 2)
            taps_high(copy_taps, 3).then_inc(s("taps_act"), 1)
            ln_tail(1, bank(6, 0, N), bank(6, 256, 512))
            act.wait_ge(s("u4_ps"), 2)
            a.activation(u4[:, 0, :, :].rearrange("p b (h a) -> p h b a", h=2),
                         bank(7, 0, 256).rearrange("p (h b a) -> p h b a", h=2, b=B), ACT.Copy).then_inc(s("u4"), 1)
            act.wait_ge(s("w3"), 1)
            a.activation(whi[:, :], w3_sb[:, :], ACT.Copy, scale=col[:, COL_WS:COL_WS + 1]).then_inc(s("whi"), 1)

            act.wait_ge(s("tc_ps"), 6)
            token_rstd(2, bank(6, 0, N).rearrange("p (g c) -> p g c", c=C))
            stack_high(2)
            for t in range(16):
                act.wait_ge(s("qk3_ps"), t + 1)
                if t >= 4:
                    act.wait_ge(s("qk3"), t - 3)
                a.activation(ee[:, t % 4, :], bank(t % 4), ACT.Exp, bias=wl[:, 28:29]).then_inc(s("qk3_exp"), 1)
                if t in (5, 7, 9, 11):
                    b = (t - 5) // 2
                    act.wait_ge(s("kxt_ps"), b + 1)
                    a.activation(kxt[:, b, :], ps[0:XA, 4 + b % 2, :], ACT.Copy).then_inc(s("kxt"), 1)
                if t in (10, 12, 14, 15):
                    b = (t - 9) // 2
                    act.wait_ge(s("kvd_ps"), b + 1)
                    a.activation(kvd[:, b, :, :], bank(6 + b % 2, 0, HG * 66).rearrange("p (g n) -> p g n", g=HG), ACT.Copy
                                 ).then_inc(s("kvd"), 1)
            for bp in range(2):
                act.wait_ge(s("rT_ps"), 2 * bp + 2)
                a.activation(rT[:, bp, :], bank(4 + bp, 0, 128).bitcast(BF16), ACT.Copy).then_inc(s("rT"), 1)
            act.wait_ge(s("xc4"), 1)
            token_rstd(3, xc4[:, :, :])
            stack_high(3)
            act.wait_ge(s("lx0"), 1)
            a.activation(lx[:, :, :], lx[:, :, :], ACT.Exp).then_inc(s("lexp4"), 1)
            for h in range(NH):
                act.wait_ge(s("fin_ps"), h + 1)
                a.activation(x_out[:, 128 * h:128 * h + 128], bank(4 + 2 * h, 0, 128), ACT.Copy).then_inc(s("x_out"), 1)

        @block.vector
        def _(dve):
            v = nc.vector
            chain_count = [0]

            def small(ins):
                chain_count[0] += 1
                ins.then_inc(s("small"), 1)
                dve.wait_ge(s("small"), chain_count[0])

            def ln_apply(nth, out_ap):
                dve.wait_ge(s("ln_center"), 2 * nth)
                dve.wait_ge(s("ln_rstd"), nth)
                v.tensor_tensor(out_ap, bank(5, 0, N), rstd[:, :], ALU.mult).then_inc(s("ln_xln"), 1)

            def normalise_stack(nth, centred):
                dve.wait_ge(s("sq4"), nth)
                v.tensor_reduce(rs4[:, :], sq4[:, :, :], AX, ALU.add).then_inc(s("var4"), 1)
                dve.wait_ge(s("rs4"), nth)
                for h in range(NH):
                    gs = slice(B * h, B * h + B)
                    v.tensor_tensor(xlt[:, gs, :], centred[:, gs, :], rs4[:, gs, None].broadcast_to([P, B, C]), ALU.mult
                                    ).then_inc(s("xlt"), 1)
                for h in range(NH):
                    gs = slice(B * h, B * h + B)
                    dve.wait_ge(s("x_high"), 2 * nth - 1 + h)
                    v.tensor_tensor(xst[:, gs, 1, :], xlt[:, gs, :], xst[:, gs, 0, :], ALU.subtract
                                    ).then_inc(s("x_low"), 1)

            def stack_second(nth):
                dve.wait_ge(s("xs_ps"), 2 * nth)
                v.tensor_copy(xs[:, 1, :, :].rearrange("p b n -> p (b n)"), bank(6).bitcast(F16)[:, 0:512]
                              ).then_inc(s("xs_b"), 1)

            v.memset(wl[:, 31:32], 1e-5)
            v.memset(wl[:, 29:30], 20.0 * LN2)
            v.memset(wl[:, 28:29], -1.0).then_inc(s("eps_ready"), 1)
            dve.wait_ge(s("in_cols"), landed["in_cols"])
            v.tensor_tensor(wl[:, 30:31], col[:, COL_GAMMA:COL_GAMMA + 1], col[:, COL_BV:COL_BV + 1], ALU.mult
                            ).then_inc(s("gbv"), 1)
            v.tensor_tensor(wl[:, 32:33], col[:, COL_BK:COL_BK + 1], col[:, COL_KL:COL_KL + 1], ALU.mult
                            ).then_inc(s("gbv"), 1)
            small(v.tensor_tensor(wl[:, 0:4], col[:, COL_LOGW:COL_LOGW + 4], col[:, COL_GUMBEL:COL_GUMBEL + 4], ALU.add))
            v.tensor_reduce(wl[:, 8:9], wl[:, 0:4], AX, ALU.max, negate=True).then_inc(s("lmax"), 1)
            dve.wait_ge(s("lexp"), 1)
            small(v.tensor_reduce(wl[:, 9:10], wl[:, 4:8], AX, ALU.add))
            small(v.reciprocal(wl[:, 10:11], wl[:, 9:10]))
            small(v.tensor_scalar(wl[:, 4:8], wl[:, 4:8], wl[:, 10:11], None, ALU.mult))
            dve.wait_ge(s("qk0"), 1)
            v.tensor_scalar(qhi[:, :], bank(4, 0, N), col[:, COL_BQ:COL_BQ + 1], float(C) ** -0.5, ALU.add, ALU.mult)
            small(v.tensor_scalar(qall[:, :], bank(4, 0, N), col[:, COL_BQ:COL_BQ + 1], col[:, COL_QL:COL_QL + 1],
                                  ALU.add, ALU.mult))
            v.scalar_tensor_tensor(out=q0[:, :], in0=qhi[:, :], scalar=col[:, COL_QS:COL_QS + 1], in1=qall[:, :],
                                   op0=ALU.mult, op1=ALU.add).then_inc(s("q0"), 1)
            dve.wait_ge(s("khi"), 2)
            v.scalar_tensor_tensor(out=k0[:, :], in0=khi[:, :], scalar=col[:, COL_KS:COL_KS + 1], in1=kall[:, :],
                                   op0=ALU.mult, op1=ALU.add).then_inc(s("k0"), 1)
            for b in range(B):
                dve.wait_ge(s("s0"), b + 1)
                reduced = v.tensor_reduce(nmax[:, :, b], sc_bank[:, b, :, :], AX, ALU.max, negate=True)
            small(reduced)

            def split_max(nth):
                small(v.tensor_copy(nmb[:, :, :], nmax[:, :, :]))
                if nth == 1:
                    dve.wait_ge(s("filled"), filled["nmhl"])
                v.tensor_copy(nmhl[:, :, :, 0], nmb[:, :, :])
                v.tensor_tensor(nmhl[:, :, :, 1], nmax[:, :, :], nmb[:, :, :], ALU.subtract).then_inc(s("max_nm"), 1)
                dve.wait_ge(s("max_nmT"), 2 * nth)
                v.tensor_copy(nmt[:, :], bank(4, 256, 512)).then_inc(s("max_nmt"), 1)

            split_max(1)
            small(v.tensor_reduce(wl[:, 11:12], wl[:, 4:8], AX, ALU.max))
            small(v.tensor_scalar(wl[:, 0:4], wl[:, 4:8], wl[:, 11:12], None, ALU.is_equal))
            small(v.tensor_scalar(wl[:, 12:13], wl[:, 0:1], -1.0, 1.0, ALU.mult, ALU.add))
            for i in range(1, NRES):
                small(v.tensor_tensor(wl[:, i:i + 1], wl[:, i:i + 1], wl[:, 12:13], ALU.mult))
                small(v.tensor_tensor(wl[:, 12:13], wl[:, 12:13], wl[:, i:i + 1], ALU.subtract))
            small(v.tensor_tensor(wl[:, 20:24], wl[:, 0:4], wl[:, 4:8], ALU.subtract))
            small(v.tensor_tensor(wl[:, 20:24], wl[:, 20:24], wl[:, 4:8], ALU.add))
            small(v.tensor_tensor(wl[:, 24:28], wl[:, 20:24], col[:, COL_RES:COL_RES + 4], ALU.mult))
            small(v.tensor_reduce(wl[:, 13:14], wl[:, 24:28], AX, ALU.add))
            dve.wait_ge(s("sig"), 2)
            small(v.tensor_tensor(wl[:, 14:15], wl[:, 13:14], wl[:, 17:18], ALU.mult))
            dve.wait_ge(s("in_c"), landed["in_c"])
            v.tensor_scalar(mixw[:, :], ksel, wl[:, 14:15], None, ALU.mult).then_inc(s("mixw"), 1)
            dve.wait_ge(s("in_d"), landed["in_d"])
            small(v.tensor_scalar(mumix[:, :], mu_sb[:, 0, :], wl[:, 20:21], None, ALU.mult))
            for i in range(1, NRES):
                small(v.scalar_tensor_tensor(out=mumix[:, :], in0=mu_sb[:, i, :], scalar=wl[:, 20 + i:21 + i],
                                             in1=mumix[:, :], op0=ALU.mult, op1=ALU.add))
            small(v.tensor_scalar(segm[:, :], seg[:, 0, :], wl[:, 0:1], None, ALU.mult))
            for i in range(1, NRES):
                small(v.scalar_tensor_tensor(out=segm[:, :], in0=seg[:, i, :], scalar=wl[:, i:i + 1], in1=segm[:, :],
                                             op0=ALU.mult, op1=ALU.add))
            dve.wait_ge(s("w2"), 2)
            v.scalar_tensor_tensor(out=w2st[:, :], in0=w2_sb[:, :], scalar=col[:, COL_WL:COL_WL + 1], in1=w2hi[:, :],
                                   op0=ALU.mult, op1=ALU.add).then_inc(s("w2st"), 1)
            dve.wait_ge(s("sum0"), 1)
            small(v.reciprocal(gy[:, :], bank(5, 0, N)))
            dve.wait_ge(s("o0"), 1)
            small(v.tensor_tensor(gy[:, :], bank(6, 0, N), gy[:, :], ALU.mult))
            dve.wait_ge(s("xg"), 1)
            small(v.scalar_tensor_tensor(out=x0[:, :], in0=gy[:, :], scalar=col[:, COL_GAMMA:COL_GAMMA + 1],
                                         in1=xg[:, :], op0=ALU.mult, op1=ALU.add))
            small(v.bn_stats(st6[:, :], x0[:, :]))
            v.bn_aggr(st2[:, :], st6[:, :]).then_inc(s("gn_stat"), 1)
            dve.wait_ge(s("gn_stat"), 1)
            dve.wait_ge(s("gn_rstd"), 1)
            v.tensor_scalar(shifted(y3, 0, 0), x0[:, :], st2[:, 0:1], rs[:, 1:2], ALU.subtract, ALU.mult
                            ).then_inc(s("y_pad"), 1)
            dve.wait_ge(s("y_pad"), 1)
            img = y3[:, 1, 1:1 + HW, :]
            v.tensor_copy(y3[:, 0, 1:1 + HW, 1:HW], img[:, :, 0:HW - 1]).then_inc(s("y_pad"), 1)
            v.tensor_copy(y3[:, 2, 1:1 + HW, 0:HW - 1], img[:, :, 1:HW]).then_inc(s("y_pad"), 1)
            v.tensor_copy(y3[:, 0, 1:1 + HW, 0:1], img[:, :, 1:2]).then_inc(s("y_pad"), 1)
            v.tensor_copy(y3[:, 2, 1:1 + HW, HW - 1:HW], img[:, :, HW - 2:HW - 1]).then_inc(s("y_pad"), 1)
            dve.wait_ge(s("y_pad"), 5)
            v.tensor_copy(y3[:, :, 0::PAD - 1, :], y3[:, :, 2::PAD - 5, :]).then_inc(s("y_pad"), 1)
            dve.wait_ge(s("y_pad"), 6)
            dve.wait_ge(s("av_ps"), 1)
            v.tensor_scalar(av[:, :, :], av_ps, 1.0 / C, None, ALU.mult).then_inc(s("av"), 1)
            small(v.bn_stats(gst6[:, :], shifted(y3, 0, 0)))
            small(v.bn_aggr(gmv[:, :], gst6[:, :]))
            v.tensor_copy(gme[:, 0:1], gmv[:, 0:1])
            v.scalar_tensor_tensor(out=gme[:, 1:2], in0=gmv[:, 0:1], scalar=gmv[:, 0:1], in1=gmv[:, 1:2],
                                   op0=ALU.mult, op1=ALU.add).then_inc(s("gme"), 1)
            dve.wait_ge(s("ptc"), 1)
            for j in range(4):
                dve.wait_ge(s("pt_ps"), 2 * j + 2)
                v.tensor_tensor(prod[:, 2 * j:2 * j + 2, :, :].rearrange("p k h n -> p k (h n)"),
                                pt[:, 2 * j:2 * j + 2, :, :].rearrange("p k h n -> p k (h n)"),
                                ptc[:, :, :].rearrange("p h n -> p (h n)")[:, None, :].broadcast_to([P, 2, N]), ALU.mult
                                ).then_inc(s("prod"), 1)
            prodc = prod[:, :, :, :].rearrange("p k h (b c) -> p (k h b) c", b=B)
            for j in (0, 1):
                dve.wait_ge(s("prod"), 2 * j + 2)
                v.tensor_reduce(dot[:, 5 * j:5 * j + 4, :].rearrange("p k g -> p (k g)"),
                                prodc[:, 32 * j:32 * j + 32, :], AX, ALU.add).then_inc(s("dot"), 1)
            dve.wait_ge(s("absd"), 1)
            v.tensor_reduce(dstat[:, 0:1], absd[:, :], AX, ALU.max)
            small(v.tensor_reduce(dstat[:, 1:2], absd[:, :], AX, ALU.min))
            small(v.tensor_tensor(dstat[:, 2:3], dstat[:, 0:1], dstat[:, 1:2], ALU.subtract))
            small(v.tensor_scalar(dstat[:, 3:4], dstat[:, 2:3], 1e-8, None, ALU.add))
            v.reciprocal(dstat[:, 4:5], dstat[:, 3:4]).then_inc(s("dstat"), 1)
            dve.wait_ge(s("n2_ps"), 1)
            n2p = n2_ps.rearrange("p k h b -> p k (h b)")
            v.tensor_scalar(n2[:, :, :], n2p, 1e-24, None, ALU.max).then_inc(s("n2"), 1)
            v.tensor_copy(dot[:, 4, :], n2p[:, 4, :]).then_inc(s("dot"), 1)
            dve.wait_ge(s("dot"), 2)
            v.memset(quarter(2)[0][:, :, 0:TAPS], 0.0).then_inc(s("dot"), 1)
            dve.wait_ge(s("gpair_ps"), 1)
            small(v.tensor_copy(gmu[:, 0:2], bank(4, 272, 274)))
            small(v.tensor_tensor(gmu[:, 6:7], gmu[:, 0:1], gmu[:, 0:1], ALU.mult))
            v.tensor_tensor(gmu[:, 2:3], gmu[:, 1:2], gmu[:, 6:7], ALU.subtract).then_inc(s("gvar"), 1)
            dve.wait_ge(s("rn0"), 1)
            small(v.scalar_tensor_tensor(out=nt[:, :, :], in0=n2[:, :, :], scalar=-0.5, in1=rn[:, :, :],
                                         op0=ALU.mult, op1=ALU.mult))
            small(v.tensor_tensor(nt[:, :, :], nt[:, :, :], rn[:, :, :], ALU.mult))
            small(v.scalar_tensor_tensor(out=n2[:, :, :], in0=nt[:, :, :], scalar=1.5, in1=rn[:, :, :],
                                         op0=ALU.add, op1=ALU.mult))
            dve.wait_ge(s("dot"), 3)
            small(v.tensor_tensor(sim[:, :, :], dot[:, :, :], n2[:, :, :], ALU.mult))
            v.tensor_tensor(sim[:, :, :], sim[:, :, :], n2[:, 4:5, :].broadcast_to([P, KN, NH * B]), ALU.mult
                            ).then_inc(s("sim"), 1)
            dve.wait_ge(s("sim"), 1)
            dve.wait_ge(s("filled"), filled["ge"])
            for d in range(1, KN):
                pairs = ge[:, :, :, :].rearrange("p j k g -> p (j k) g")[:, d:(KN - d) * KN:KN + 1, :]
                compare = v.tensor_tensor(pairs, sim[:, 0:KN - d, :], sim[:, d:KN, :], ALU.is_ge)
            small(compare)
            small(v.tensor_tensor(gd[:, :, :, :], ge[:, :, :, :], ge[:, :, :, :].rearrange("p j k g -> p k j g"),
                                  ALU.subtract))
            dve.wait_ge(s("grstd"), 1)
            small(v.tensor_tensor(gmu[:, 5:6], gmu[:, 4:5], col[:, COL_GNW:COL_GNW + 1], ALU.mult))
            small(v.tensor_tensor(gmu[:, 6:7], gmu[:, 0:1], gmu[:, 5:6], ALU.mult))
            v.tensor_tensor(gmu[:, 7:8], col[:, COL_GNB:COL_GNB + 1], gmu[:, 6:7], ALU.subtract).then_inc(s("gab"), 1)
            small(v.tensor_reduce(rank[:, :, :], gd[:, :, :, :].rearrange("p j k g -> p k g j"), AX, ALU.add))
            dve.wait_ge(s("cntT_ps"), 1)
            small(v.tensor_scalar(wsum[:, :], bank(4, 256, 264), -MAGIC, None, ALU.add))
            small(v.tensor_tensor(rk[:, :, :], wsum[:, None, :].broadcast_to([P, KN, NH * B]),
                                  rankoff[:, 0:KN, None].broadcast_to([P, KN, NH * B]), ALU.add))
            small(v.tensor_tensor(rank[:, :, :], rank[:, :, :], rk[:, :, :], ALU.is_le))
            dve.wait_ge(s("simexp"), 1)
            small(v.tensor_tensor(wts[:, :, :], wts[:, :, :], rank[:, :, :], ALU.mult))
            small(v.tensor_reduce(wsum[:, :], wts[:, :, :].rearrange("p k g -> p g k"), AX, ALU.add))
            small(v.reciprocal(wsum[:, :], wsum[:, :]))
            small(v.tensor_tensor(wts[:, :, :], wts[:, :, :], wsum[:, None, :].broadcast_to([P, KN, NH * B]), ALU.mult))
            dve.wait_ge(s("gtap"), 4)
            v.scalar_tensor_tensor(out=gtap[:, :, 0:TAPS], in0=mumix[:, :].rearrange("p (g l) -> p g l", g=8),
                                   scalar=TAP_SCALE, in1=gtap[:, :, 0:TAPS], op0=ALU.mult, op1=ALU.add
                                   ).then_inc(s("gtap_mu"), 1)
            dve.wait_ge(s("gtap_ps"), 4)
            for k in range(KN):
                src = ptc if k == 4 else pt[:, k - (k > 4), :, :]
                v.tensor_tensor(wprod[:, k, :, :].rearrange("p h (b c) -> p (h b) c", b=B),
                                src[:, :, :].rearrange("p h (b c) -> p (h b) c", b=B),
                                wts[:, k, :, None].broadcast_to([P, NH * B, C]), ALU.mult).then_inc(s("wprod"), 1)
            dve.wait_ge(s("att1_ps"), 1)
            dve.wait_ge(s("gy"), 1)
            v.tensor_tensor(enh[:, :], bank(7, 0, N), gy[:, :], ALU.add).then_inc(s("enh"), 1)
            dve.wait_ge(s("enh"), 1)
            small(v.tensor_tensor(xe[:, :], enh[:, :], x0[:, :], ALU.add))
            dve.wait_ge(s("hid_ps"), 2)
            v.tensor_scalar(hid[:, 1, :], bank(0, 0, N), col[:, COL_B1:COL_B1 + 1], 0.0, ALU.add, ALU.max
                            ).then_inc(s("hid_b"), 1)
            dve.wait_ge(s("mlp_ps"), 1)
            v.scalar_tensor_tensor(out=x1[:, :], in0=bank(5, 0, N), scalar=col[:, COL_B2:COL_B2 + 1], in1=xe[:, :],
                                   op0=ALU.add, op1=ALU.add).then_inc(s("x1"), 1)
            dve.wait_ge(s("tc_ps"), 4)
            normalise_stack(1, bank(5, 0, N).rearrange("p (g c) -> p g c", c=C))
            stack_second(1)
            for h in range(NH):
                dve.wait_ge(s("ghi"), h + 1)
                v.scalar_tensor_tensor(out=gst[:, h, :, :].rearrange("p b n -> p (b n)"), in0=bank(h),
                                       scalar=col[:, COL_WL:COL_WL + 1],
                                       in1=ghi[:, h, :, :].rearrange("p b n -> p (b n)"), op0=ALU.mult, op1=ALU.add
                                       ).then_inc(s("gst"), 1)
            for b in range(B):
                dve.wait_ge(s("s2"), b + 1)
                v.tensor_reduce(nmax[:, 0, b:b + 1], bank(b, 0, 128), AX, ALU.max, negate=True)
                reduced = v.tensor_reduce(nmax[:, 1, b:b + 1], bank(b, 128, 384), AX, ALU.max, negate=True)
            small(reduced)
            split_max(2)
            dve.wait_ge(s("taps_act"), 2)
            taps_low(v.tensor_tensor, 1).then_inc(s("taps_dve"), 1)
            dve.wait_ge(s("sum2"), 1)
            small(v.reciprocal(gy[:, :], bank(5, 0, N)))
            dve.wait_ge(s("o2"), 1)
            small(v.tensor_tensor(gy[:, :], bank(6, 0, N), gy[:, :], ALU.mult))
            v.tensor_tensor(t2[:, :], x1[:, :], gy[:, :], ALU.add).then_inc(s("t2"), 1)
            dve.wait_ge(s("taps_act"), 3)
            taps_low(v.tensor_tensor, 2).then_inc(s("taps_dve"), 1)
            ln_apply(1, xln[:, :])
            dve.wait_ge(s("ln_xln"), 1)
            v.transpose(xtr[:, :, :, :], xln[:, :].rearrange("p (h a r) -> p h r a", h=2, r=PH)).then_inc(s("xtr"), 1)
            dve.wait_ge(s("u4"), 1)
            v.tensor_tensor(u4[:, 1, :, :].rearrange("p b (h a) -> p h b a", h=2),
                            bank(7, 0, 256).rearrange("p (h b a) -> p h b a", h=2, b=B),
                            u4[:, 0, :, :].rearrange("p b (h a) -> p h b a", h=2), ALU.subtract).then_inc(s("u4"), 1)
            dve.wait_ge(s("whi"), 1)
            v.scalar_tensor_tensor(out=wst[:, :], in0=w3_sb[:, :], scalar=col[:, COL_WL:COL_WL + 1], in1=whi[:, :],
                                   op0=ALU.mult, op1=ALU.add).then_inc(s("wst"), 1)
            dve.wait_ge(s("w2h_ps"), 1)
            w2p = ps[0:XA, 1, :].rearrange("p (h e) -> p h e", h=HEADS)
            v.tensor_scalar(w2h[:, :, 0:C], w2p, col[0:XA, COL_MCOS:COL_MCOS + 1], None, ALU.mult)
            v.tensor_scalar(w2h[:, :, C:2 * C], w2p, col[0:XA, COL_MSIN:COL_MSIN + 1], None, ALU.mult)
            v.tensor_copy(w2h[:, :, 2 * C:2 * C + 2], kone_sb[:, None, :].broadcast_to([XA, HEADS, 2])).then_inc(s("w2h"), 1)
            dve.wait_ge(s("y_ps"), 1)
            v.tensor_tensor(ys[:, :, :, :], bank(0, 0, N).rearrange("p (b h a) -> p h b a", b=B, h=2),
                            segm[:, :].rearrange("p (h a) -> p h a", h=2)[:, :, None, :].broadcast_to([P, 2, B, NA // 2]),
                            ALU.mult).then_inc(s("ys"), 1)
            dve.wait_ge(s("z_ps"), 2)
            small(v.transpose(ych[:, :].rearrange("p (h r a) -> p h r a", h=2, r=PH),
                              bank(1, 0, N).rearrange("p (h r a) -> p h r a", h=2, r=PH)))
            v.tensor_tensor(t3[:, :].rearrange("p (h a r) -> p h a r", h=2, r=PH),
                            t2[:, :].rearrange("p (h a r) -> p h a r", h=2, r=PH),
                            ych[:, :].rearrange("p (h r a) -> p h a r", h=2, r=PH), ALU.add).then_inc(s("t3"), 1)
            dve.wait_ge(s("tc_ps"), 8)
            normalise_stack(2, bank(5, 0, N).rearrange("p (g c) -> p g c", c=C))
            stack_second(2)
            dve.wait_ge(s("filled"), filled["ksb"])
            for t in range(16):
                dve.wait_ge(s("qk3_exp"), t + 1)
                if t < 8:
                    dst, z, e = kf[:, t // 2, t % 2, :], bank(t % 4), ee[:, t % 4, :]
                else:
                    g0 = 2 * (t % 2)
                    dst = qf[:, g0:g0 + 2, (t - 8) // 2, :]
                    z = bank(t % 4).rearrange("p (g n) -> p g n", g=2)
                    e = ee[:, t % 4, :].rearrange("p (g n) -> p g n", g=2)
                v.scalar_tensor_tensor(out=dst, in0=e, scalar=1.0, in1=z, op0=ALU.min, op1=ALU.max
                                       ).then_inc(s("qk3"), 1)
                if t in (13, 15):
                    bp = (t - 13) // 2
                    dve.wait_ge(s("kvd"), 2 * bp + 2)
                    v.tensor_tensor(ksb[:, 2 * HG * bp:2 * HG * bp + 2 * HG, 0:8].rearrange("p g (k t) -> p g k t", t=2),
                                    kvd[:, 2 * bp:2 * bp + 2, :, 64:66].rearrange("p b g t -> p (b g) t")[
                                        :, :, None, :].broadcast_to([P, 2 * HG, 4, 2]),
                                    col[:, None, COL_KVM:COL_KVM + 4, None].broadcast_to([P, 2 * HG, 4, 2]), ALU.mult
                                    ).then_inc(s("ksb"), 1)
            dve.wait_ge(s("in_g"), landed["in_g"])
            for bp in range(2):
                dve.wait_ge(s("den_ps"), bp + 1)
                v.tensor_tensor(dcs[:, 2 * bp:2 * bp + 2, :], bank(4 + bp).rearrange("p (b n) -> p b n", b=2),
                                csd[:, None, :].broadcast_to([P, 2, N]), ALU.mult).then_inc(s("dcs"), 1)
            dve.wait_ge(s("filled"), filled["r3"])
            for bp in range(2):
                dve.wait_ge(s("dent_ps"), bp + 1)
                dv = den[:, :, 2 * HEADS * bp:2 * HEADS * bp + 2 * HEADS].rearrange("p h (b k) -> p h b k", b=2)
                parts = [r3[:, :, 2 * bp:2 * bp + 2, HEADS * k:HEADS * k + HEADS] for k in range(3)]
                small(v.tensor_scalar(den[:, :, 2 * HEADS * bp:2 * HEADS * bp + 2 * HEADS],
                                      bank(7 - bp, 0, 4 * HEADS).rearrange("p (h k) -> p h k", h=NH), 1e-5, None, ALU.add))
                small(v.reciprocal(den[:, :, 2 * HEADS * bp:2 * HEADS * bp + 2 * HEADS],
                                   den[:, :, 2 * HEADS * bp:2 * HEADS * bp + 2 * HEADS]))
                small(v.tensor_copy(parts[0], dv))
                small(v.tensor_tensor(dv, dv, parts[0], ALU.subtract))
                small(v.tensor_copy(parts[1], dv))
                small(v.tensor_tensor(dv, dv, parts[1], ALU.subtract))
                v.tensor_copy(parts[2], dv).then_inc(s("r3"), 1)
            for t in range(8):
                dve.wait_ge(s("rb_ps"), t + 1)
                b, gp = 2 * (t // 4) + t % 2, t // 2 % 2
                dst = qf[:, 2 * gp:2 * gp + 2, b, :]
                v.tensor_tensor(dst, dst, bank(t % 4).rearrange("p (g n) -> p g n", g=2), ALU.mult).then_inc(s("qs"), 1)
            for bp in range(2):
                dve.wait_ge(s("y3_ps"), bp + 1)
                v.tensor_tensor(ycs[:, bp, :], bank(6 + bp, 0, N), csy, ALU.mult).then_inc(s("ycs"), 1)
            dve.wait_ge(s("t4_ps"), 1)
            small(v.tensor_tensor(t4[:, :, :], bank(4, 0, N).rearrange("p (h n) -> p h n", h=NH),
                                  denseb_sb[:, None, :].broadcast_to([P, NH, P]), ALU.add))
            t4g = t4[:, :, :].rearrange("p h (b c) -> p (h b) c", b=B)
            small(v.tensor_reduce(mn4[:, :], t4g, AX, ALU.add))
            v.scalar_tensor_tensor(out=xc4[:, :, :], in0=mn4[:, :, None].broadcast_to([P, NH * B, C]),
                                   scalar=-1.0 / C, in1=t4g, op0=ALU.mult, op1=ALU.add).then_inc(s("xc4"), 1)
            dve.wait_ge(s("xc4"), 1)
            normalise_stack(3, xc4)
            stack_second(3)
            dve.wait_ge(s("rout_ps"), 1)
            dve.wait_ge(s("in_g"), landed["in_g"])
            small(v.tensor_copy(lg[:, :, :].rearrange("p g e -> p (g e)"), bank(5, 0, NH * B * NE)))
            small(v.tensor_reduce(lm[:, :], lg[:, :, :], AX, ALU.max))
            v.tensor_tensor(lx[:, :, :], lg[:, :, :], lm[:, :, None].broadcast_to([P, NH * B, NE]), ALU.subtract
                            ).then_inc(s("lx0"), 1)
            dve.wait_ge(s("filled"), filled["ge4"])
            for d in range(1, NE):
                pairs = ge4[:, :, :, :].rearrange("p g j k -> p g (j k)")[:, :, d:(NE - d) * NE:NE + 1]
                compare = v.tensor_tensor(pairs, lg[:, :, 0:NE - d], lg[:, :, d:NE], ALU.is_ge)
            small(compare)
            small(v.tensor_tensor(gd4[:, :, :, :], ge4[:, :, :, :].rearrange("p g j k -> p g k j"), ge4[:, :, :, :],
                                  ALU.subtract))
            small(v.tensor_reduce(rank4[:, :, :], gd4[:, :, :, :], AX, ALU.add))
            small(v.tensor_tensor(rank4[:, :, :], rank4[:, :, :],
                                  rankoff[:, None, 2:2 + NE].broadcast_to([P, NH * B, NE]), ALU.is_le))
            dve.wait_ge(s("lexp4"), 1)
            small(v.tensor_tensor(lx[:, :, :], lx[:, :, :], rank4[:, :, :], ALU.mult))
            small(v.tensor_reduce(lm[:, :], lx[:, :, :], AX, ALU.add))
            small(v.reciprocal(lm[:, :], lm[:, :]))
            small(v.tensor_tensor(lx[:, :, :], lx[:, :, :], lm[:, :, None].broadcast_to([P, NH * B, NE]), ALU.mult))
            dve.wait_ge(s("exp_ps"), 1)
            for h in range(NH):
                for b in range(B):
                    src = sc_bank[:, b, h, :].rearrange("p (e c) -> p e c", e=NE)
                    v.tensor_tensor(eprod[:, :, h, C * b:C * b + C], src,
                                    lx[:, B * h + b, :, None].broadcast_to([P, NE, C]), ALU.mult).then_inc(s("eprod"), 1)
            dve.wait_ge(s("eprod"), NH * B)
            v.tensor_reduce(esum[:, :], eprod[:, 0:NE_SUM, 1, :].rearrange("p e n -> p n e"), AX, ALU.add
                            ).then_inc(s("esum"), 1)

        @block.tensor
        def _(pe):
            t = nc.tensor

            def keep_clock(n, free):
                for _ in range(n):
                    t.matmul(bank(free), ones_bf[:, 0:P], ones_bf[:, :], start=True, stop=True)

            def strip(tile, b, lo=0, hi=N, rows=32):
                return tile[32 * b:32 * b + rows, lo:hi]

            def ln_matmuls(nth, src):
                for k in (6, 5):
                    t.matmul(bank(k, 0, N), center, src, start=True, stop=True).then_inc(s("ln_center"), 1)
                pe.wait_ge(s("ln_sq"), nth)
                t.matmul(bank(6, 256, 512), meanw, sq[:, :], start=True, stop=True).then_inc(s("ln_var"), 1)

            def max_rows(nth, n):
                pe.wait_ge(s("max_nm"), nth)
                for h in range(NH):
                    t.transpose(bank(4, 256 + 128 * h, 384 + 128 * h),
                                nmhl[:, h, :, :].rearrange("p b c -> p (b c)"), ident).then_inc(s("max_nmT"), 1)
                keep_clock(n, 7)
                pe.wait_ge(s("max_nmt"), nth)

            def turn_stack(nth):
                for h in range(NH):
                    pe.wait_ge(s("x_low"), 2 * nth - 1 + h)
                    for b in range(B):
                        g = B * h + b
                        mm = t.transpose(bank(7 - h).bitcast(F16)[:, 128 * b:128 * b + 128],
                                         xst[:, g, :, :].rearrange("p k c -> p (k c)"), ident_hf[:, :])
                    mm.then_inc(s("xs_ps"), 1)
                pe.wait_ge(s("xs_a"), nth)

            def centre_tokens(src):
                for k in (6, 5):
                    for h in range(NH):
                        t.matmul(bank(k, 128 * h, 128 * h + 128), src[:, 128 * h:128 * h + 128], center,
                                 start=True, stop=True).then_inc(s("tc_ps"), 1)

            pe.wait_ge(s("filled"), filled["ones_bf"])
            keep_clock(6, 0)
            pe.wait_ge(s("in_a"), landed["in_a"])
            for k in range(2):
                t.matmul(bank(4 + 3 * k, 0, N), w0_sb[:, k, :], x_cl[:, :], start=True, stop=True
                         ).then_inc(s("qk0"), 1)
            for h in range(NH):
                mm = t.matmul(bank(5, 128 * h, 128 * h + 128), x_cl[:, 128 * h:128 * h + 128], w0_sb[:, 2, :],
                              start=True, stop=True)
            mm.then_inc(s("v0_ps"), 1)
            keep_clock(3, 0)
            pe.wait_ge(s("q0"), 1)
            pe.wait_ge(s("k0"), 1)
            for b in range(B):
                for h in range(NH):
                    mm = t.matmul(sc_bank[:, b, h, :], strip(q0, b, 128 * h, 128 * h + 128, 4 * DQ), strip(k0, b, rows=4 * DQ),
                                  start=True, stop=True)
                mm.then_inc(s("s0"), 1)
            pe.wait_ge(s("in_d"), landed["in_d"])
            t.matmul(bank(6, 0, P), wqk2_sb[:, 0, :], wqk2_sb[:, 1, :], start=True, stop=True).then_inc(s("w2_ps"), 1)
            pe.wait_ge(s("in_b"), landed["in_b"])
            keep_clock(4, 7)
            max_rows(1, 3)
            for b in range(B):
                for h in range(NH):
                    t.matmul(sc_bank[:, b, h, :], strip(k0, b, 128 * h, 128 * h + 128, 4 * DQ), strip(q0, b, rows=4 * DQ),
                             start=True, stop=False)
                    mm = t.matmul(sc_bank[:, b, h, :], strip(ones_bf, b, 0, P, 2), strip(nmt, b, rows=2),
                                  start=False, stop=True)
                mm.then_inc(s("sT0"), 1)
            pe.wait_ge(s("v0"), 2)
            pe.wait_ge(s("filled"), filled["ones_f"])
            pe.wait_ge(s("w2"), 1)

            def attend0(b, k, weights, m):
                return t.matmul(ps[32 * b:32 * b + 32, k, 0:N], weights, pT[:, b, m, :],
                                start=(m == 0), stop=(m == 1), tile_position=(0, 32 * b))

            for b in range(B):
                pe.wait_ge(s("pT0"), b + 1)
                attend0(b, 6, vtok[:, 0, b, :], 0)
            for m in range(NH):
                for b in range(B):
                    mm = attend0(b, 5, ones_f[:, :], m)
            mm.then_inc(s("sum0"), 1)
            for b in range(B):
                mm = attend0(b, 6, vtok[:, 1, b, :], 1)
            mm.then_inc(s("o0"), 1)
            pe.wait_ge(s("mixw"), 1)
            for k in range(2):
                t.matmul(ps[0:2 * KF, 7 - 4 * k, :], mixw[:, :], mstu_sb[:, 512 * k:512 * k + 512],
                         start=True, stop=True).then_inc(s("ms_ps"), 1)

            pe.wait_ge(s("y_pad"), 1)
            for h in range(NH):
                mm = t.transpose(bank(5, 128 * h, 128 * h + 128), shifted(y3, 0, 0, h), ident)
            mm.then_inc(s("ptc_ps"), 1)
            for h in range(NH):
                mm = t.matmul(av_ps[:, h, :], shifted(y3, 0, 0, h), bo, start=True, stop=True)
            mm.then_inc(s("av_ps"), 1)
            pe.wait_ge(s("y_pad"), 6)
            for k, (dy, dx) in enumerate(nbr[:4] + nbr[5:]):
                if k == 6:
                    pe.wait_ge(s("ms"), 2)
                for h in range(NH):
                    mm = t.transpose(pt[:, k, h, :], shifted(y3, dy, dx, h), ident)
                mm.then_inc(s("pt_ps"), 1)
            pe.wait_ge(s("av"), 1)
            pe.wait_ge(s("in_c"), landed["in_c"])
            for h in range(NH):
                mm = t.matmul(ps[0:B, 4, 0:N], av[:, h, :], lap[:, h, :], start=(h == 0), stop=(h == NH - 1))
            mm.then_inc(s("lap_ps"), 1)
            pe.wait_ge(s("ysq"), 1)
            pe.wait_ge(s("ptc"), 1)
            for k, (dy, dx) in enumerate(nbr):
                for h in range(NH):
                    mm = t.matmul(n2_ps[:, k, h, :], shifted(sq3, dy, dx, h), bo, start=True, stop=True)
            mm.then_inc(s("n2_ps"), 1)
            pe.wait_ge(s("gme"), 1)
            pe.wait_ge(s("absd"), 1)
            t.matmul(bank(4, 272, 274), pairw, gme[:, :], start=True, stop=True).then_inc(s("gpair_ps"), 1)

            def spectral_taps(k):
                for eg in (2 * k, 2 * k + 1):
                    mm = t.matmul(bank(7 - k % 2, 256 * (eg % 2), 256 * (eg % 2) + 256),
                                  ms[:, 128 * eg:128 * eg + 128], phi_sb[:, :], start=True, stop=True)
                mm.then_inc(s("gtap_ps"), 1)

            pe.wait_ge(s("phi"), 1)
            spectral_taps(0)
            spectral_taps(1)
            for k in (2, 3):
                pe.wait_ge(s("gtap"), k - 1)
                spectral_taps(k)
                if k == 2:
                    pe.wait_ge(s("cnt"), 2)
                    pe.wait_ge(s("gvar"), 1)
                    for h in range(NH):
                        mm = t.transpose(bank(4, 256 + B * h, 260 + B * h), cnt[:, 128 * h:128 * h + 128], ident[0:B, 0:B])
                    mm.then_inc(s("cntT_ps"), 1)
            keep_clock(3, 5)
            pe.wait_ge(s("gtap"), 4)
            for k in range(KN):
                pe.wait_ge(s("wprod"), k + 1)
                for h in range(NH):
                    mm = t.matmul(bank(7, 128 * h, 128 * h + 128), wprod[:, k, h, :], ident, start=(k == 0 and h == 0),
                                  stop=(k == KN - 1), skip_group_check=True)
            mm.then_inc(s("att1_ps"), 1)
            pe.wait_ge(s("in_e"), landed["in_e"])
            pe.wait_ge(s("enh"), 1)
            for j in range(2):
                t.matmul(bank(4 - 4 * j, 0, N), wmlp1_sb[:, j, :], enh[:, :], start=True, stop=True
                         ).then_inc(s("hid_ps"), 1)
            pe.wait_ge(s("hid_a"), 1)
            t.matmul(bank(5, 0, N), wmlp2_sb[:, 0, :], hid[:, 0, :], start=True, stop=False)
            pe.wait_ge(s("hid_b"), 1)
            t.matmul(bank(5, 0, N), wmlp2_sb[:, 1, :], hid[:, 1, :], start=False, stop=True).then_inc(s("mlp_ps"), 1)

            pe.wait_ge(s("x1"), 1)
            centre_tokens(x1)
            keep_clock(8, 0)
            pe.wait_ge(s("filled"), filled["ident_hf"])
            turn_stack(1)
            pe.wait_ge(s("w2st"), 1)
            for h in range(NH):
                if h == 1:
                    pe.wait_ge(s("xs_b"), 1)
                t.matmul(bank(h), w2st[:, 0:P], xs[:, h, :, :].rearrange("p b n -> p (b n)"), start=True, stop=True
                         ).then_inc(s("gq_ps"), 1)
            for h in range(NH):
                for b in range(B):
                    mm = t.matmul(bank(4, 128 * h + C * b, 128 * h + C * b + C), xs[:, h, b, :], w2st[:, P:P + C],
                                  start=True, stop=True)
            mm.then_inc(s("v2_ps"), 1)
            keep_clock(5, 7)
            pe.wait_ge(s("gst"), 2)
            pe.wait_ge(s("filled"), filled["causal_bf"])
            pe.wait_ge(s("filled"), filled["ident_bf"])
            for b in range(B):
                t.matmul(bank(b, 0, 128), gst[:, 0, b, :], xs[:, 0, b, :], start=True, stop=False)
                t.matmul(bank(b, 0, 128), ident_bf[:, :], causal_bf[:, 0, :], start=False, stop=True)
                t.matmul(bank(b, 128, 384), gst[:, 1, b, :], xs[:, :, b, :], start=True, stop=False)
                t.matmul(bank(b, 256, 384), ident_bf[:, :], causal_bf[:, 0, :], start=False, stop=True
                         ).then_inc(s("s2"), 1)
            pe.wait_ge(s("v2"), 2)
            keep_clock(4, 7)
            max_rows(2, 3)
            for b in range(B):
                t.matmul(bank(b, 0, 256), xs[:, 0, b, :], gst[:, :, b, :], start=True, stop=False)
                t.matmul(bank(b, 0, 128), ident_bf[:, :], causal_bf[:, 1, :], start=False, stop=False)
                t.matmul(bank(b, 0, 256), strip(ones_bf, b, 0, P, 2), strip(nmt, b, rows=2), start=False, stop=True)
                t.matmul(bank(b, 256, 384), xs[:, 1, b, :], gst[:, 1, b, :], start=True, stop=False)
                t.matmul(bank(b, 256, 384), ident_bf[:, :], causal_bf[:, 1, :], start=False, stop=False)
                t.matmul(bank(b, 256, 384), strip(ones_bf, b, 0, P, 2), strip(nmt, b, 128, 256, 2), start=False, stop=True
                         ).then_inc(s("sT2"), 1)
            pe.wait_ge(s("v2"), 2)
            pe.wait_ge(s("filled"), filled["ones_f"])

            def attend(b, k, weights, m):
                lo, p0 = (0, 0) if m == 0 else (128, 256)
                return t.matmul(ps[32 * b:32 * b + 32, k, lo:N], weights,
                                pT[:, b, :, :].rearrange("p h n -> p (h n)")[:, p0:p0 + N - lo],
                                start=(m == 0), stop=(m == 1), tile_position=(0, 32 * b))

            for b in range(B):
                pe.wait_ge(s("pT2"), b + 1)
                attend(b, 6, vtok[:, 0, b, :], 0)
            for m in range(2):
                for b in range(B):
                    mm = attend(b, 5, ones_f[:, :], m)
            mm.then_inc(s("sum2"), 1)
            for b in range(B):
                mm = attend(b, 6, vtok[:, 1, b, :], 1)
            mm.then_inc(s("o2"), 1)

            keep_clock(7, 0)
            pe.wait_ge(s("t2"), 1)
            ln_matmuls(1, t2[:, :])
            pe.wait_ge(s("in_f"), landed["in_f"])
            for g in range(HG):
                mm = t.matmul(ps[0:XA, 1, 128 * g:128 * g + 128], wva_sb[:, g, :], dwbd_sb[:, g, :], start=True, stop=True)
            mm.then_inc(s("w2h_ps"), 1)
            keep_clock(6, 2)
            pe.wait_ge(s("xtr"), 1)
            for h in range(2):
                t.transpose(bank(7, 128 * h, 128 * h + 128), xtr[:, h, :, :].rearrange("p r d -> p (r d)"), ident
                            ).then_inc(s("u4_ps"), 1)
            pe.wait_ge(s("taps_act"), 4)
            yv = bank(0, 0, N).rearrange("p (b a) -> p b a", b=B)
            for tap_part, u_part in ((0, 0), (0, 1), (1, 0)):
                pe.wait_ge(s("u4"), u_part + 1)
                if tap_part == 1:
                    pe.wait_ge(s("taps_dve"), 2)
                    pe.wait_ge(s("taps_pool"), 2)
                for j in range(NA):
                    mm = t.matmul(yv[:, :, j:NA], ftap[:, tap_part, PH * j:PH * j + PH, :].rearrange("p r e -> p (r e)"),
                                  u4[:, u_part, :, 0:NA - j], start=(tap_part == u_part == j == 0),
                                  stop=(tap_part == 1 and j == NA - 1))
            mm.then_inc(s("y_ps"), 1)
            keep_clock(2, 2)
            pe.wait_ge(s("ys"), 1)
            pe.wait_ge(s("w2h"), 1)
            for h in range(2):
                t.transpose(bank(1, 128 * h, 128 * h + 128), ys[:, h, :, :].rearrange("p b a -> p (b a)"), ident
                            ).then_inc(s("z_ps"), 1)

            keep_clock(4, 2)
            pe.wait_ge(s("t3"), 1)
            centre_tokens(t3)
            keep_clock(8, 2)
            turn_stack(2)
            pe.wait_ge(s("wst"), 1)
            pe.wait_ge(s("filled"), filled["ones_bf"])

            def key_values(b):
                for h in range(NH):
                    pe.wait_ge(s("qk3"), 2 * b + h + 1)
                    if b == 0:
                        pe.wait_ge(s("xa"), h + 1)
                        pe.wait_ge(s("filled"), filled["xa"])
                    if b >= 2 and h == 0:
                        pe.wait_ge(s("kxt"), b - 1)
                    mm = t.matmul(ps[0:XA, 4 + b % 2, :], xa[:, h, b, :], kf[:, b, h, :], start=(h == 0),
                                  stop=(h == NH - 1))
                mm.then_inc(s("kxt_ps"), 1)

            def fold_values(b):
                pe.wait_ge(s("kxt"), b + 1)
                if b >= 2:
                    pe.wait_ge(s("kvd"), b - 1)
                for hd in range(HEADS):
                    q = 32 * (hd % 4)
                    mm = t.matmul(ps[q:q + 32, 6 + b % 2, 66 * (hd // 4):66 * (hd // 4) + 66],
                                  kxt[:, b, 32 * hd:32 * hd + 32], w2h[:, hd, :], start=True, stop=True,
                                  tile_position=(0, q))
                mm.then_inc(s("kvd_ps"), 1)

            def denominators(bp):
                pe.wait_ge(s("qk3"), 12 + 4 * bp)
                pe.wait_ge(s("ksb"), bp + 1)
                for b in (2 * bp, 2 * bp + 1):
                    for g in range(HG):
                        mm = t.matmul(ps[32 * g:32 * g + 32, 4 + bp, 256 * (b % 2):256 * (b % 2) + 256],
                                      ksb[:, HG * b + g, :], qf[:, g, b, :], start=True, stop=True,
                                      tile_position=(0, 32 * g))
                mm.then_inc(s("den_ps"), 1)

            pe.wait_ge(s("w2h"), 1)
            for n in range(16):
                if n >= 4:
                    pe.wait_ge(s("qk3"), n - 3)
                if n < 8:
                    b, h = n // 2, n % 2
                    if n == 1:
                        pe.wait_ge(s("xs_b"), 2)
                    t.matmul(bank(n % 4), xs[:, h, b, :], wst[:, WK:WE], start=True, stop=True
                             ).then_inc(s("qk3_ps"), 1)
                else:
                    b, gp = (n - 8) // 2, n % 2
                    for g in (2 * gp, 2 * gp + 1):
                        o = bank(n % 4, 256 * (g % 2), 256 * (g % 2) + 256)
                        mm = t.matmul(o, wst[:, WQ + 128 * g:WQ + 128 * g + 128], xs[:, :, b, :], start=True, stop=True)
                    mm.then_inc(s("qk3_ps"), 1)
                if n in (5, 7, 9, 11):
                    key_values((n - 5) // 2)
                if n in (9, 11, 13, 15):
                    fold_values((n - 9) // 2)
            for bp in range(2):
                denominators(bp)
            for bp in range(2):
                pe.wait_ge(s("dcs"), bp + 1)
                for h in range(NH):
                    for b in (2 * bp, 2 * bp + 1):
                        c0 = HEADS * (2 * h + b % 2)
                        mm = t.matmul(bank(7 - bp, c0, c0 + HEADS), dcs[:, b, 128 * h:128 * h + 128], seld,
                                      start=True, stop=True)
                mm.then_inc(s("dent_ps"), 1)
            keep_clock(5, 0)

            def spread(n):
                b, gp = 2 * (n // 4) + n % 2, n // 2 % 2
                if n >= 4:
                    pe.wait_ge(s("qs"), n - 3)
                q = 64 * (b % 2)
                for g in (2 * gp, 2 * gp + 1):
                    mm = t.matmul(bank(n % 4, 256 * (g % 2), 256 * (g % 2) + 256), selr_bf[q:q + 48, g, :],
                                  rT[q:q + 48, b // 2, :], start=True, stop=True)
                mm.then_inc(s("rb_ps"), 1)

            def attended(bp, gp):
                pe.wait_ge(s("qs"), 4 * bp + 2 * gp + 2)
                for g in (2 * gp, 2 * gp + 1):
                    for b in (2 * bp, 2 * bp + 1):
                        q = 64 * (b % 2)
                        mm = t.matmul(ps[q:q + 64, 6 + bp, 0:N], kvd[:, b, g, 0:64], qf[:, g, b, :],
                                      start=(g == 0), stop=(g == HG - 1), tile_position=(0, q))
                if gp == 1:
                    mm.then_inc(s("y3_ps"), 1)

            pe.wait_ge(s("filled"), filled["selr_bf"])
            for bp in range(2):
                pe.wait_ge(s("r3"), bp + 1)
                for h in range(NH):
                    o = ps[:, 4 + bp, 64 * h:64 * h + 64].bitcast(BF16)
                    t.transpose(o, r3[:, h, 2 * bp:2 * bp + 2, :].rearrange("p b n -> p (b n)"), ident_bf[:, :]
                                ).then_inc(s("rT_ps"), 1)
                if bp == 0:
                    pe.wait_ge(s("rT"), 1)
                    for n in range(4):
                        spread(n)
            for h in range(NH):
                t.matmul(bank(4, 128 * h, 128 * h + 128), t3[:, 128 * h:128 * h + 128], ident,
                         start=(h == 0), stop=False, skip_group_check=True)
            keep_clock(2, 6)
            pe.wait_ge(s("rT"), 2)
            for n in range(4, 8):
                spread(n)
                if n % 2:
                    attended(0, n // 2 % 2)
            for gp in range(2):
                attended(1, gp)
            for bp in range(2):
                pe.wait_ge(s("ycs"), bp + 1)
                for h in range(NH):
                    c0 = 128 * h + 64 * bp
                    mm = t.matmul(bank(4, c0, c0 + 64), ycs[:, bp, 128 * h:128 * h + 128], sely, start=False, stop=True,
                                  skip_group_check=True)
            mm.then_inc(s("t4_ps"), 1)

            keep_clock(10, 0)
            turn_stack(3)
            for h in range(NH):
                if h == 1:
                    pe.wait_ge(s("xs_b"), 3)
                for b in range(B):
                    g = B * h + b
                    mm = t.matmul(bank(5, NE * g, NE * g + NE), xs[:, h, b, :], wst[:, WR:W3S], start=True, stop=True)
            mm.then_inc(s("rout_ps"), 1)
            for h in range(NH):
                for b in range(B):
                    mm = t.matmul(sc_bank[:, b, h, :], xs[:, h, b, :], wst[:, WE:WR], start=True, stop=True)
            mm.then_inc(s("exp_ps"), 1)
            for h in range(NH):
                t.matmul(bank(4 + 2 * h, 0, 128), t4[:, h, :], ident, start=True, stop=False)
            keep_clock(8, 7)
            for h in range(NH):
                pe.wait_ge(s("eprod"), B * (h + 1))
                for e in range(NE_SUM * h, NE):
                    mm = t.matmul(bank(4 + 2 * h, 0, 128), eprod[:, e, h, :], ident, start=False,
                                  stop=(h == 0 and e == NE - 1))
                if h == 1:
                    pe.wait_ge(s("esum"), 1)
                    mm = t.matmul(bank(6, 0, 128), esum[:, :], ident, start=False, stop=True)
                mm.then_inc(s("fin_ps"), 1)


def blocks(m):
    m = np.asarray(m)
    r, c = m.shape
    o = np.zeros((4 * r, 4 * c), m.dtype)
    for b in range(4):
        o[b * r:(b + 1) * r, b * c:(b + 1) * c] = m
    return o


def constants():
    f = np.float32
    eye = np.eye(P, dtype=f)
    ones = np.kron(np.eye(4, dtype=f), np.ones((32, 32), f))
    c1 = np.concatenate([eye, eye - ones / f(C), ones / f(C), np.kron(np.eye(4, dtype=f), np.ones((32, 1), f))], 1)
    lap = np.zeros((N, N), f)
    for r in range(HW):
        for c in range(HW):
            lap[r * HW + c, r * HW + c] = 4
            for dr, dc in ((0, 1), (0, -1), (1, 0), (-1, 0)):
                if 0 <= r + dr < HW and 0 <= c + dc < HW:
                    lap[(r + dr) * HW + c + dc, r * HW + c] = -1
    lower = (np.arange(KN)[:, None] < np.arange(KN)[None, :]).astype(f)
    rankoff = np.arange(NE + 2, dtype=f) - 8
    pair = np.kron(np.eye(64, dtype=f), np.full((2, 2), 0.5, f))
    i = np.arange(P)
    c2 = np.concatenate([
        lap.reshape(NH, P, N).transpose(1, 0, 2).reshape(P, -1),
        np.broadcast_to(lower.reshape(1, -1), (P, KN * KN)),
        np.broadcast_to(rankoff, (P, NE + 2)), pair,
        np.where(i[None, :] > i[:, None], MASKED, 0).astype(f),
        np.where(i[:, None] > i[None, :], MASKED, 0).astype(f)], 1)
    seg = np.stack([(np.arange(NA) < NA >> k) for k in range(NRES)]).astype(f) / f(TAP_SCALE)
    selr = np.zeros((2, 64, HG, 4, 32), f)
    for k in range(3):
        for hd in range(HEADS):
            selr[:, 16 * k + hd, hd // 4, hd % 4, :] = 1
    ksel = np.tile(np.eye(2 * KF, dtype=f), (NRES, 1))
    c3 = np.concatenate([np.broadcast_to(seg.reshape(1, -1), (P, NRES * NA)), selr.reshape(P, -1), ksel], 1)
    pos = f(1.57) * np.arange(N, dtype=f) / f(N)
    rows = np.arange(P)
    trig = np.stack([np.cos(pos), np.sin(pos)]).astype(f)
    strip = rows % 32
    csd = np.where((strip < 8)[:, None], trig[rows % 2], 0)
    csy = trig[rows // 32 % 2]
    seld = ((strip < 8)[:, None] & (rows[:, None] // 32 * 4 + strip[:, None] // 2 == np.arange(HEADS))).astype(f)
    sely = (rows[:, None] // 64 * C + strip[:, None] == np.arange(2 * C)).astype(f)
    c4 = np.concatenate([csd, csy, seld, sely], 1).astype(f)
    kone = np.zeros((XA, 2), f)
    kone[C, 0] = kone[2 * C + 1, 1] = 1
    return dict(
        c1=c1, c2=c2, c3=c3, c4=c4,
        sign=np.concatenate([np.ones((KF, N), f), np.tile(np.where(np.arange(N) % 2, -1, 1).astype(f), (KF, 1))]),
        kone=kone,
        cols=dict(cos=np.cos(pos).reshape(NH, P).T, sin=np.sin(pos).reshape(NH, P).T,
                  res=(rows[:, None] // 32 == np.arange(4)).astype(f),
                  mcos=(rows < C + 1).astype(f)[:, None], msin=((rows > C) & (rows < XA)).astype(f)[:, None],
                  kvm=(rows[:, None] // 32 == np.arange(4)).astype(f),
                  split=np.stack([
                      np.where(rows % 16 < 8, 1, -1), np.where(rows % 16 < 8, 0, C ** -0.5),
                      np.where(rows % 8 < 4, 1, -1), np.where(rows % 8 < 4, 0, 1),
                      np.where((rows < 64) | (rows == 96), 1, -1),
                      np.where((rows < 64) | (rows == 96), 0, 1),
                      (rows == 96) | (rows == 97)], 1).astype(f)))


def kernel(**inputs):
    import numpy as _np
    import concourse.bacc as _bacc
    from concourse import mybir as _mybir
    from concourse.bass_utils import run_bass_kernel_spmd as _run

    f = _np.float32
    a = {k: _np.asarray(v) for k, v in inputs.items()}
    k = constants()
    kc = k.pop("cols")

    def strips(v):
        return _np.tile(v, 4)[:, None]

    def qpad(v):
        return _np.concatenate([_np.tile(v, 4), _np.zeros(32 - 4 * v.shape[0], v.dtype)])

    def wpad(m):
        return _np.concatenate([_np.tile(m.T, (1, 4)), _np.zeros((C, 32 - 4 * m.shape[0]), m.dtype)], 1)

    def row(v):
        return _np.broadcast_to(v.reshape(1, -1), (P, v.size))

    cols = _np.concatenate([
        strips(qpad(a["L0_conv_bq"])), strips(qpad(a["L0_conv_bk"])), row(a["L0_conv_gamma"]),
        strips(a["L0_conv_bv"]), strips(a["L1_conv_gn_weight"]), strips(a["L1_conv_gn_bias"]),
        _np.tile(a["L1_conv_b1"], 2)[:, None], strips(a["L1_conv_b2"]),
        _np.tile(a["L2_ffn_sigma"], 8)[:, None], kc["cos"], kc["sin"],
        row(a["L2_ffn_log_weights"]), row(a["L2_ffn_gumbel"]), kc["res"], kc["mcos"], kc["msin"], kc["kvm"], kc["split"]], 1)
    w0 = _np.stack([blocks(wpad(a["L0_conv_wq"])), blocks(wpad(a["L0_conv_wk"])), blocks(a["L0_conv_wv"].T)], 1)
    zero = _np.zeros((C, C), f)
    wqk2 = _np.stack([_np.concatenate([a[w]] * 3 + [zero], 1) for w in ("L2_attn_Wq", "L2_attn_Wk")], 1)
    m1, m2 = blocks(a["L1_conv_w1"].T), blocks(a["L1_conv_w2"].T)
    mstu = _np.stack([a["L2_ffn_M_phi_plus"], a["L2_ffn_M_phi_minus"]], 1)
    mstu = mstu.transpose(0, 1, 2, 4, 3).reshape(P, C * C)
    phi = _np.tile(a["L2_ffn_phi"][:N].T, (2, 1))
    mu = a["L2_ffn_M_u"].reshape(NRES, TAPS, C, 8, 4).transpose(4, 2, 0, 3, 1).reshape(P, NRES, 8 * TAPS)
    wv = _np.concatenate([a["L3_attn_wv_w"], a["L3_attn_wv_b"][:, None]], 1)
    wva = _np.concatenate([wv, wv], 1).reshape(HG, P, XA).transpose(1, 0, 2)
    dw = a["L3_attn_dense_w"].T.reshape(HG, 4, 32, C)
    dwbd = _np.zeros((4, 32, HG, 4, C), f)
    for h in range(4):
        dwbd[h, :, :, h] = dw[:, h].transpose(1, 0, 2)
    weights3 = _np.concatenate([a["L3_attn_wq_w"].T, a["L3_attn_wk_w"].T,
                                a["L3_ffn_expert_w"].transpose(1, 0, 2).reshape(C, NE * C), a["L3_ffn_router_w"]], 1)
    biases3 = _np.concatenate([a["L3_attn_wq_b"], a["L3_attn_wk_b"], a["L3_ffn_expert_b"].reshape(-1),
                               a["L3_ffn_router_b"]])[None, :]
    w3 = _np.concatenate([weights3] * 3 + [biases3, biases3, _np.zeros((C - 2, W3S), f)])
    arrays = dict(
        x=a["x"].reshape(P, N), w0=w0, cols=cols, c1=k["c1"], c2=k["c2"], c3=k["c3"], c4=k["c4"], wqk2=wqk2,
        wv2=_np.concatenate([a["L2_attn_Wv"].T] * 3 + [zero]),
        wmlp1=m1.reshape(P, 2, P), wmlp2=m2.reshape(2, P, P).transpose(1, 0, 2), mstu=mstu, phi=phi, sign=k["sign"],
        mu=mu, wva=wva, dwbd=dwbd.reshape(P, HG, P), kone=k["kone"],
        denseb=row(_np.tile(a["L3_attn_dense_b"], 4)), w3=w3)

    nc = _bacc.Bacc("TRN2", target_bir_lowering=False, num_devices=1)
    feeds, args = {}, {}
    for name, v in arrays.items():
        v = _np.ascontiguousarray(v)
        feeds["in_" + name] = v
        args[name] = nc.dram_tensor("in_" + name, v.shape, _mybir.dt.from_np(v.dtype), kind="ExternalInput").ap()
    o = nc.dram_tensor("out_0", (P, N), _mybir.dt.float32, kind="ExternalOutput").ap()
    build(nc, out=o, **args)
    r = _run(nc, [feeds], core_ids=[0])
    return r.results[0]["out_0"].reshape(B, C, HW, HW)
```
